# Optimizing a Trainium2 kernel written in Bass

```python
import numpy as np
import jax
import jax.numpy as jnp

def _softmax(x, axis=-1):
    return jax.nn.softmax(x, axis=axis)

def _gelu(x):
    return jax.nn.gelu(x, approximate=True)

def _silu(x):
    return jax.nn.silu(x)

def _sigmoid(x):
    return jax.nn.sigmoid(x)

def _layernorm(x, axis=-1, eps=1e-05):
    m = jnp.mean(x, axis=axis, keepdims=True)
    v = jnp.var(x, axis=axis, keepdims=True)
    return (x - m) / jnp.sqrt(v + eps)

def _scatter_add(tgt, idx, src, axis=0):
    return tgt.at[idx].add(src)

def _segment_sum(src, seg, n):
    return jax.ops.segment_sum(src, seg, n)
kernel_name = 'mk_adaln_d1_jaxref_r4_468797'

def setup_inputs(seed: int=0):
    np.random.seed(seed)
    _w = jnp.asarray

    def _L0_attn_setup():
        import jax, jax.numpy as jnp
        import numpy as np
        import math
        N_HEAD = 16
        ATTN_THRESHOLD = -0.1
        EPS = 1e-06
        key = jax.random.key(seed)
        ks = jax.random.split(key, 5)
        B, T, C = (2, 512, 512)
        s = 1.0 / math.sqrt(C)
        return {'x': jax.random.normal(ks[0], (B, T, C), dtype=jnp.float32), 'Wq': jax.random.normal(ks[1], (C, C), dtype=jnp.float32) * s, 'Wk': jax.random.normal(ks[2], (C, C), dtype=jnp.float32) * s, 'Wv': jax.random.normal(ks[3], (C, C), dtype=jnp.float32) * s, 'Wo': jax.random.normal(ks[4], (C, C), dtype=jnp.float32) * s}
    _L0_attn_in = _L0_attn_setup()

    def _L0_ffn_setup():
        import jax, jax.numpy as jnp
        import numpy as np
        E = 64
        K = 4
        H = 512
        I = 384
        C = 64
        B, S = (1, 512)
        key = jax.random.key(seed)
        ks = jax.random.split(key, 8)
        sh = 1.0 / np.sqrt(H).astype(np.float32)
        si = 1.0 / np.sqrt(I).astype(np.float32)
        return {'x': jax.random.normal(ks[0], (B, S, H), jnp.float32), 'w_router': jax.random.normal(ks[1], (E, H), jnp.float32) * sh, 'w_gate': jax.random.normal(ks[2], (E, H, I), jnp.float32) * sh, 'w_up': jax.random.normal(ks[3], (E, H, I), jnp.float32) * sh, 'w_down': jax.random.normal(ks[4], (E, I, H), jnp.float32) * si, 'w_sh_gate': jax.random.normal(ks[5], (H, I), jnp.float32) * sh, 'w_sh_up': jax.random.normal(ks[6], (H, I), jnp.float32) * sh, 'w_sh_down': jax.random.normal(ks[7], (I, H), jnp.float32) * si}
    _L0_ffn_in = _L0_ffn_setup()
    _L0_c = _w((lambda *s: np.random.randn(*s).astype(np.float32) * 0.05)(1, 512))
    _L0_wmod = _w((lambda *s: np.random.randn(*s).astype(np.float32) * 0.05)(512, 6 * 512) * 512 ** (-0.5))
    _d = {'L0_attn_x': _L0_attn_in['x'], 'L0_attn_Wq': _L0_attn_in['Wq'], 'L0_attn_Wk': _L0_attn_in['Wk'], 'L0_attn_Wv': _L0_attn_in['Wv'], 'L0_attn_Wo': _L0_attn_in['Wo'], 'L0_ffn_w_router': _L0_ffn_in['w_router'], 'L0_ffn_w_gate': _L0_ffn_in['w_gate'], 'L0_ffn_w_up': _L0_ffn_in['w_up'], 'L0_ffn_w_down': _L0_ffn_in['w_down'], 'L0_ffn_w_sh_gate': _L0_ffn_in['w_sh_gate'], 'L0_ffn_w_sh_up': _L0_ffn_in['w_sh_up'], 'L0_ffn_w_sh_down': _L0_ffn_in['w_sh_down'], 'L0_c': _L0_c, 'L0_wmod': _L0_wmod}
    _x0 = _d['L0_attn_x']
    _d['L0_attn_x'] = jax.random.normal(jax.random.fold_in(jax.random.key(seed), 1), (1, 4096, 512), dtype=_x0.dtype)
    del _x0
    return _d

def reference(L0_attn_x, L0_attn_Wq, L0_attn_Wk, L0_attn_Wv, L0_attn_Wo, L0_ffn_w_router, L0_ffn_w_gate, L0_ffn_w_up, L0_ffn_w_down, L0_ffn_w_sh_gate, L0_ffn_w_sh_up, L0_ffn_w_sh_down, L0_c, L0_wmod):

    def _L0_attn_ref(x, Wq, Wk, Wv, Wo):
        import jax, jax.numpy as jnp
        import numpy as np
        import math
        N_HEAD = 16
        ATTN_THRESHOLD = -0.1
        EPS = 1e-06
        B, T, C = x.shape
        H = N_HEAD
        hd = C // H
        scale = 1.0 / math.sqrt(hd)

        def proj(W):
            return jnp.einsum('btc,oc->bto', x, W).reshape(B, T, H, hd).swapaxes(1, 2)
        q, k, v = (proj(Wq), proj(Wk), proj(Wv))
        scores = jnp.einsum('bhqd,bhkd->bhqk', q, k) * scale
        causal = jnp.tril(jnp.ones((T, T), dtype=bool))
        w = jnp.where(causal, jax.nn.relu(scores - ATTN_THRESHOLD), 0.0)
        w = w / (jnp.sum(w, axis=-1, keepdims=True) + EPS)
        out = jnp.einsum('bhqk,bhkd->bhqd', w, v)
        out = out.swapaxes(1, 2).reshape(B, T, C)
        return jnp.einsum('btc,oc->bto', out, Wo)

    def _L0_ffn_ref(x, w_router, w_gate, w_up, w_down, w_sh_gate, w_sh_up, w_sh_down):
        import jax, jax.numpy as jnp
        import numpy as np
        E = 64
        K = 4
        H = 512
        I = 384
        C = 64
        B, S = (1, 512)
        b, s, h = x.shape
        xf = x.reshape(-1, h)
        T = xf.shape[0]
        P = T * K
        logits = xf @ w_router.T
        top_vals, top_idx = jax.lax.top_k(logits, K)
        w_tok = jax.nn.softmax(top_vals.astype(jnp.float32), axis=-1)
        e_flat = top_idx.reshape(-1)
        tok_flat = jnp.repeat(jnp.arange(T), K)
        w_flat = w_tok.reshape(-1)
        order = jnp.argsort(e_flat)
        tok_s = tok_flat[order]
        w_s = w_flat[order]
        counts = jnp.zeros((E,), jnp.int32).at[e_flat].add(1)
        offsets = jnp.cumsum(counts) - counts
        pos = offsets[:, None] + jnp.arange(C)[None, :]
        valid = jnp.arange(C)[None, :] < counts[:, None]
        pos_c = jnp.clip(pos, 0, P - 1)
        tok_ec = tok_s[pos_c]
        w_ec = jnp.where(valid, w_s[pos_c], 0.0)
        x_ec = xf[tok_ec]
        g = jax.nn.silu(jnp.einsum('ech,ehi->eci', x_ec, w_gate))
        u = jnp.einsum('ech,ehi->eci', x_ec, w_up)
        y = jnp.einsum('eci,eih->ech', g * u, w_down)
        contrib = (y * w_ec[..., None]).reshape(-1, h)
        combined = jnp.zeros_like(xf).at[tok_ec.reshape(-1)].add(contrib)
        sg = jax.nn.silu(xf @ w_sh_gate)
        su = xf @ w_sh_up
        combined = combined + sg * su @ w_sh_down
        return combined.reshape(b, s, h)
    x = L0_attn_x
    mod = (_silu(L0_c) @ L0_wmod).reshape(L0_c.shape[0], 6, 1, -1)
    sa, ca, ga, sb, cb, gb = (mod[:, 0], mod[:, 1], mod[:, 2], mod[:, 3], mod[:, 4], mod[:, 5])
    ga = (2 * (ga >= 0) - 1) * jnp.maximum(jnp.abs(ga), 0.25)
    gb = (2 * (gb >= 0) - 1) * jnp.maximum(jnp.abs(gb), 0.25)
    h = _layernorm(x, axis=-1) * (1 + ca) + sa
    x = x + ga * _L0_attn_ref(h, L0_attn_Wq, L0_attn_Wk, L0_attn_Wv, L0_attn_Wo)
    h = _layernorm(x, axis=-1) * (1 + cb) + sb
    x = x + gb * _L0_ffn_ref(h, L0_ffn_w_router, L0_ffn_w_gate, L0_ffn_w_up, L0_ffn_w_down, L0_ffn_w_sh_gate, L0_ffn_w_sh_up, L0_ffn_w_sh_down)
    return x

_drawn_inputs = setup_inputs


def setup_inputs(seed=0):
    import zlib

    import numpy as np

    out = dict(_drawn_inputs(seed))
    spreads = {}
    factors = {'L0_attn_Wq': 2.68, 'L0_attn_Wk': 2.675}
    for name, (base, spread) in spreads.items():
        noise = np.random.default_rng([zlib.crc32(name.encode()), seed]).standard_normal(out[name].shape)
        drawn = base * np.exp(spread * noise) if base else spread * noise
        out[name] = jnp.asarray(drawn.astype(out[name].dtype))
    for name, factor in factors.items():
        out[name] = (out[name] * factor).astype(out[name].dtype)
    return out
```

```python
import concourse.bass as bass
from concourse import mybir
from contextlib import ExitStack

F32 = mybir.dt.float32
F32R = mybir.dt.float32r
U32 = mybir.dt.uint32
ALU = mybir.AluOpType
ACT = mybir.ActivationFunctionType

P = 128
C = 512
KT = C // P
H = 16
HD = C // H
HG = P // HD
NG = H // HG
TT = 512
TB = TT // P
SHIFT = 0.1
ATT_EPS = 1e-6
LN_EPS = 1e-5
NE = 64
TOPK = 4
CAP = 64
FI = 384
FT = FI // P
MODS = 6
SA, CA, GA, SB, CB, GB = range(MODS)


def wait_apart(eng, passed, *waits):
    for sem, value in zip(waits[::2], waits[1::2]):
        eng.wait_ge(sem, value)
    eng.sem_inc(passed, 1)


def chained(eng, sem, base=0):
    count = [base]

    def done(ins, passed=None):
        count[0] = count[0] + 1
        ins.then_inc(sem, 1)
        if passed:
            wait_apart(eng, passed, sem, count[0])
        else:
            eng.wait_ge(sem, count[0])

    return done


def modulation(nc, c, wmod, keep):
    with ExitStack() as ctx:
        ccol = ctx.enter_context(nc.sbuf_tensor("ccol", [P, KT], F32))
        cexp = ctx.enter_context(nc.sbuf_tensor("cexp", [P, KT], F32))
        crep = ctx.enter_context(nc.sbuf_tensor("crep", [P, KT, P], F32))
        wm = ctx.enter_context(nc.sbuf_tensor("wm", [P, KT, MODS * C], F32))
        rows = ctx.enter_context(nc.sbuf_tensor("mod_rows", [P, MODS, C], F32))
        sign = ctx.enter_context(nc.sbuf_tensor("gate_sign", [P, C], F32))
        size = ctx.enter_context(nc.sbuf_tensor("gate_size", [P, C], F32))
        banks = ctx.enter_context(nc.psum_tensor("mod_ps", [P, MODS, C], F32))
        turned = ctx.enter_context(nc.psum_tensor("mod_turned", [P, 2, C], F32))
        c_in = ctx.enter_context(nc.semaphore("c_in"))
        wm_in = ctx.enter_context(nc.semaphore("wm_in"))
        c_exp = ctx.enter_context(nc.semaphore("c_exp"))
        c_ready = ctx.enter_context(nc.semaphore("c_ready"))
        dve_step = ctx.enter_context(nc.semaphore("mod_dve_step"))
        pool_step = ctx.enter_context(nc.semaphore("mod_pool_step"))
        mod_ready = ctx.enter_context(nc.semaphore("mod_ready"))
        rows_ready = ctx.enter_context(nc.semaphore("rows_ready"))
        turned_ready = ctx.enter_context(nc.semaphore("turned_ready"))
        turned_used = ctx.enter_context(nc.semaphore("turned_used"))
        block = ctx.enter_context(nc.Block())
        ident, cols, gates = keep["ident"], keep["cols"], keep["gates"]
        columns = [SA, CA, SB, CB]

        @block.sync
        def _(sp):
            sp.dma_start(ccol[:, :], c[0, :].rearrange("(p k) -> p k", p=P)).then_inc(c_in, 16)
            sp.dma_start(wm[:, :, :], wmod.rearrange("(p k) n -> p k n", p=P)).then_inc(wm_in, 16)

        @block.gpsimd
        def _(pool):
            done = chained(pool, pool_step)
            done(pool.memset(ident[:, :], 0.0))
            done(pool.affine_select(out=ident[:, :], in_=ident[:, :], compare_op=ALU.not_equal, fill=1.0,
                                    base=0, pattern=[[-1, P]], channel_multiplier=1))
            done(pool.memset(keep["ones"][:, :], 1.0))

        @block.scalar
        def _(act):
            act.wait_ge(c_in, 16)
            nc.scalar.activation(cexp[:, :], ccol[:, :], ACT.Exp, scale=-1.0).then_inc(c_exp, 1)
            for m in range(MODS):
                act.wait_ge(mod_ready, m + 1)
                nc.scalar.copy(rows[:, m, :], banks[:, m, :]).then_inc(rows_ready, 1)

        @block.vector
        def _(dve):
            done = chained(dve, dve_step)
            dve.wait_ge(c_exp, 1)
            done(nc.vector.tensor_scalar(cexp[:, :], cexp[:, :], 1.0, None, ALU.add))
            done(nc.vector.reciprocal(cexp[:, :], cexp[:, :]))
            done(nc.vector.tensor_tensor(ccol[:, :], ccol[:, :], cexp[:, :], ALU.mult))
            done(nc.vector.memset(crep[:, :, :], 1.0))
            for k in range(KT):
                nc.vector.tensor_scalar(crep[:, k, :], crep[:, k, :], ccol[:, k:k + 1], None,
                                        ALU.mult).then_inc(c_ready, 1)
            for n, m in enumerate(columns):
                dve.wait_ge(turned_ready, n + 1)
                one = 1.0 if m in (CA, CB) else 0.0
                src = turned[:, n % 2, :].rearrange("p (k t) -> p k t", k=KT)[:, :, 0]
                nc.vector.tensor_scalar(cols[:, m, :], src, one, None, ALU.add).then_inc(turned_used, 1)
            for n, m in enumerate((GA, GB)):
                dve.wait_ge(rows_ready, m + 1)
                g = rows[:, m, :]
                done(nc.vector.tensor_scalar(sign[:, :], g, 0.0, 2.0, ALU.is_ge, ALU.mult))
                done(nc.vector.tensor_scalar(sign[:, :], sign[:, :], 1.0, None, ALU.subtract))
                done(nc.vector.scalar_tensor_tensor(size[:, :], g, -1.0, g, ALU.mult, ALU.max))
                done(nc.vector.scalar_tensor_tensor(gates[:, n, :], size[:, :], 0.25, sign[:, :],
                                                    ALU.max, ALU.mult))

        @block.tensor
        def _(pe):
            pe.wait_ge(c_ready, KT)
            pe.wait_ge(wm_in, 16)
            for m in range(MODS):
                for k in range(KT):
                    last = nc.tensor.matmul(banks[:, m, :], crep[:, k, :], wm[:, k, m * C:(m + 1) * C],
                                            start=(k == 0), stop=(k == KT - 1))
                last.then_inc(mod_ready, 1)
            pe.wait_ge(pool_step, 2)
            for n, m in enumerate(columns):
                pe.wait_ge(rows_ready, m + 1)
                if n >= 2:
                    pe.wait_ge(turned_used, n - 1)
                for k in range(KT):
                    last = nc.tensor.transpose(turned[:, n % 2, k * P:(k + 1) * P],
                                               rows[:, m, k * P:(k + 1) * P], ident[:, :])
                last.then_inc(turned_ready, 1)


def normalize_rows(nc, dve, done, xb, xn, stats, mv, rs, var_ready, sd_ready, sd_count, passed=None):
    for t in range(TB):
        last = nc.vector.bn_stats(stats[:, t, :], xb[:, t, :])
    done(last, passed)
    for t in range(TB):
        last = nc.vector.bn_aggr(mv[:, t, :], stats[:, t, :])
    done(last)
    nc.vector.tensor_scalar(rs[:, 0, :], mv[:, :, 1], LN_EPS, None, ALU.add).then_inc(var_ready, 1)
    dve.wait_ge(sd_ready, sd_count)
    done(nc.vector.reciprocal(rs[:, 2, :], rs[:, 1, :]))
    done(nc.vector.tensor_tensor(rs[:, 1, :], rs[:, 2, :], rs[:, 2, :], ALU.mult))
    done(nc.vector.tensor_tensor(rs[:, 1, :], rs[:, 1, :], rs[:, 0, :], ALU.mult))
    done(nc.vector.tensor_scalar(rs[:, 1, :], rs[:, 1, :], -0.5, 1.5, ALU.mult, ALU.add))
    done(nc.vector.tensor_tensor(rs[:, 2, :], rs[:, 2, :], rs[:, 1, :], ALU.mult))
    for t in range(TB):
        last = nc.vector.tensor_scalar(xn[:, t, :], xb[:, t, :], mv[:, t, 0:1], rs[:, 2, t:t + 1],
                                       ALU.subtract, ALU.mult)
    return last


def first_norm(nc, x, hT, keep):
    T = x.shape[0]
    NT = T // TT
    with ExitStack() as ctx:
        xb = [ctx.enter_context(nc.sbuf_tensor(f"n1_x{b}", [P, TB, C], F32)) for b in range(2)]
        stats = ctx.enter_context(nc.sbuf_tensor("n1_stats", [P, TB, 6], F32))
        mv = ctx.enter_context(nc.sbuf_tensor("n1_mv", [P, TB, 2], F32))
        rs = ctx.enter_context(nc.sbuf_tensor("n1_rs", [P, 3, TB], F32))
        ps = ctx.enter_context(nc.psum_tensor("n1_ps", [P, 2, KT, TT], F32))
        x_in = [ctx.enter_context(nc.semaphore(f"n1_x_in{b}")) for b in range(2)]
        var_ready = ctx.enter_context(nc.semaphore("n1_var_ready"))
        sd_ready = ctx.enter_context(nc.semaphore("n1_sd_ready"))
        xn_ready = ctx.enter_context(nc.semaphore("n1_xn_ready"))
        turned = ctx.enter_context(nc.semaphore("n1_turned"))
        written = ctx.enter_context(nc.semaphore("n1_written"))
        dve_step = ctx.enter_context(nc.semaphore("n1_dve_step"))
        block = ctx.enter_context(nc.Block())
        ident, cols = keep["ident"], keep["cols"]

        @block.sync
        def _(sp):
            for n in range(NT):
                if n >= 2:
                    sp.wait_ge(turned, KT * (n - 1))
                sp.dma_start(xb[n % 2][:, :, :], x[n * TT:(n + 1) * TT, :].rearrange(
                    "(t p) c -> p t c", p=P)).then_inc(x_in[n % 2], 16)

        @block.vector
        def _(dve):
            done = chained(dve, dve_step)
            for n in range(NT):
                dve.wait_ge(x_in[n % 2], 16 * (n // 2 + 1))
                last = normalize_rows(nc, dve, done, xb[n % 2], xb[n % 2], stats, mv, rs, var_ready, sd_ready, n + 1)
                last.then_inc(xn_ready, 1)

        @block.scalar
        def _(act):
            def root(n):
                act.wait_ge(var_ready, n + 1)
                nc.scalar.activation(rs[:, 1, :], rs[:, 0, :], ACT.Sqrt).then_inc(sd_ready, 1)

            root(0)
            for n in range(NT):
                if n + 1 < NT:
                    root(n + 1)
                for k in range(KT):
                    act.wait_ge(turned, KT * n + k + 1)
                    nc.scalar.activation(hT[:, k, n * TT:(n + 1) * TT], ps[:, n % 2, k, :], ACT.Identity,
                                         scale=cols[:, CA, k:k + 1],
                                         bias=cols[:, SA, k:k + 1]).then_inc(written, 1)

        @block.tensor
        def _(pe):
            for n in range(NT):
                pe.wait_ge(xn_ready, n + 1)
                for k in range(KT):
                    if n >= 2:
                        pe.wait_ge(written, KT * (n - 2) + k + 1)
                    for t in range(TB):
                        last = nc.tensor.transpose(ps[:, n % 2, k, t * P:(t + 1) * P],
                                                   xb[n % 2][:, t, k * P:(k + 1) * P], ident[:, :])
                    last.then_inc(turned, 1)


def attention_plan(NT):
    plan = [("w", 0, 0), ("w", 1, 0), ("w", 2, 0), ("k", 0, 0), ("q", 0, 0), ("v", 0, 0)]
    late = None
    for i in range(NT):
        for j in range(TB * (i + 1)):
            plan.append(("s", i, j))
            if i + 1 < NT and j < 3:
                plan.append(("kqv"[j], i + 1, 0))
            if late:
                plan.append(("p",) + late)
                if late[0] < i:
                    plan.append(("n", late[0], 0))
            late = (i, j)
    plan += [("p",) + late, ("n", NT - 1, 0)]
    return plan


def attention(nc, hT, wq, wk, wv, oT_dram, keep):
    T = hT.shape[2]
    NT = T // TT
    plan = attention_plan(NT)
    STEPS = sum(e[0] == "s" for e in plan)
    kinds = [e[0] for e in plan if e[0] in "wkqv"]
    JOBS = len(kinds)
    RESTS = 2 * NT
    assert STEPS % 2 == 0 and NT % 2 == 0
    scale = HD ** -0.5
    with ExitStack() as ctx:
        wraw = ctx.enter_context(nc.sbuf_tensor("w_rows", [P, 3, C], F32))
        wT = ctx.enter_context(nc.sbuf_tensor("w_turned", [P, 3, KT, P], F32))
        kst = ctx.enter_context(nc.sbuf_tensor("k_stack", [P, HG, T], F32R))
        qst = ctx.enter_context(nc.sbuf_tensor("q_stack", [P, 2, HG, TT], F32R))
        kpart = ctx.enter_context(nc.sbuf_tensor("k_parts", [P, 2, TT], F32R))
        qpart = ctx.enter_context(nc.sbuf_tensor("q_parts", [P, 2, TT], F32R))
        vals = ctx.enter_context(nc.sbuf_tensor("vals", [P, T // P, P], F32))
        w = ctx.enter_context(nc.sbuf_tensor("att_w", [P, 2, HG, TT], F32))
        rden = ctx.enter_context(nc.sbuf_tensor("att_rden", [P, TT], F32))
        o = ctx.enter_context(nc.sbuf_tensor("att_o", [P, 2, TT], F32))
        s_ps = ctx.enter_context(nc.psum_tensor("s_ps", [P, HG, TT], F32))
        num = ctx.enter_context(nc.psum_tensor("num_ps", [P, TT], F32))
        den = ctx.enter_context(nc.psum_tensor("den_ps", [P, TT], F32))
        job_ps = ctx.enter_context(nc.psum_tensor("job_ps", [P, 2, TT], F32))
        sems = {n: ctx.enter_context(nc.semaphore("at_" + n)) for n in (
            "w_in", "w_turned", "job_ready", "job_hi", "rest_done", "k_in", "q_in", "s_ready", "relu0", "relu1",
            "masked", "pv_done", "o_ready", "rd", "nd")}
        w_in, job_ready, job_hi, rest_done = sems["w_in"], sems["job_ready"], sems["job_hi"], sems["rest_done"]
        k_in, q_in, s_ready, relu = sems["k_in"], sems["q_in"], sems["s_ready"], (sems["relu0"], sems["relu1"])
        masked, pv_done, o_ready, rd, nd = sems["masked"], sems["pv_done"], sems["o_ready"], sems["rd"], sems["nd"]
        o_out = [ctx.enter_context(nc.semaphore(f"at_o_out{b}")) for b in range(2)]
        pool_passed = ctx.enter_context(nc.semaphore("at_pool_passed"))
        block = ctx.enter_context(nc.Block())
        ident, ones = keep["ident"], keep["ones"]
        MOVES = 16 * 4 * HG

        def width(i, j):
            return max(0, (j - TB * i) * P)

        def step_of(i):
            return TB * (i + 1) * (i + 2) // 2

        def rests(jobs):
            return sum(kind in "kq" for kind in kinds[:jobs])

        @block.sync
        def _(sp):
            with sp.Fori(0, NG) as g:
                for n, src in enumerate((wq, wk, wv)):
                    sp.dma_start(wraw[:, n, :], src[bass.ds(g * P, P), :]).then_inc(w_in, 16)
                job = 0
                for kind, i, j in plan:
                    if kind in "wkqv":
                        job += 1
                    if kind in "kq":
                        sp.wait_ge(rest_done, g * RESTS + rests(job))
                        for h in range(HG):
                            for r in range(4):
                                part, dst, sem = ((kpart[:, r % 2, :], kst[:, h, i * TT:(i + 1) * TT], k_in)
                                                  if kind == "k" else
                                                  (qpart[:, r // 2, :], qst[:, i % 2, h, :], q_in))
                                sp.dma_start(dst[r * HD:(r + 1) * HD, :].bitcast(F32),
                                             part[h * HD:(h + 1) * HD, :].bitcast(F32)).then_inc(sem, 16)
                    elif kind == "n":
                        sp.wait_ge(o_ready, g * NT + i + 1)
                        sp.dma_start(oT_dram[bass.ds(g * P, P), i * TT:(i + 1) * TT],
                                     o[:, i % 2, :]).then_inc(o_out[i % 2], 16)
            for b in range(2):
                sp.wait_ge(o_out[b], 16 + 16 * NG * NT // 2)

        @block.scalar
        def _(act):
            with act.Fori(0, NG) as g:
                job = step = 0
                for kind, i, j in plan:
                    if kind in "wkqv":
                        bank = job_ps[:, job % 2, :]
                        job += 1
                        act.wait_ge(job_ready, g * JOBS + job)
                        if kind == "w":
                            nc.scalar.copy(wT[:, i, :, :], bank.rearrange("p (k o) -> p k o", k=KT)
                                           ).then_inc(job_hi, 1)
                        elif kind == "v":
                            nc.scalar.copy(vals[:, TB * i:TB * (i + 1), :],
                                           bank.rearrange("p (t o) -> p t o", t=TB)).then_inc(job_hi, 1)
                        elif kind == "k":
                            nc.scalar.copy(kpart[:, 0, :], bank).then_inc(job_hi, 1)
                        else:
                            nc.scalar.mul(qpart[:, 0, :], bank, scale).then_inc(job_hi, 1)
                    elif kind == "s":
                        q0 = width(i, j)
                        act.wait_ge(s_ready, 2 * (g * STEPS + step) + 1)
                        act.wait_ge(pv_done, g * STEPS + step + 1)
                        nc.scalar.activation(w[:, step % 2, 0:2, q0:], s_ps[:, 0:2, q0:], ACT.Relu,
                                             bias=SHIFT).then_inc(relu[0], 1)
                        step += 1

        @block.vector
        def _(dve):
            nc.vector.memset(rden[:, :], 0.0).then_inc(pv_done, 2)
            nc.vector.memset(o[:, 0, :], 0.0).then_inc(o_out[0], 16)
            nc.vector.memset(o[:, 1, :], 0.0).then_inc(o_out[1], 16)
            with dve.Fori(0, NG) as g:
                job = step = 0
                for kind, i, j in plan:
                    if kind in "wkqv":
                        bank = job_ps[:, job % 2, :]
                        job += 1
                        if kind in "kq":
                            part = kpart if kind == "k" else qpart
                            dve.wait_ge(job_hi, g * JOBS + job)
                            nc.vector.scalar_tensor_tensor(
                                part[:, 1, :], bank, 1.0 if kind == "k" else scale,
                                part[:, 0, :].bitcast(F32), ALU.mult, ALU.subtract).then_inc(rest_done, 1)
                    elif kind == "s":
                        q0 = width(i, j)
                        dve.wait_ge(s_ready, 2 * (g * STEPS + step) + 2)
                        dve.wait_ge(pv_done, g * STEPS + step + 1)
                        nc.vector.tensor_scalar(w[:, step % 2, 2:4, q0:], s_ps[:, 2:4, q0:], SHIFT, 0.0,
                                                ALU.add, ALU.max).then_inc(relu[1], 1)
                        step += 1
                    elif kind == "n":
                        dve.wait_ge(pv_done, g * STEPS + step_of(i) + 2)
                        nc.vector.tensor_scalar(rden[:, :], den[:, :], ATT_EPS, None, ALU.add).then_inc(rd, 1)
                        dve.wait_ge(rd, 2 * (g * NT + i) + 1)
                        nc.vector.reciprocal(rden[:, :], rden[:, :]).then_inc(rd, 1)
                        dve.wait_ge(rd, 2 * (g * NT + i) + 2)
                        dve.wait_ge(o_out[i % 2], 16 * (g * (NT // 2) + i // 2) + 16)
                        nc.vector.tensor_tensor(o[:, i % 2, :], num[:, :], rden[:, :],
                                                ALU.mult).then_inc(o_ready, 1)

        @block.gpsimd
        def _(pool):
            with pool.Fori(0, NG) as g:
                step = diag = 0
                for kind, i, j in plan:
                    if kind != "s":
                        continue
                    if j >= TB * i:
                        q0 = width(i, j)
                        wait_apart(pool, pool_passed, relu[0], g * STEPS + step + 1, relu[1], g * STEPS + step + 1)
                        tri = w[:, step % 2, :, q0:q0 + P]
                        pool.affine_select(out=tri, in_=tri, compare_op=ALU.is_ge, fill=0.0, base=0,
                                           pattern=[[0, HG], [1, P]], channel_multiplier=-1).then_inc(masked, 1)
                        diag += 1
                    step += 1

        @block.tensor
        def _(pe):
            with pe.Fori(0, NG) as g:
                job = step = pvs = diag = 0
                for kind, i, j in plan:
                    if kind in "wkqv":
                        bank = job_ps[:, job % 2, :]
                        if job == 0:
                            pe.wait_ge(w_in, 48 * g + 48)
                        elif job >= 2 and kinds[job - 2] in "kq":
                            pe.wait_ge(rest_done, g * RESTS + rests(job - 1))
                        elif job >= 2:
                            pe.wait_ge(job_hi, g * JOBS + job - 1)
                        if kind == "w":
                            for k in range(KT):
                                last = nc.tensor.transpose(bank[:, k * P:(k + 1) * P], wraw[:, i, k * P:(k + 1) * P],
                                                           ident[:, :])
                        elif kind in "kq":
                            if i == 0 and kind == "k":
                                pe.wait_ge(job_hi, g * JOBS + 3)
                            for k in range(KT):
                                last = nc.tensor.matmul(bank, wT[:, "qk".index(kind), k, :],
                                                        hT[:, k, i * TT:(i + 1) * TT],
                                                        start=(k == 0), stop=(k == KT - 1))
                        else:
                            for t in range(TB):
                                at = (TB * i + t) * P
                                for k in range(KT):
                                    last = nc.tensor.matmul(bank[:, t * P:(t + 1) * P], hT[:, k, at:at + P],
                                                            wT[:, 2, k, :], start=(k == 0), stop=(k == KT - 1))
                        last.then_inc(job_ready, 1)
                        job += 1
                    elif kind == "s":
                        q0 = width(i, j)
                        if j == 0:
                            pe.wait_ge(k_in, MOVES * (g * NT + i + 1))
                            pe.wait_ge(q_in, MOVES * (g * NT + i + 1))
                        for b in range(2):
                            if step >= 1:
                                pe.wait_ge(relu[b], g * STEPS + step)
                            for h in (2 * b, 2 * b + 1):
                                last = nc.tensor.matmul(s_ps[:, h, q0:], kst[:, h, j * P:(j + 1) * P],
                                                        qst[:, i % 2, h, q0:], start=True, stop=True)
                            last.then_inc(s_ready, 1)
                        step += 1
                    elif kind == "p":
                        q0 = width(i, j)
                        if j == 0:
                            pe.wait_ge(job_hi, g * JOBS + 3 + 3 * (i + 1))
                            if i >= 1:
                                pe.wait_ge(o_ready, g * NT + i)
                        for b in range(2):
                            pe.wait_ge(relu[b], g * STEPS + pvs + 1)
                        if j >= TB * i:
                            diag += 1
                            pe.wait_ge(masked, g * TB * NT + diag)
                        last_j = j == TB * (i + 1) - 1
                        for acc in (num, den):
                            for h in range(HG):
                                lhsT = vals[:, j, h * HD:(h + 1) * HD] if acc is num else ones[:, 0:HD]
                                last = nc.tensor.matmul(acc[h * HD:(h + 1) * HD, q0:], lhsT,
                                                        w[:, pvs % 2, h, q0:], start=(j == 0), stop=last_j)
                        last.then_inc(pv_done, 1)
                        pvs += 1


def turn_weights(nc, wo, w_router, woT, wrT, w_shd, w_sh_down, keep):
    with ExitStack() as ctx:
        rows = ctx.enter_context(nc.sbuf_tensor("tw_rows", [P, KT, C], F32))
        rrows = ctx.enter_context(nc.sbuf_tensor("tw_router", [NE, C], F32))
        ps = ctx.enter_context(nc.psum_tensor("tw_ps", [P, KT, C], F32))
        rps = ctx.enter_context(nc.psum_tensor("tw_rps", [P, KT, P], F32))
        w_in = ctx.enter_context(nc.semaphore("tw_in"))
        d_in = ctx.enter_context(nc.semaphore("tw_down_in"))
        turned = ctx.enter_context(nc.semaphore("tw_turned"))
        block = ctx.enter_context(nc.Block())
        ident, gates = keep["ident"], keep["gates"]

        @block.sync
        def _(sp):
            sp.dma_start(rows[:, :, :], wo.rearrange("(o p) c -> p o c", p=P)).then_inc(w_in, 16)
            sp.dma_start(rrows[:, :], w_router).then_inc(w_in, 16)
            sp.dma_start(w_shd[:, :, :], w_sh_down.rearrange("(f p) c -> p f c", p=P)).then_inc(d_in, 16)

        @block.tensor
        def _(pe):
            pe.wait_ge(w_in, 32)
            for k in range(KT):
                for o in range(KT):
                    last = nc.tensor.transpose(ps[:, k, o * P:(o + 1) * P], rows[:, o, k * P:(k + 1) * P],
                                               ident[:, :])
                last.then_inc(turned, 1)
            for k in range(KT):
                last = nc.tensor.transpose(rps[:, k, 0:NE], rrows[:, k * P:(k + 1) * P], ident[0:NE, 0:NE])
            last.then_inc(turned, 1)

        @block.vector
        def _(dve):
            dve.wait_ge(d_in, 16)
            for f in range(FT):
                nc.vector.tensor_tensor(w_shd[:, f, :], w_shd[:, f, :], gates[:, 1, :], ALU.mult)
            for k in range(KT):
                dve.wait_ge(turned, k + 1)
                nc.vector.tensor_tensor(woT[:, k, :], ps[:, k, :], gates[:, 0, :], ALU.mult)

        @block.scalar
        def _(act):
            act.wait_ge(turned, KT + 1)
            nc.scalar.copy(wrT[:, :, :], rps[:, :, 0:NE])


def dense_part(nc, x, oT_dram, rows_dram, acc_dram, w_sh_gate, w_sh_up, woT, wrT, w_shd, keyT, keep):
    T = x.shape[0]
    NT = T // TT
    MISC = 13
    CHAIN = 2 + 5 + 3 * FT + 2 + TOPK + 3 + 1
    with ExitStack() as ctx:
        def sb(name, shape, dt=F32):
            return ctx.enter_context(nc.sbuf_tensor("d_" + name, shape, dt))

        def sem(name):
            return ctx.enter_context(nc.semaphore("d_" + name))

        oTb = [sb(f"oT{b}", [P, KT, TT]) for b in range(2)]
        xb = [sb(f"x{b}", [P, TB, C]) for b in range(2)]
        xn = [sb(f"xn{b}", [P, TB, C]) for b in range(2)]
        h2T = [sb(f"h2T{b}", [P, KT, TT]) for b in range(2)]
        shg, shu = sb("sh_gate", [P, KT, FI]), sb("sh_up", [P, KT, FI])
        sig = sb("sig", [P, FT, TT])
        hid = sb("hid", [P, FT, TT])
        stats, mv, rs = sb("stats", [P, TB, 6]), sb("mv", [P, TB, 2]), sb("rs", [P, 3, TB])
        lT = sb("logitsT", [NE, TT])
        lg = sb("logits", [P, TB, NE])
        top = sb("top", [P, TB, 8])
        topi = sb("topi", [P, TB, 8], U32)
        topf = sb("topf", [P, TB, 8])
        chosen = sb("chosen", [P, TB, NE])
        soft = sb("soft", [P, TB, NE])
        total = sb("total", [P, TB])
        wt = [sb(f"wt{b}", [P, TB, NE]) for b in range(2)]
        keys = sb("keys", [P, TB, 2, NE])
        left = sb("left", [P, TB])
        lefti = sb("lefti", [P, TB], mybir.dt.int32)
        experts = sb("experts", [P, NE])
        expertsi = sb("expertsi", [P, NE], mybir.dt.int32)
        zero = sb("zero", [P, C])
        y_ps = ctx.enter_context(nc.psum_tensor("d_y_ps", [P, 2, C], F32))
        misc = ctx.enter_context(nc.psum_tensor("d_misc_ps", [P, 2, TT], F32))
        gu_ps = ctx.enter_context(nc.psum_tensor("d_gu_ps", [P, 2, 2, TT], F32))
        sh_in = sem("sh_in")
        blk_in = [sem(f"blk_in{b}") for b in range(2)]
        xn_out = [sem(f"xn_out{b}") for b in range(2)]
        wt_out = [sem(f"wt_out{b}") for b in range(2)]
        acc_out = [sem(f"acc_out{b}") for b in range(2)]
        zero_out = sem("zero_out")
        consts = sem("consts")
        const_step = sem("const_step")
        y_ready, y_used = sem("y_ready"), sem("y_used")
        var_ready, sd_ready, xn_ready = sem("var_ready"), sem("sd_ready"), sem("xn_ready")
        misc_ready, misc_done = sem("misc_ready"), sem("misc_done")
        gu_ready, gu_exp, gu_done = sem("gu_ready"), sem("gu_exp"), sem("gu_done")
        soft_in, soft_out, wt_ready, keys_ready = sem("soft_in"), sem("soft_out"), sem("wt_ready"), sem("keys_ready")
        dve_step, dve_passed, pe_passed = sem("dve_step"), sem("dve_passed"), sem("pe_passed")
        block = ctx.enter_context(nc.Block())
        ident, cols = keep["ident"], keep["cols"]
        NL = NT // 2

        def misc_at(b, what, k=0):
            return {"xn": 6 * b + k, "logitsT": 6 * b + 4, "logits": 6 * b + 5, "keys": 12}[what]

        def misc_bank(u):
            return misc[:, u % 2, :]

        @block.sync
        def _(sp):
            sp.dma_start(shg[:, :, :], w_sh_gate.rearrange("(k p) i -> p k i", p=P)).then_inc(sh_in, 16)
            sp.dma_start(shu[:, :, :], w_sh_up.rearrange("(k p) i -> p k i", p=P)).then_inc(sh_in, 16)
            with sp.Fori(0, NL) as it:
                for b in range(2):
                    rows = bass.ds((2 * it + b) * TT, TT)
                    sp.wait_ge(xn_ready, 2 * it + b + 1)
                    sp.dma_start(rows_dram[rows, 0:C].rearrange("(t p) c -> p t c", p=P),
                                   xn[b][:, :, :]).then_inc(xn_out[b], 16)
                    sp.wait_ge(wt_ready, 2 * it + b + 1)
                    sp.dma_start(rows_dram[rows, C:C + NE].rearrange("(t p) c -> p t c", p=P),
                                   wt[b][:, :, :]).then_inc(wt_out[b], 16)
                    sp.wait_ge(y_used, 2 * TB * (2 * it + b) + 2 * TB + 2)
                    sp.dma_start(acc_dram[rows, :].rearrange("(t p) c -> p t c", p=P),
                                   xb[b][:, :, :]).then_inc(acc_out[b], 16)
            for b in range(2):
                sp.wait_ge(xn_out[b], 16 * NL + 16)
                sp.wait_ge(wt_out[b], 16 * NL + 16)
                sp.wait_ge(acc_out[b], 16 * NL + 16)

        @block.gpsimd
        def _(pool):
            done = chained(pool, const_step)
            done(pool.iota(lefti[:, :], [[-P, TB]], base=T, channel_multiplier=-1))
            done(pool.iota(expertsi[:, :], [[1, NE]], base=0, channel_multiplier=0))
            pool.tensor_copy(left[:, :], lefti[:, :]).then_inc(consts, 1)
            pool.tensor_copy(experts[:, :], expertsi[:, :]).then_inc(consts, 1)
            done(pool.memset(zero[:, :], 0.0))
            pool.dma_start(acc_dram[T:T + P, :], zero[:, :]).then_inc(zero_out, 16)
            with pool.Fori(0, NL) as it:
                for b in range(2):
                    pool.wait_ge(acc_out[b], 16 * it + 16)
                    pool.dma_start(oTb[b][:, :, :], oT_dram[:, bass.ds((2 * it + b) * TT, TT)].rearrange(
                        "(k p) t -> p k t", p=P)).then_inc(blk_in[b], 16)
                    pool.dma_start(xb[b][:, :, :], x[bass.ds((2 * it + b) * TT, TT), :].rearrange(
                        "(t p) c -> p t c", p=P)).then_inc(blk_in[b], 16)
            pool.wait_ge(zero_out, 16)

        @block.scalar
        def _(act):
            with act.Fori(0, NL) as it:
                def misc_out(b, what, k=0):
                    u = misc_at(b, what, k)
                    act.wait_ge(misc_ready, MISC * it + u + 1)
                    return misc_bank(u)

                def negated_exp(b, f):
                    act.wait_ge(gu_ready, FT * (2 * it + b) + f + 1)
                    nc.scalar.activation(sig[:, f, :], gu_ps[:, (FT * b + f) % 2, 0, :], ACT.Exp,
                                         scale=-1.0).then_inc(gu_exp, 1)

                for b in range(2):
                    act.wait_ge(var_ready, 2 * it + b + 1)
                    nc.scalar.activation(rs[:, 1, :], rs[:, 0, :], ACT.Sqrt).then_inc(sd_ready, 1)
                    for k in range(KT):
                        bank = misc_out(b, "xn", k)
                        nc.scalar.activation(h2T[b][:, k, :], bank, ACT.Identity, scale=cols[:, CB, k:k + 1],
                                             bias=cols[:, SB, k:k + 1]).then_inc(misc_done, 1)
                    bank = misc_out(b, "logitsT")
                    nc.scalar.copy(lT[:, :], bank[0:NE, :]).then_inc(misc_done, 1)
                    negated_exp(b, 0)
                    bank = misc_out(b, "logits")
                    nc.scalar.copy(lg[:, :, :], bank[:, 0:TB * NE].rearrange("p (t e) -> p t e", t=TB)
                                   ).then_inc(misc_done, 1)
                    negated_exp(b, 1)
                    act.wait_ge(soft_in, 2 * it + b + 1)
                    nc.scalar.activation(soft[:, :, :], soft[:, :, :], ACT.Exp).then_inc(soft_out, 1)
                    negated_exp(b, 2)
                bank = misc_out(1, "keys")
                nc.scalar.copy(keyT[:, bass.ds(it * TT, TT)], bank).then_inc(misc_done, 1)

        @block.vector
        def _(dve):
            nc.vector.memset(keys[:, 0, :, :], 0.0).then_inc(y_used, 2)
            nc.vector.memset(keys[:, 1, :, :], 0.0).then_inc(misc_done, 2)
            nc.vector.memset(keys[:, 2, :, :], 0.0).then_inc(gu_done, 2)
            for b in range(2):
                nc.vector.memset(wt[b][:, 0, :], 0.0).then_inc(acc_out[b], 16)
                nc.vector.memset(wt[b][:, 1, :], 0.0).then_inc(xn_out[b], 16)
                nc.vector.memset(wt[b][:, 2, :], 0.0).then_inc(wt_out[b], 16)
            dve.wait_ge(consts, 2)
            DONES = 2 * CHAIN
            with dve.Fori(0, NL) as it:
                done = chained(dve, dve_step, DONES * it)

                def silu_gated(b, f):
                    pair = gu_ps[:, (FT * b + f) % 2, :, :]
                    dve.wait_ge(gu_exp, FT * (2 * it + b) + f + 1)
                    done(nc.vector.tensor_scalar(sig[:, f, :], sig[:, f, :], 1.0, None, ALU.add))
                    done(nc.vector.reciprocal(sig[:, f, :], sig[:, f, :]))
                    done(nc.vector.tensor_tensor(sig[:, f, :], pair[:, 0, :], sig[:, f, :], ALU.mult))
                    nc.vector.tensor_tensor(hid[:, f, :], pair[:, 1, :], sig[:, f, :],
                                            ALU.mult).then_inc(gu_done, 1)

                for b in range(2):
                    dve.wait_ge(blk_in[b], 32 * it + 32)
                    for t in range(TB):
                        dve.wait_ge(y_ready, 2 * TB * (2 * it + b) + t + 1)
                        last = nc.vector.tensor_tensor(xb[b][:, t, :], y_ps[:, t % 2, :], xb[b][:, t, :], ALU.add)
                        last.then_inc(y_used, 1)
                    dve.wait_ge(y_used, 2 * TB * (2 * it + b) + TB + 2)
                    dve.wait_ge(xn_out[b], 16 * it + 16)
                    normalize_rows(nc, dve, done, xb[b], xn[b], stats, mv, rs, var_ready, sd_ready,
                                   2 * it + b + 1, passed=dve_passed).then_inc(xn_ready, 1)
                    silu_gated(b, 0)
                    wait_apart(dve, dve_passed, misc_done, MISC * it + misc_at(b, "logits") + 1 + 2)
                    for t in range(TB):
                        last = nc.vector.max(top[:, t, :], lg[:, t, :])
                    done(last, dve_passed)
                    for t in range(TB):
                        nc.vector.max_index(topi[:, t, :], top[:, t, :], lg[:, t, :])
                        last = nc.vector.tensor_scalar(soft[:, t, :], lg[:, t, :], top[:, t, 0:1], None, ALU.subtract)
                    last.then_inc(soft_in, 1)
                    dve.wait_ge(soft_in, 2 * it + b + 1)
                    done(nc.vector.tensor_copy(topf[:, :, :], topi[:, :, :]))
                    for t in range(TB):
                        last = nc.vector.tensor_scalar(chosen[:, t, :], experts[:, :], topf[:, t, 0:1], None,
                                                       ALU.is_equal)
                    done(last)
                    for r in range(1, TOPK):
                        for t in range(TB):
                            last = nc.vector.scalar_tensor_tensor(chosen[:, t, :], experts[:, :], topf[:, t, r:r + 1],
                                                                  chosen[:, t, :], ALU.is_equal, ALU.add)
                        done(last)
                    silu_gated(b, 1)
                    dve.wait_ge(soft_out, 2 * it + b + 1)
                    done(nc.vector.tensor_tensor(soft[:, :, :], soft[:, :, :], chosen[:, :, :], ALU.mult))
                    done(nc.vector.reduce_sum(total[:, :], soft[:, :, :], axis=mybir.AxisListType.X))
                    done(nc.vector.reciprocal(total[:, :], total[:, :]))
                    dve.wait_ge(wt_out[b], 16 * it + 16)
                    for t in range(TB):
                        last = nc.vector.tensor_scalar(wt[b][:, t, :], soft[:, t, :], total[:, t:t + 1], None, ALU.mult)
                    last.then_inc(wt_ready, 1)
                    if b == 0:
                        dve.wait_ge(misc_done, MISC * it + 2)
                    for t in range(TB):
                        last = nc.vector.tensor_scalar(keys[:, t, b, :], chosen[:, t, :], left[:, t:t + 1], None,
                                                       ALU.mult)
                    last.then_inc(keys_ready, 1)
                    dve.wait_ge(keys_ready, 2 * it + b + 1)
                    done(nc.vector.tensor_scalar(left[:, :], left[:, :], float(TT), None, ALU.subtract))
                    silu_gated(b, 2)
                    for t in range(TB):
                        dve.wait_ge(y_ready, 2 * TB * (2 * it + b) + TB + t + 1)
                        last = nc.vector.tensor_tensor(xb[b][:, t, :], y_ps[:, t % 2, :], xb[b][:, t, :], ALU.add)
                        last.then_inc(y_used, 1)

        @block.tensor
        def _(pe):
            pe.wait_ge(sh_in, 32)
            with pe.Fori(0, NL) as it:
                def misc_in(b, what, k=0):
                    u = misc_at(b, what, k)
                    pe.wait_ge(misc_done, MISC * it + (u + 1 if u else 2))
                    return misc_bank(u)

                def y_bank(b, u):
                    pe.wait_ge(y_used, 2 * TB * (2 * it + b) + u + 1)
                    return y_ps[:, u % 2, :]

                def gate_up(b, f):
                    pe.wait_ge(gu_done, FT * (2 * it + b) + f + 1)
                    for n, w in enumerate((shg, shu)):
                        for k in range(KT):
                            last = nc.tensor.matmul(gu_ps[:, (FT * b + f) % 2, n, :], w[:, k, f * P:(f + 1) * P],
                                                    h2T[b][:, k, :], start=(k == 0), stop=(k == KT - 1))
                    last.then_inc(gu_ready, 1)

                for b in range(2):
                    pe.wait_ge(blk_in[b], 32 * it + 32)
                    for t in range(TB):
                        bank = y_bank(b, t)
                        for k in range(KT):
                            last = nc.tensor.matmul(bank, oTb[b][:, k, t * P:(t + 1) * P], woT[:, k, :],
                                                    start=(k == 0), stop=(k == KT - 1))
                        last.then_inc(y_ready, 1)
                    pe.wait_ge(xn_ready, 2 * it + b + 1)
                    for k in range(KT):
                        bank = misc_in(b, "xn", k)
                        for t in range(TB):
                            last = nc.tensor.transpose(bank[:, t * P:(t + 1) * P], xn[b][:, t, k * P:(k + 1) * P],
                                                       ident[:, :])
                        last.then_inc(misc_ready, 1)
                    bank = misc_in(b, "logitsT")
                    pe.wait_ge(misc_done, MISC * it + misc_at(b, "xn", KT - 1) + 1 + 2)
                    for k in range(KT):
                        last = nc.tensor.matmul(bank[0:NE, :], wrT[:, k, :], h2T[b][:, k, :],
                                                start=(k == 0), stop=(k == KT - 1))
                    last.then_inc(misc_ready, 1)
                    gate_up(b, 0)
                    bank = misc_bank(misc_at(b, "logits"))
                    wait_apart(pe, pe_passed, misc_done, MISC * it + misc_at(b, "logitsT") + 1 + 2)
                    for t in range(TB):
                        last = nc.tensor.transpose(bank[:, t * NE:(t + 1) * NE], lT[:, t * P:(t + 1) * P],
                                                   ident[0:NE, 0:NE])
                    last.then_inc(misc_ready, 1)
                    gate_up(b, 1)
                    gate_up(b, 2)
                    pe.wait_ge(gu_done, FT * (2 * it + b) + FT + 2)
                    for t in range(TB):
                        bank = y_bank(b, TB + t)
                        for f in range(FT):
                            last = nc.tensor.matmul(bank, hid[:, f, t * P:(t + 1) * P], w_shd[:, f, :],
                                                    start=(f == 0), stop=(f == FT - 1))
                        last.then_inc(y_ready, 1)
                bank = misc_in(1, "keys")
                pe.wait_ge(keys_ready, 2 * it + 2)
                for t in range(TB):
                    last = nc.tensor.transpose(bank[:, t * P:(t + 1) * P], keys[:, t, :, :].rearrange(
                        "p b e -> p (b e)"), ident[:, :])
                last.then_inc(misc_ready, 1)


def slot_lists(nc, keyT, keys_dram, gather_at, add_at, T, keep):
    LARGEST = 2 * (CAP // 8) - 1
    with ExitStack() as ctx:
        half = ctx.enter_context(nc.sbuf_tensor("l_half", [P, CAP], F32))
        both = ctx.enter_context(nc.sbuf_tensor("l_both", [NE, 2, CAP], F32))
        first = ctx.enter_context(nc.sbuf_tensor("l_first", [NE, CAP], F32))
        pairs = ctx.enter_context(nc.sbuf_tensor("l_pairs", [NE // 2, 2 * CAP], F32))
        key = ctx.enter_context(nc.sbuf_tensor("l_key", [P, NE // 2], F32))
        tok = ctx.enter_context(nc.sbuf_tensor("l_tok", [P, NE // 2], F32))
        own = ctx.enter_context(nc.sbuf_tensor("l_own", [P, 2], F32))
        spare = ctx.enter_context(nc.sbuf_tensor("l_spare", [P, NE // 2], F32))
        sparei = ctx.enter_context(nc.sbuf_tensor("l_sparei", [P, NE // 2], mybir.dt.int32))
        ps = ctx.enter_context(nc.psum_tensor("l_ps", [P, C], F32))
        step = ctx.enter_context(nc.semaphore("l_step"))
        both_in = ctx.enter_context(nc.semaphore("l_both_in"))
        first_out = ctx.enter_context(nc.semaphore("l_first_out"))
        pairs_in = ctx.enter_context(nc.semaphore("l_pairs_in"))
        turned = ctx.enter_context(nc.semaphore("l_turned"))
        consts = ctx.enter_context(nc.semaphore("l_consts"))
        block = ctx.enter_context(nc.Block())

        @block.gpsimd
        def _(pool):
            done = chained(pool, consts)
            done(pool.memset(own[:, :], 1.0))
            done(pool.affine_select(out=own[:, 0:1], in_=own[:, 0:1], compare_op=ALU.is_ge, fill=0.0,
                                    base=CAP - 1, pattern=[[0, 1]], channel_multiplier=-1))
            done(pool.affine_select(out=own[:, 1:2], in_=own[:, 1:2], compare_op=ALU.is_ge, fill=0.0,
                                    base=-CAP, pattern=[[0, 1]], channel_multiplier=1))
            done(pool.iota(sparei[:, :], [[0, NE // 2]], base=T, channel_multiplier=1))
            done(pool.tensor_copy(spare[:, :], sparei[:, :]))

        @block.sync
        def _(sp):
            sp.wait_ge(step, LARGEST)
            for b in range(2):
                sp.dma_start(both[:, b, :], half[b * NE:(b + 1) * NE, :]).then_inc(both_in, 16)
            sp.wait_ge(step, 2 * LARGEST)
            sp.dma_start(keys_dram, first[:, :]).then_inc(first_out, 16)
            sp.wait_ge(first_out, 16)
            sp.dma_start(pairs[:, :], keys_dram.rearrange("(m b) s -> m (b s)", b=2)).then_inc(pairs_in, 16)

        @block.tensor
        def _(pe):
            pe.wait_ge(pairs_in, 16)
            nc.tensor.transpose(ps[:, 0:NE // 2], pairs[:, :], keep["ident"][0:NE // 2, 0:NE // 2]).then_inc(turned, 1)

        @block.vector
        def _(dve):
            done = chained(dve, step)

            def largest(out, src):
                for r in range(0, CAP, 8):
                    done(nc.vector.max(out[:, r:r + 8], src))
                    if r + 8 < CAP:
                        done(nc.vector.match_replace(src, out[:, r:r + 8], src, 0.0))

            largest(half[:, :], keyT[:, :])
            dve.wait_ge(both_in, 32)
            largest(first[:, :], both[:, :, :].rearrange("p b s -> p (b s)"))
            dve.wait_ge(turned, 1)
            dve.wait_ge(consts, 5)
            done(nc.vector.memset(gather_at[:, NE // 2:], 0))
            done(nc.vector.memset(add_at[:, :, NE // 2:], 0))
            done(nc.vector.tensor_copy(key[:, :], ps[:, 0:NE // 2]))
            done(nc.vector.tensor_scalar(tok[:, :], key[:, :], -1.0, float(T), ALU.mult, ALU.add))
            done(nc.vector.tensor_scalar(gather_at[:, 0:NE // 2], tok[:, :], float(T - 1), None, ALU.min))
            for b in range(2):
                done(nc.vector.tensor_tensor(tok[:, :], tok[:, :], spare[:, :], ALU.subtract))
                done(nc.vector.scalar_tensor_tensor(tok[:, :], key[:, :], 0.0, tok[:, :], ALU.is_gt, ALU.mult))
                done(nc.vector.scalar_tensor_tensor(tok[:, :], tok[:, :], own[:, b:b + 1], spare[:, :],
                                                    ALU.mult, ALU.add))
                done(nc.vector.tensor_copy(add_at[:, b, 0:NE // 2], tok[:, :]))
                done(nc.vector.tensor_scalar(tok[:, :], key[:, :], -1.0, float(T), ALU.mult, ALU.add))


def experts_part(nc, rows_dram, acc_dram, w_gate, w_up, w_down, gather_at, add_at, T, keep):
    NL = NE // 4
    RW = C + NE
    with ExitStack() as ctx:
        def sb(name, shape, dt=F32):
            return ctx.enter_context(nc.sbuf_tensor("e_" + name, shape, dt))

        def sem(name):
            return ctx.enter_context(nc.semaphore("e_" + name))

        wg = [sb(f"wg{b}", [P, 2, KT, FI]) for b in range(2)]
        wu = [sb(f"wu{b}", [P, 2, KT, FI]) for b in range(2)]
        wd = [sb(f"wd{b}", [P, 2, FT, C]) for b in range(2)]
        xg = [sb(f"xg{b}", [P, RW]) for b in range(2)]
        xeT = [sb(f"xeT{b}", [P, KT, P]) for b in range(2)]
        sig = [sb(f"sig{b}", [P, FI]) for b in range(2)]
        hidT = [sb(f"hidT{b}", [P, FT, P]) for b in range(2)]
        wcol = [sb(f"wcol{b}", [P, 1]) for b in range(2)]
        at = [sb(f"at{b}", [P, 3], U32) for b in range(2)]
        y = [sb(f"y{b}", [P, C]) for b in range(2)]
        x_ps = ctx.enter_context(nc.psum_tensor("e_x_ps", [P, KT, P], F32))
        gu_ps = ctx.enter_context(nc.psum_tensor("e_gu_ps", [P, 2, C], F32))
        h_ps = ctx.enter_context(nc.psum_tensor("e_h_ps", [P, C], F32))
        y_ps = ctx.enter_context(nc.psum_tensor("e_y_ps", [P, 2, C], F32))
        gu_in = [sem(f"gu_in{b}") for b in range(2)]
        d_in = [sem(f"d_in{b}") for b in range(2)]
        x_in = [sem(f"x_in{b}") for b in range(2)]
        added, pair_added = sem("added"), sem("pair_added")
        at_ready = sem("at_ready")
        x_ready, xe_ready = sem("x_ready"), sem("xe_ready")
        gu_ready, sig_ready, hid_ready = sem("gu_ready"), sem("sig_ready"), sem("hid_ready")
        hT_ready, hT_copied, y_ready, y_done = sem("hT_ready"), sem("hT_copied"), sem("y_ready"), sem("y_done")
        step, pool_passed = sem("step"), sem("pool_passed")
        block = ctx.enter_context(nc.Block())
        ident, cols, gates = keep["ident"], keep["cols"], keep["gates"]
        slots = [slice(0, CAP), slice(CAP, 2 * CAP)]

        @block.sync
        def _(sp):
            with sp.Fori(0, NL) as it:
                for b in range(2):
                    n = 2 * it + b
                    sp.wait_ge(gu_ready, n + 1)
                    sp.dma_start(wg[b][:, :, :, :], w_gate[bass.ds(n * 2, 2), :, :].rearrange(
                        "e (k p) i -> p e k i", p=P)).then_inc(gu_in[b], 16)
                    sp.dma_start(wu[b][:, :, :, :], w_up[bass.ds(n * 2, 2), :, :].rearrange(
                        "e (k p) i -> p e k i", p=P)).then_inc(gu_in[b], 16)
                    sp.wait_ge(y_ready, n + 1)
                    sp.dma_start(wd[b][:, :, :, :], w_down[bass.ds(n * 2, 2), :, :].rearrange(
                        "e (f p) c -> p e f c", p=P)).then_inc(d_in[b], 16)

        @block.gpsimd
        def _(pool):
            def gather(b, n):
                wait_apart(pool, pool_passed, at_ready, n + 1)
                pool.indirect_dma_start(xg[b][:, :], None, rows_dram, bass.IndirectOffsetOnAxis(
                    ap=at[b][:, 0:1], axis=0), bounds_check=T - 1, oob_is_err=True).then_inc(x_in[b], 16)

            gather(0, 0)
            with pool.Fori(0, NL) as it:
                for b in range(2):
                    n = 2 * it + b
                    gather(1 - b, n + 1)
                    wait_apart(pool, pool_passed, y_done, n + 1)
                    for one in range(2):
                        pool.indirect_dma_start(acc_dram, bass.IndirectOffsetOnAxis(
                            ap=at[b][:, 1 + one:2 + one], axis=0), y[b][:, :], None, bounds_check=T + P - 1,
                            oob_is_err=True, compute_op=ALU.add).then_inc(added, 16)
                        wait_apart(pool, pool_passed, added, 16 * (2 * n + one + 1))
                    pool.sem_inc(pair_added, 1)
            pool.wait_ge(x_in[0], 16 * (NL + 1))

        @block.scalar
        def _(act):
            with act.Fori(0, NL) as it:
                for b in range(2):
                    n = 2 * it + b
                    act.wait_ge(x_ready, n + 1)
                    for k in range(KT):
                        last = nc.scalar.activation(xeT[b][:, k, :], x_ps[:, k, :], ACT.Identity,
                                                    scale=cols[:, CB, k:k + 1], bias=cols[:, SB, k:k + 1])
                    last.then_inc(xe_ready, 1)
                    act.wait_ge(gu_ready, n + 3)
                    nc.scalar.activation(sig[b][:, :], gu_ps[:, 0, 0:FI], ACT.Exp, scale=-1.0).then_inc(sig_ready, 1)
                    act.wait_ge(hT_ready, n + 1)
                    nc.scalar.copy(hidT[b][:, :, :], h_ps[:, 0:FT * P].rearrange("p (f s) -> p f s", f=FT)
                                   ).then_inc(hT_copied, 1)

        @block.vector
        def _(dve):
            nc.vector.memset(wcol[0][:, :], 0.0).then_inc(gu_ready, 2)
            nc.vector.memset(wcol[1][:, :], 0.0).then_inc(y_ready, 2)
            nc.vector.memset(y[0][:, :], 0.0).then_inc(pair_added, 1)

            def rows_of(b, n):
                nc.vector.tensor_copy(at[b][:, 0:1], gather_at[:, bass.ds(n, 1)])
                nc.vector.tensor_copy(at[b][:, 1:2], add_at[:, 0, bass.ds(n, 1)])
                return nc.vector.tensor_copy(at[b][:, 2:3], add_at[:, 1, bass.ds(n, 1)])

            rows_of(0, 0).then_inc(at_ready, 1)
            with dve.Fori(0, NL) as it:
                done = chained(dve, step, 8 * it)
                for b in range(2):
                    n = 2 * it + b
                    dve.wait_ge(sig_ready, n + 1)
                    done(nc.vector.tensor_scalar(sig[b][:, :], sig[b][:, :], 1.0, None, ALU.add))
                    done(nc.vector.reciprocal(sig[b][:, :], sig[b][:, :]))
                    done(nc.vector.tensor_tensor(sig[b][:, :], gu_ps[:, 0, 0:FI], sig[b][:, :], ALU.mult))
                    nc.vector.tensor_tensor(sig[b][:, :], gu_ps[:, 1, 0:FI], sig[b][:, :],
                                            ALU.mult).then_inc(hid_ready, 1)
                    dve.wait_ge(pair_added, n + 1)
                    rows_of(1 - b, n + 1).then_inc(at_ready, 1)
                    dve.wait_ge(x_in[b], 16 * it + 16)
                    nc.vector.tensor_copy(wcol[b][0:CAP, :], xg[b][0:CAP, bass.ds(2 * n + C, 1)])
                    done(nc.vector.tensor_copy(wcol[b][CAP:, :], xg[b][CAP:, bass.ds(2 * n + C + 1, 1)]))
                    dve.wait_ge(y_ready, n + 3)
                    nc.vector.scalar_tensor_tensor(y[b][:, :], y_ps[:, b, :], wcol[b][:, 0:1], gates[:, 1, :],
                                                   ALU.mult, ALU.mult).then_inc(y_done, 1)

        @block.tensor
        def _(pe):
            with pe.Fori(0, NL) as it:
                for b in range(2):
                    n = 2 * it + b
                    pe.wait_ge(x_in[b], 16 * it + 16)
                    for k in range(KT):
                        last = nc.tensor.transpose(x_ps[:, k, :], xg[b][:, k * P:(k + 1) * P], ident[:, :])
                    last.then_inc(x_ready, 1)
                    pe.wait_ge(xe_ready, n + 1)
                    pe.wait_ge(gu_in[b], 32 * it + 32)
                    for j, wj in enumerate((wg[b], wu[b])):
                        for k in range(KT):
                            for e in range(2):
                                last = nc.tensor.matmul(gu_ps[slots[e], j, 0:FI], xeT[b][:, k, slots[e]],
                                                        wj[:, e, k, :], start=(k == 0), stop=(k == KT - 1))
                    last.then_inc(gu_ready, 1)
                    pe.wait_ge(hid_ready, n + 1)
                    for f in range(FT):
                        last = nc.tensor.transpose(h_ps[:, f * P:(f + 1) * P], sig[b][:, f * P:(f + 1) * P],
                                                   ident[:, :])
                    last.then_inc(hT_ready, 1)
                    pe.wait_ge(hT_copied, n + 1)
                    pe.wait_ge(d_in[b], 16 * it + 16)
                    for f in range(FT):
                        for e in range(2):
                            last = nc.tensor.matmul(y_ps[slots[e], b, :], hidT[b][:, f, slots[e]], wd[b][:, e, f, :],
                                                    start=(f == 0), stop=(f == FT - 1))
                    last.then_inc(y_ready, 1)


def copy_out(nc, acc_dram, out, T):
    with nc.semaphore("out_done") as out_done, nc.Block() as block:
        @block.sync
        def _(sp):
            for n in range(T // TT):
                sp.dma_start(out[n * TT:(n + 1) * TT, :], acc_dram[n * TT:(n + 1) * TT, :]).then_inc(out_done, 16)
            sp.wait_ge(out_done, 16 * (T // TT))


def layer_kernel(nc, x3, wq, wk, wv, wo, w_router, w_gate, w_up, w_down, w_sh_gate, w_sh_up, w_sh_down,
                 c, wmod, out3):
    x, out = x3[0], out3[0]
    T = x.shape[0]
    oT_dram = nc.dram_tensor("oT_scratch", (C, T), F32).ap()
    rows_dram = nc.dram_tensor("rows_scratch", (T, C + NE), F32).ap()
    acc_dram = nc.dram_tensor("acc_scratch", (T + P, C), F32).ap()
    keys_dram = nc.dram_tensor("keys_scratch", (NE, CAP), F32).ap()
    with ExitStack() as ctx:
        keep = {
            "ident": ctx.enter_context(nc.sbuf_tensor("ident", [P, P], F32)),
            "ones": ctx.enter_context(nc.sbuf_tensor("ones", [P, P], F32)),
            "cols": ctx.enter_context(nc.sbuf_tensor("mod_cols", [P, MODS, KT], F32)),
            "gates": ctx.enter_context(nc.sbuf_tensor("gates", [P, 2, C], F32)),
        }
        modulation(nc, c, wmod, keep)
        with nc.sbuf_tensor("hT", [P, KT, T], F32) as hT:
            first_norm(nc, x, hT, keep)
            attention(nc, hT, wq, wk, wv, oT_dram, keep)
        gather_at = ctx.enter_context(nc.sbuf_tensor("gather_at", [P, NE // 2 + 1], U32))
        add_at = ctx.enter_context(nc.sbuf_tensor("add_at", [P, 2, NE // 2 + 1], U32))
        with (nc.sbuf_tensor("keyT", [P, T // 2], F32) as keyT, nc.sbuf_tensor("woT", [P, KT, C], F32) as woT,
              nc.sbuf_tensor("wrT", [P, KT, NE], F32) as wrT, nc.sbuf_tensor("w_shd", [P, FT, C], F32) as w_shd):
            turn_weights(nc, wo, w_router, woT, wrT, w_shd, w_sh_down, keep)
            dense_part(nc, x, oT_dram, rows_dram, acc_dram, w_sh_gate, w_sh_up, woT, wrT, w_shd, keyT, keep)
            slot_lists(nc, keyT, keys_dram, gather_at, add_at, T, keep)
        experts_part(nc, rows_dram, acc_dram, w_gate, w_up, w_down, gather_at, add_at, T, keep)
        copy_out(nc, acc_dram, out, T)


_INS = ['L0_attn_x', 'L0_attn_Wq', 'L0_attn_Wk', 'L0_attn_Wv', 'L0_attn_Wo', 'L0_ffn_w_router', 'L0_ffn_w_gate',
        'L0_ffn_w_up', 'L0_ffn_w_down', 'L0_ffn_w_sh_gate', 'L0_ffn_w_sh_up', 'L0_ffn_w_sh_down', 'L0_c', 'L0_wmod']
_OUTS = [((1, 4096, 512), 'float32')]


def kernel(**inputs):
    import numpy as _np
    import concourse.bacc as _bacc
    from concourse import mybir as _mybir
    from concourse.bass_utils import run_bass_kernel_spmd as _run

    nc = _bacc.Bacc("TRN2", target_bir_lowering=False, num_devices=1)
    arrays, args = {}, []
    for name in _INS:
        a = _np.ascontiguousarray(inputs[name])
        arrays[f"in_{name}_dram"] = a
        args.append(nc.dram_tensor(f"in_{name}_dram", a.shape, _mybir.dt.from_np(a.dtype), kind="ExternalInput").ap())
    for i, (shape, dtype) in enumerate(_OUTS):
        dt = _mybir.dt.from_np(_np.dtype(dtype))
        args.append(nc.dram_tensor(f"out_{i}_dram", shape, dt, kind="ExternalOutput").ap())
    layer_kernel(nc, *args)
    r = _run(nc, [arrays], core_ids=[0])
    return r.results[0]["out_0_dram"]
```

```python
import concourse.bass as bass
from concourse import mybir
from contextlib import ExitStack

F32 = mybir.dt.float32
F32R = mybir.dt.float32r
U32 = mybir.dt.uint32
ALU = mybir.AluOpType
ACT = mybir.ActivationFunctionType

P = 128
C = 512
KT = C // P
H = 16
HD = C // H
HG = P // HD
NG = H // HG
TT = 512
TB = TT // P
SHIFT = 0.1
ATT_EPS = 1e-6
LN_EPS = 1e-5
NE = 64
TOPK = 4
CAP = 64
FI = 384
FT = FI // P
MODS = 6
SA, CA, GA, SB, CB, GB = range(MODS)
GATED = 0.5


def wait_apart(eng, passed, *waits):
    for sem, value in zip(waits[::2], waits[1::2]):
        eng.wait_ge(sem, value)
    eng.sem_inc(passed, 1)


def chained(eng, sem, base=0):
    count = [base]

    def done(ins, passed=None):
        count[0] = count[0] + 1
        ins.then_inc(sem, 1)
        if passed:
            wait_apart(eng, passed, sem, count[0])
        else:
            eng.wait_ge(sem, count[0])

    return done


def modulation(nc, c, wmod, keep):
    with ExitStack() as ctx:
        ccol = ctx.enter_context(nc.sbuf_tensor("ccol", [P, KT], F32))
        cexp = ctx.enter_context(nc.sbuf_tensor("cexp", [P, KT], F32))
        crep = ctx.enter_context(nc.sbuf_tensor("crep", [P, KT, P], F32))
        wm = ctx.enter_context(nc.sbuf_tensor("wm", [P, KT, MODS * C], F32))
        rows = ctx.enter_context(nc.sbuf_tensor("mod_rows", [P, MODS, C], F32))
        sign = ctx.enter_context(nc.sbuf_tensor("gate_sign", [P, C], F32))
        size = ctx.enter_context(nc.sbuf_tensor("gate_size", [P, C], F32))
        banks = ctx.enter_context(nc.psum_tensor("mod_ps", [P, MODS, C], F32))
        turned = ctx.enter_context(nc.psum_tensor("mod_turned", [P, 2, C], F32))
        c_in = ctx.enter_context(nc.semaphore("c_in"))
        wm_in = ctx.enter_context(nc.semaphore("wm_in"))
        c_exp = ctx.enter_context(nc.semaphore("c_exp"))
        c_ready = ctx.enter_context(nc.semaphore("c_ready"))
        dve_step = ctx.enter_context(nc.semaphore("mod_dve_step"))
        pool_step = ctx.enter_context(nc.semaphore("mod_pool_step"))
        mod_ready = ctx.enter_context(nc.semaphore("mod_ready"))
        rows_ready = ctx.enter_context(nc.semaphore("rows_ready"))
        turned_ready = ctx.enter_context(nc.semaphore("turned_ready"))
        turned_used = ctx.enter_context(nc.semaphore("turned_used"))
        block = ctx.enter_context(nc.Block())
        ident, cols, gates = keep["ident"], keep["cols"], keep["gates"]
        columns = [SA, CA, SB, CB]

        @block.sync
        def _(sp):
            sp.dma_start(ccol[:, :], c[0, :].rearrange("(p k) -> p k", p=P)).then_inc(c_in, 16)
            sp.dma_start(wm[:, :, :], wmod.rearrange("(p k) n -> p k n", p=P)).then_inc(wm_in, 16)

        @block.gpsimd
        def _(pool):
            done = chained(pool, pool_step)
            done(pool.memset(ident[:, :], 0.0))
            done(pool.affine_select(out=ident[:, :], in_=ident[:, :], compare_op=ALU.not_equal, fill=1.0,
                                    base=0, pattern=[[-1, P]], channel_multiplier=1))
            done(pool.memset(keep["ones"][:, :], 1.0))

        @block.scalar
        def _(act):
            act.wait_ge(c_in, 16)
            nc.scalar.activation(cexp[:, :], ccol[:, :], ACT.Exp, scale=-1.0).then_inc(c_exp, 1)
            for m in range(MODS):
                act.wait_ge(mod_ready, m + 1)
                nc.scalar.copy(rows[:, m, :], banks[:, m, :]).then_inc(rows_ready, 1)

        @block.vector
        def _(dve):
            done = chained(dve, dve_step)
            dve.wait_ge(c_exp, 1)
            done(nc.vector.tensor_scalar(cexp[:, :], cexp[:, :], 1.0, None, ALU.add))
            done(nc.vector.reciprocal(cexp[:, :], cexp[:, :]))
            done(nc.vector.tensor_tensor(ccol[:, :], ccol[:, :], cexp[:, :], ALU.mult))
            done(nc.vector.memset(crep[:, :, :], 1.0))
            for k in range(KT):
                nc.vector.tensor_scalar(crep[:, k, :], crep[:, k, :], ccol[:, k:k + 1], None,
                                        ALU.mult).then_inc(c_ready, 1)
            for n, m in enumerate(columns):
                dve.wait_ge(turned_ready, n + 1)
                one = 1.0 if m in (CA, CB) else 0.0
                src = turned[:, n % 2, :].rearrange("p (k t) -> p k t", k=KT)[:, :, 0]
                nc.vector.tensor_scalar(cols[:, m, :], src, one, None, ALU.add).then_inc(turned_used, 1)
            for n, (m, part) in enumerate(((GA, 1.0), (GB, GATED))):
                dve.wait_ge(rows_ready, m + 1)
                g = rows[:, m, :]
                done(nc.vector.tensor_scalar(sign[:, :], g, 0.0, 2.0 * part, ALU.is_ge, ALU.mult))
                done(nc.vector.tensor_scalar(sign[:, :], sign[:, :], part, None, ALU.subtract))
                done(nc.vector.scalar_tensor_tensor(size[:, :], g, -1.0, g, ALU.mult, ALU.max))
                done(nc.vector.scalar_tensor_tensor(gates[:, n, :], size[:, :], 0.25, sign[:, :],
                                                    ALU.max, ALU.mult))

        @block.tensor
        def _(pe):
            pe.wait_ge(c_ready, KT)
            pe.wait_ge(wm_in, 16)
            for m in range(MODS):
                for k in range(KT):
                    last = nc.tensor.matmul(banks[:, m, :], crep[:, k, :], wm[:, k, m * C:(m + 1) * C],
                                            start=(k == 0), stop=(k == KT - 1))
                last.then_inc(mod_ready, 1)
            pe.wait_ge(pool_step, 2)
            for n, m in enumerate(columns):
                pe.wait_ge(rows_ready, m + 1)
                if n >= 2:
                    pe.wait_ge(turned_used, n - 1)
                for k in range(KT):
                    last = nc.tensor.transpose(turned[:, n % 2, k * P:(k + 1) * P],
                                               rows[:, m, k * P:(k + 1) * P], ident[:, :])
                last.then_inc(turned_ready, 1)


def normalize_rows(nc, dve, done, xb, xn, stats, mv, rs, var_ready, sd_ready, sd_count, passed=None):
    for t in range(TB):
        last = nc.vector.bn_stats(stats[:, t, :], xb[:, t, :])
    done(last, passed)
    for t in range(TB):
        last = nc.vector.bn_aggr(mv[:, t, :], stats[:, t, :])
    done(last)
    nc.vector.tensor_scalar(rs[:, 0, :], mv[:, :, 1], LN_EPS, None, ALU.add).then_inc(var_ready, 1)
    dve.wait_ge(sd_ready, sd_count)
    done(nc.vector.reciprocal(rs[:, 2, :], rs[:, 1, :]))
    done(nc.vector.tensor_tensor(rs[:, 1, :], rs[:, 2, :], rs[:, 2, :], ALU.mult))
    done(nc.vector.tensor_tensor(rs[:, 1, :], rs[:, 1, :], rs[:, 0, :], ALU.mult))
    done(nc.vector.tensor_scalar(rs[:, 1, :], rs[:, 1, :], -0.5, 1.5, ALU.mult, ALU.add))
    done(nc.vector.tensor_tensor(rs[:, 2, :], rs[:, 2, :], rs[:, 1, :], ALU.mult))
    for t in range(TB):
        last = nc.vector.tensor_scalar(xn[:, t, :], xb[:, t, :], mv[:, t, 0:1], rs[:, 2, t:t + 1],
                                       ALU.subtract, ALU.mult)
    return last


def first_norm(nc, x, hT_dram, keep):
    T = x.shape[0]
    NT = T // TT
    with ExitStack() as ctx:
        xb = [ctx.enter_context(nc.sbuf_tensor(f"n1_x{b}", [P, TB, C], F32)) for b in range(2)]
        hT = ctx.enter_context(nc.sbuf_tensor("n1_hT", [P, 2, KT, TT], F32))
        stats = ctx.enter_context(nc.sbuf_tensor("n1_stats", [P, TB, 6], F32))
        mv = ctx.enter_context(nc.sbuf_tensor("n1_mv", [P, TB, 2], F32))
        rs = ctx.enter_context(nc.sbuf_tensor("n1_rs", [P, 3, TB], F32))
        ps = ctx.enter_context(nc.psum_tensor("n1_ps", [P, 2, KT, TT], F32))
        x_in = [ctx.enter_context(nc.semaphore(f"n1_x_in{b}")) for b in range(2)]
        var_ready = ctx.enter_context(nc.semaphore("n1_var_ready"))
        sd_ready = ctx.enter_context(nc.semaphore("n1_sd_ready"))
        xn_ready = ctx.enter_context(nc.semaphore("n1_xn_ready"))
        turned = ctx.enter_context(nc.semaphore("n1_turned"))
        written = ctx.enter_context(nc.semaphore("n1_written"))
        hT_out = [ctx.enter_context(nc.semaphore(f"n1_hT_out{b}")) for b in range(2)]
        dve_step = ctx.enter_context(nc.semaphore("n1_dve_step"))
        block = ctx.enter_context(nc.Block())
        ident, cols = keep["ident"], keep["cols"]

        @block.sync
        def _(sp):
            def store(n):
                sp.wait_ge(written, KT * (n + 1))
                sp.dma_start(hT_dram[:, n * TT:(n + 1) * TT].rearrange("(k p) t -> p k t", p=P),
                             hT[:, n % 2, :, :]).then_inc(hT_out[n % 2], 16)

            for n in range(NT):
                if n >= 2:
                    sp.wait_ge(turned, KT * (n - 1))
                sp.dma_start(xb[n % 2][:, :, :], x[n * TT:(n + 1) * TT, :].rearrange(
                    "(t p) c -> p t c", p=P)).then_inc(x_in[n % 2], 16)
                if n >= 1:
                    store(n - 1)
            store(NT - 1)
            for b in range(2):
                sp.wait_ge(hT_out[b], 16 * (NT // 2))

        @block.vector
        def _(dve):
            done = chained(dve, dve_step)
            for n in range(NT):
                dve.wait_ge(x_in[n % 2], 16 * (n // 2 + 1))
                last = normalize_rows(nc, dve, done, xb[n % 2], xb[n % 2], stats, mv, rs, var_ready, sd_ready, n + 1)
                last.then_inc(xn_ready, 1)

        @block.scalar
        def _(act):
            def root(n):
                act.wait_ge(var_ready, n + 1)
                nc.scalar.activation(rs[:, 1, :], rs[:, 0, :], ACT.Sqrt).then_inc(sd_ready, 1)

            root(0)
            for n in range(NT):
                if n + 1 < NT:
                    root(n + 1)
                if n >= 2:
                    act.wait_ge(hT_out[n % 2], 16 * (n // 2))
                for k in range(KT):
                    act.wait_ge(turned, KT * n + k + 1)
                    nc.scalar.activation(hT[:, n % 2, k, :], ps[:, n % 2, k, :], ACT.Identity,
                                         scale=cols[:, CA, k:k + 1],
                                         bias=cols[:, SA, k:k + 1]).then_inc(written, 1)

        @block.tensor
        def _(pe):
            for n in range(NT):
                pe.wait_ge(xn_ready, n + 1)
                for k in range(KT):
                    if n >= 2:
                        pe.wait_ge(written, KT * (n - 2) + k + 1)
                    for t in range(TB):
                        last = nc.tensor.transpose(ps[:, n % 2, k, t * P:(t + 1) * P],
                                                   xb[n % 2][:, t, k * P:(k + 1) * P], ident[:, :])
                    last.then_inc(turned, 1)


def attention_plan(NT):
    plan, late, quarters = [], [], []
    for i in range(NT):
        steps = TB * (i + 1)
        jobs = [("k", i + 1, 0), ("q", i + 1, 0), ("v", i + 1, 0), ("h", i + 2, 0)]
        if i + 1 == NT:
            jobs = [("w", 0, 0), ("w", 1, 0), ("w", 2, 0)] + jobs
        first = TB if i + 1 == NT else 0
        at = {}
        for n, job in enumerate(jobs):
            at.setdefault(first + n * (steps - first) // len(jobs), []).append(job)
        for j in range(steps):
            plan.append(("s", i, j))
            late.append((i, j))
            if len(late) > 2:
                products(plan, quarters, NT, *late.pop(0))
            plan.append(("t", i, j))
            plan += at.get(j, [])
            if quarters:
                plan.append(quarters.pop(0))
            li, lj = late[0]
            if len(late) > 1 and lj < TB * li:
                plan.append(("a", li, lj))
    for i, j in late:
        products(plan, quarters, NT, i, j)
    return plan + quarters


def products(plan, quarters, NT, i, j):
    if j % TB == 1 and j > 1:
        plan.append(("d", i, j // TB - 1))
    plan.append(("p", i, j))
    if j == TB * (i + 1) - 1:
        plan.append(("n", i, 0))
        quarters += [("r", i, q) for q in range(4)]


def attention(nc, hT_dram, T, wq, wk, wv, oT_dram, keep):
    NT = T // TT
    plan = attention_plan(NT)
    first_jobs = [("w", 0, 0), ("w", 1, 0), ("w", 2, 0), ("k", 0, 0), ("q", 0, 0), ("v", 0, 0)]
    STEPS = sum(e[0] == "s" for e in plan)
    ADDS = sum(e[0] == "a" and e[2] % TB > 0 for e in plan)
    CHUNKS = sum(e[0] == "d" for e in plan)
    kinds = [e[0] for e in plan if e[0] in "wkqv"]
    JOBS = len(kinds)
    RESTS = 2 * NT
    assert STEPS % 4 == 0 and NT % 2 == 0 and CHUNKS % 2 == 0
    scale = HD ** -0.5
    MOVES = 16 * 4 * HG

    def before(event, what, order=plan):
        return sum(what(e) for e in order[:order.index(event) + 1])

    def rests(jobs):
        return sum(kind in "kq" for kind in kinds[:jobs])

    def step_of(i, j):
        return TB * i * (i + 1) // 2 + j

    def width(i, j):
        return max(0, (j - TB * i) * P)

    def adds_for(i, j):
        if j >= TB * i:
            return 0
        return before(("a", i, j if j % TB else j + 1), lambda e: e[0] == "a" and e[2] % TB > 0)

    with ExitStack() as ctx:
        def sb(name, shape, dt=F32):
            return ctx.enter_context(nc.sbuf_tensor("at_" + name, shape, dt))

        def sem(name):
            return ctx.enter_context(nc.semaphore("at_" + name))

        wraw, wT = sb("w_rows", [P, 3, C]), sb("w_turned", [P, 3, KT, P])
        hT = sb("hT", [P, 2, KT, TT])
        kst, qst = sb("k_stack", [P, HG, T], F32R), sb("q_stack", [P, 2, HG, TT], F32R)
        kpart, qpart = sb("k_parts", [P, 2, TT], F32R), sb("q_parts", [P, 2, TT], F32R)
        vals = sb("vals", [P, T // P, P])
        w = sb("w", [P, 4, HG, TT])
        acc = sb("acc", [P, 2, HG, TT])
        rden, o = sb("rden", [P, TT]), sb("o", [P, 2, TT])
        s_ps = ctx.enter_context(nc.psum_tensor("s_ps", [P, HG, TT], F32))
        num = ctx.enter_context(nc.psum_tensor("num_ps", [P, TT], F32))
        den = ctx.enter_context(nc.psum_tensor("den_ps", [P, TT], F32))
        job_ps = ctx.enter_context(nc.psum_tensor("job_ps", [P, 2, TT], F32))
        w_in, job_ready, job_hi, rest_done = sem("w_in"), sem("job_ready"), sem("job_hi"), sem("rest_done")
        hT_in = [sem(f"hT_in{b}") for b in range(2)]
        k_in, q_in, s_ready = sem("k_in"), sem("q_in"), sem("s_ready")
        relu_a, relu_b_act, relu_b_dve = sem("relu_a"), sem("relu_b_act"), sem("relu_b_dve")
        masked, pv_done, added, chunk_done = sem("masked"), sem("pv_done"), sem("added"), sem("chunk_done")
        num_out, den_out, rden_ready, o_ready = sem("num_out"), sem("den_out"), sem("rden_ready"), sem("o_ready")
        o_out = [sem(f"o_out{b}") for b in range(2)]
        pool_passed = sem("pool_passed")
        block = ctx.enter_context(nc.Block())
        ident, ones = keep["ident"], keep["ones"]

        def relu_done(eng, g, step, half):
            if half == 0:
                eng.wait_ge(relu_a, g * STEPS + step + 1)
            elif step % 4 == 0:
                eng.wait_ge(relu_b_dve, g * (STEPS // 4) + step // 4 + 1)
            else:
                eng.wait_ge(relu_b_act, g * (STEPS // 4 * 3) + step - step // 4)

        def w_free(eng, g, i, j):
            step = step_of(i, j)
            eng.wait_ge(pv_done, g * STEPS + step + 1)
            if step >= 4:
                li = i if j >= 4 else i - 1
                need = adds_for(li, j - 4 if j >= 4 else TB * i + j - 4)
                if need:
                    eng.wait_ge(added, g * ADDS + need)

        @block.sync
        def _(sp):
            def load_w(g):
                for n, src in enumerate((wq, wk, wv)):
                    sp.dma_start(wraw[:, n, :], src[bass.ds(g * P, P), :]).then_inc(w_in, 16)

            def load_h(i):
                sp.dma_start(hT[:, i % 2, :, :], hT_dram[:, i * TT:(i + 1) * TT].rearrange(
                    "(k p) t -> p k t", p=P)).then_inc(hT_in[i % 2], 16)

            def stack(kind, i, count):
                sp.wait_ge(rest_done, count)
                for h in range(HG):
                    for r in range(4):
                        part, dst, done = ((kpart[:, r % 2, :], kst[:, h, i * TT:(i + 1) * TT], k_in)
                                           if kind == "k" else
                                           (qpart[:, r // 2, :], qst[:, i % 2, h, :], q_in))
                        sp.dma_start(dst[r * HD:(r + 1) * HD, :].bitcast(F32),
                                     part[h * HD:(h + 1) * HD, :].bitcast(F32)).then_inc(done, 16)

            load_w(0)
            load_h(0)
            load_h(1)
            stack("k", 0, 1)
            stack("q", 0, 2)
            with sp.Fori(0, NG) as g:
                job = 0
                for kind, i, j in plan:
                    if kind in "wkqv":
                        job += 1
                    if kind in "kq":
                        stack(kind, i % NT, g * RESTS + 2 + rests(job))
                    elif kind == "v" and i == 1:
                        sp.wait_ge(job_ready, g * JOBS + 6)
                        load_w((g + 1) % NG)
                    elif kind == "h":
                        sp.wait_ge(job_ready, g * JOBS + 6 + job - 3)
                        load_h(i % NT)
                    elif kind == "r" and j == 3:
                        sp.wait_ge(o_ready, 4 * (g * NT + i) + 4)
                        sp.dma_start(oT_dram[bass.ds(g * P, P), i * TT:(i + 1) * TT],
                                     o[:, i % 2, :]).then_inc(o_out[i % 2], 16)
            for b in range(2):
                sp.wait_ge(o_out[b], 16 + 16 * NG * NT // 2)
                sp.wait_ge(hT_in[b], 16 * (NG * NT // 2 + 1))
            for done in (k_in, q_in):
                sp.wait_ge(done, MOVES * (NG * NT + 1))

        @block.scalar
        def _(act):
            def take_job(kind, i, job, count):
                bank = job_ps[:, job % 2, :]
                act.wait_ge(job_ready, count)
                if kind == "w":
                    nc.scalar.copy(wT[:, i, :, :], bank.rearrange("p (k o) -> p k o", k=KT)).then_inc(job_hi, 1)
                elif kind == "v":
                    nc.scalar.copy(vals[:, TB * i:TB * (i + 1), :],
                                   bank.rearrange("p (t o) -> p t o", t=TB)).then_inc(job_hi, 1)
                elif kind == "k":
                    nc.scalar.copy(kpart[:, 0, :], bank).then_inc(job_hi, 1)
                else:
                    nc.scalar.mul(qpart[:, 0, :], bank, scale).then_inc(job_hi, 1)

            for job, (kind, i, _) in enumerate(first_jobs):
                take_job(kind, i, job, job + 1)
            with act.Fori(0, NG) as g:
                job = 0
                for kind, i, j in plan:
                    if kind in "wkqv":
                        take_job(kind, i % NT, job, g * JOBS + 6 + job + 1)
                        job += 1
                    elif kind == "s":
                        q0, step = width(i, j), step_of(i, j)
                        w_free(act, g, i, j)
                        act.wait_ge(s_ready, 2 * (g * STEPS + step) + 1)
                        nc.scalar.activation(w[:, step % 4, 0:2, q0:], s_ps[:, 0:2, q0:], ACT.Relu,
                                             bias=SHIFT).then_inc(relu_a, 1)
                    elif kind == "t":
                        q0, step = width(i, j), step_of(i, j)
                        if step % 4:
                            act.wait_ge(s_ready, 2 * (g * STEPS + step) + 2)
                            nc.scalar.activation(w[:, step % 4, 2:4, q0:], s_ps[:, 2:4, q0:], ACT.Relu,
                                                 bias=SHIFT).then_inc(relu_b_act, 1)
                    elif kind == "n":
                        act.wait_ge(pv_done, g * STEPS + step_of(i + 1, 0) + 4)
                        act.wait_ge(o_out[i % 2], 16 * (g * (NT // 2) + i // 2) + 16)
                        nc.scalar.copy(o[:, i % 2, :], num[:, :]).then_inc(num_out, 1)

        @block.vector
        def _(dve):
            def take_job(kind, job):
                part = kpart if kind == "k" else qpart
                nc.vector.scalar_tensor_tensor(part[:, 1, :], job_ps[:, job % 2, :], 1.0 if kind == "k" else scale,
                                               part[:, 0, :].bitcast(F32), ALU.mult, ALU.subtract
                                               ).then_inc(rest_done, 1)

            nc.vector.memset(rden[:, :], 0.0).then_inc(pv_done, 4)
            nc.vector.memset(acc[:, 0, 0, :], 0.0).then_inc(chunk_done, 2)
            nc.vector.memset(o[:, 0, :], 0.0).then_inc(o_out[0], 16)
            nc.vector.memset(o[:, 1, :], 0.0).then_inc(o_out[1], 16)
            for job, (kind, i, _) in enumerate(first_jobs):
                if kind in "kq":
                    dve.wait_ge(job_hi, job + 1)
                    take_job(kind, job)
            with dve.Fori(0, NG) as g:
                job = adds = chunk = 0
                for kind, i, j in plan:
                    if kind in "wkqv":
                        if kind in "kq":
                            dve.wait_ge(job_hi, g * JOBS + 6 + job + 1)
                            take_job(kind, job)
                        job += 1
                    elif kind == "t" and step_of(i, j) % 4 == 0:
                        q0, step = width(i, j), step_of(i, j)
                        w_free(dve, g, i, j)
                        dve.wait_ge(s_ready, 2 * (g * STEPS + step) + 2)
                        nc.vector.tensor_scalar(w[:, step % 4, 2:4, q0:], s_ps[:, 2:4, q0:], SHIFT, 0.0,
                                                ALU.add, ALU.max).then_inc(relu_b_dve, 1)
                    elif kind == "a" and j % TB:
                        step = step_of(i, j)
                        relu_done(dve, g, step, 0)
                        relu_done(dve, g, step, 1)
                        total = acc[:, chunk % 2, :, :]
                        if j % TB == 1:
                            dve.wait_ge(chunk_done, g * CHUNKS + chunk + 1)
                            prev = w[:, (step - 1) % 4, :, :]
                        else:
                            dve.wait_ge(added, g * ADDS + adds)
                            prev = total
                        nc.vector.tensor_tensor(total, prev, w[:, step % 4, :, :], ALU.add).then_inc(added, 1)
                        adds += 1
                        chunk += j % TB == TB - 1
                    elif kind == "n":
                        if i >= 1:
                            dve.wait_ge(o_ready, 4 * (g * NT + i))
                        dve.wait_ge(pv_done, g * STEPS + step_of(i + 1, 0) + 4)
                        nc.vector.tensor_scalar(rden[:, :], den[:, :], ATT_EPS, None, ALU.add).then_inc(den_out, 1)
                    elif kind == "r":
                        cut = slice(j * P, (j + 1) * P)
                        dve.wait_ge(den_out, g * NT + i + 1)
                        nc.vector.reciprocal(rden[:, cut], rden[:, cut]).then_inc(rden_ready, 1)
                        dve.wait_ge(rden_ready, 4 * (g * NT + i) + j + 1)
                        dve.wait_ge(num_out, g * NT + i + 1)
                        nc.vector.tensor_tensor(o[:, i % 2, cut], o[:, i % 2, cut], rden[:, cut],
                                                ALU.mult).then_inc(o_ready, 1)

        @block.gpsimd
        def _(pool):
            with pool.Fori(0, NG) as g:
                for kind, i, j in plan:
                    if kind == "t" and j >= TB * i:
                        q0, step = width(i, j), step_of(i, j)
                        relu_done(pool, g, step, 0)
                        relu_done(pool, g, step, 1)
                        pool.sem_inc(pool_passed, 1)
                        tri = w[:, step % 4, :, q0:q0 + P]
                        pool.affine_select(out=tri, in_=tri, compare_op=ALU.is_ge, fill=0.0, base=0,
                                           pattern=[[0, HG], [1, P]], channel_multiplier=-1).then_inc(masked, 1)

        @block.tensor
        def _(pe):
            def do_job(kind, i, job):
                bank, rows = job_ps[:, job % 2, :], hT[:, i % 2, :, :]
                if kind == "w":
                    for k in range(KT):
                        last = nc.tensor.transpose(bank[:, k * P:(k + 1) * P], wraw[:, i, k * P:(k + 1) * P],
                                                   ident[:, :])
                elif kind in "kq":
                    for k in range(KT):
                        last = nc.tensor.matmul(bank, wT[:, "qk".index(kind), k, :], rows[:, k, :],
                                                start=(k == 0), stop=(k == KT - 1))
                else:
                    for t in range(TB):
                        for k in range(KT):
                            last = nc.tensor.matmul(bank[:, t * P:(t + 1) * P], rows[:, k, t * P:(t + 1) * P],
                                                    wT[:, 2, k, :], start=(k == 0), stop=(k == KT - 1))
                last.then_inc(job_ready, 1)

            for job, (kind, i, _) in enumerate(first_jobs):
                if job == 0:
                    pe.wait_ge(w_in, 48)
                elif job in (2, 3):
                    pe.wait_ge(job_hi, job - 1 if job == 2 else 3)
                elif job == 4:
                    pe.wait_ge(job_hi, 3)
                elif job == 5:
                    pe.wait_ge(rest_done, 1)
                if kind == "k":
                    pe.wait_ge(hT_in[0], 16)
                do_job(kind, i, job)
            with pe.Fori(0, NG) as g:
                job = chunk = diag = 0
                for kind, i, j in plan:
                    if kind in "wkqv":
                        if job == 0:
                            pe.wait_ge(job_hi, g * JOBS + 6)
                        elif job == 1:
                            pe.wait_ge(rest_done, g * RESTS + 2)
                        elif kinds[job - 2] in "kq":
                            pe.wait_ge(rest_done, g * RESTS + 2 + rests(job - 1))
                        else:
                            pe.wait_ge(job_hi, g * JOBS + 6 + job - 1)
                        if kind == "w" and i == 0:
                            pe.wait_ge(w_in, 48 * g + 96)
                        if kind == "k":
                            pe.wait_ge(hT_in[i % 2], 16 * (g * (NT // 2) + i // 2 + 1))
                            if i == NT:
                                pe.wait_ge(job_hi, g * JOBS + 6 + job)
                        do_job(kind, i % NT if kind != "w" else i, job)
                        job += 1
                    elif kind in "st":
                        q0, step, half = width(i, j), step_of(i, j), "st".index(kind)
                        if j == 0 and half == 0:
                            pe.wait_ge(k_in, MOVES * (g * NT + i + 1))
                            pe.wait_ge(q_in, MOVES * (g * NT + i + 1))
                        if step >= 1:
                            relu_done(pe, g, step - 1, half)
                        for h in (2 * half, 2 * half + 1):
                            last = nc.tensor.matmul(s_ps[:, h, q0:], kst[:, h, j * P:(j + 1) * P],
                                                    qst[:, i % 2, h, q0:], start=True, stop=True)
                        last.then_inc(s_ready, 1)
                    elif kind == "p":
                        q0, step = width(i, j), step_of(i, j)
                        if j == 0:
                            pe.wait_ge(job_hi, g * JOBS + 6 + 3 * i)
                            if i >= 1:
                                pe.wait_ge(num_out, g * NT + i)
                                pe.wait_ge(den_out, g * NT + i)
                        relu_done(pe, g, step, 0)
                        relu_done(pe, g, step, 1)
                        cut = j >= TB * i
                        if cut:
                            diag += 1
                            pe.wait_ge(masked, g * TB * NT + diag)
                        last_j = j == TB * (i + 1) - 1
                        for h in range(HG):
                            last = nc.tensor.matmul(num[h * HD:(h + 1) * HD, q0:], vals[:, j, h * HD:(h + 1) * HD],
                                                    w[:, step % 4, h, q0:], start=(j == 0), stop=last_j)
                        if cut:
                            for h in range(HG):
                                last = nc.tensor.matmul(den[h * HD:(h + 1) * HD, q0:], ones[:, 0:HD],
                                                        w[:, step % 4, h, q0:], start=(j == 0 or (i, j) == (1, TB)),
                                                        stop=last_j)
                        last.then_inc(pv_done, 1)
                    elif kind == "d":
                        pe.wait_ge(added, g * ADDS + 3 * (chunk + 1))
                        for h in range(HG):
                            last = nc.tensor.matmul(den[h * HD:(h + 1) * HD, :], ones[:, 0:HD],
                                                    acc[:, chunk % 2, h, :], start=(j == 0 and i > 1), stop=False)
                        last.then_inc(chunk_done, 1)
                        chunk += 1


def turn_weights(nc, wo, w_router, woT, wrT, w_shd, w_sh_down, keep):
    with ExitStack() as ctx:
        rows = ctx.enter_context(nc.sbuf_tensor("tw_rows", [P, KT, C], F32))
        rrows = ctx.enter_context(nc.sbuf_tensor("tw_router", [NE, C], F32))
        ps = ctx.enter_context(nc.psum_tensor("tw_ps", [P, KT, C], F32))
        rps = ctx.enter_context(nc.psum_tensor("tw_rps", [P, KT, P], F32))
        w_in = ctx.enter_context(nc.semaphore("tw_in"))
        d_in = ctx.enter_context(nc.semaphore("tw_down_in"))
        turned = ctx.enter_context(nc.semaphore("tw_turned"))
        block = ctx.enter_context(nc.Block())
        ident, gates = keep["ident"], keep["gates"]

        @block.sync
        def _(sp):
            sp.dma_start(rows[:, :, :], wo.rearrange("(o p) c -> p o c", p=P)).then_inc(w_in, 16)
            sp.dma_start(rrows[:, :], w_router).then_inc(w_in, 16)
            sp.dma_start(w_shd[:, :, :], w_sh_down.rearrange("(f p) c -> p f c", p=P)).then_inc(d_in, 16)

        @block.tensor
        def _(pe):
            pe.wait_ge(w_in, 32)
            for k in range(KT):
                for o in range(KT):
                    last = nc.tensor.transpose(ps[:, k, o * P:(o + 1) * P], rows[:, o, k * P:(k + 1) * P],
                                               ident[:, :])
                last.then_inc(turned, 1)
            for k in range(KT):
                last = nc.tensor.transpose(rps[:, k, 0:NE], rrows[:, k * P:(k + 1) * P], ident[0:NE, 0:NE])
            last.then_inc(turned, 1)

        @block.vector
        def _(dve):
            dve.wait_ge(d_in, 16)
            for f in range(FT):
                nc.vector.tensor_tensor(w_shd[:, f, :], w_shd[:, f, :], gates[:, 1, :], ALU.mult)
            for k in range(KT):
                dve.wait_ge(turned, k + 1)
                nc.vector.tensor_tensor(woT[:, k, :], ps[:, k, :], gates[:, 0, :], ALU.mult)

        @block.scalar
        def _(act):
            act.wait_ge(turned, KT + 1)
            nc.scalar.copy(wrT[:, :, :], rps[:, :, 0:NE])


def dense_part(nc, x, oT_dram, rows_dram, acc_dram, w_sh_gate, w_sh_up, woT, wrT, shg, shu, h2T, keyT, keep):
    T = x.shape[0]
    NT = T // TT
    NL = NT // 2
    NORM = 7
    CHOICE = 6 + TOPK
    MERGE = 2 * (CAP // 8) - 1
    PER_BODY = 2 * NORM + 2 * CHOICE + MERGE
    with ExitStack() as ctx:
        def sb(name, shape, dt=F32):
            return ctx.enter_context(nc.sbuf_tensor("d_" + name, shape, dt))

        def sem(name):
            return ctx.enter_context(nc.semaphore("d_" + name))

        oTb = [sb(f"oT{b}", [P, KT, TT]) for b in range(2)]
        xb = [sb(f"x{b}", [P, TB, C]) for b in range(2)]
        xn = [sb(f"xn{b}", [P, TB, C]) for b in range(2)]
        stats, mv, rs = sb("stats", [P, TB, 6]), sb("mv", [P, TB, 2]), sb("rs", [P, 3, TB])
        lT = sb("logitsT", [NE, TT])
        lg = sb("logits", [P, TB, NE])
        top = sb("top", [P, TB, 8])
        topi = sb("topi", [P, TB, 8], U32)
        topf = sb("topf", [P, TB, 8])
        chosen = sb("chosen", [P, TB, NE])
        soft = sb("soft", [P, TB, NE])
        total = sb("total", [P, TB])
        wt = [sb(f"wt{b}", [P, TB, NE]) for b in range(2)]
        keys = sb("keys", [P, TB, 2, NE])
        largest = sb("largest", [P, CAP])
        left = sb("left", [P, TB])
        lefti = sb("lefti", [P, TB], mybir.dt.int32)
        experts = sb("experts", [P, NE])
        expertsi = sb("expertsi", [P, NE], mybir.dt.int32)
        zero = sb("zero", [P, C])
        y_ps = ctx.enter_context(nc.psum_tensor("d_y_ps", [P, TB, C], F32))
        misc = ctx.enter_context(nc.psum_tensor("d_misc_ps", [P, KT, TT], F32))
        sh_in = sem("sh_in")
        oT_in = [sem(f"oT_in{b}") for b in range(2)]
        x_in = [sem(f"x_in{b}") for b in range(2)]
        xn_out = [sem(f"xn_out{b}") for b in range(2)]
        wt_out = [sem(f"wt_out{b}") for b in range(2)]
        acc_out = [sem(f"acc_out{b}") for b in range(2)]
        zero_out = sem("zero_out")
        consts = sem("consts")
        const_step = sem("const_step")
        y_ready, x1_ready = sem("y_ready"), sem("x1_ready")
        var_ready, sd_ready, xn_ready = sem("var_ready"), sem("sd_ready"), sem("xn_ready")
        xT_ready, xT_copied = sem("xT_ready"), sem("xT_copied")
        lT_ready, lT_copied = sem("lT_ready"), sem("lT_copied")
        lg_ready, lg_copied = sem("lg_ready"), sem("lg_copied")
        kT_ready, kT_copied, merged = sem("kT_ready"), sem("kT_copied"), sem("merged")
        soft_in, soft_out, wt_ready, keys_ready = sem("soft_in"), sem("soft_out"), sem("wt_ready"), sem("keys_ready")
        dve_step, dve_passed, pe_passed = sem("dve_step"), sem("dve_passed"), sem("pe_passed")
        block = ctx.enter_context(nc.Block())
        ident, cols = keep["ident"], keep["cols"]

        @block.sync
        def _(sp):
            def put_x1(b, m):
                sp.wait_ge(x1_ready, TB * m + TB)
                sp.dma_start(acc_dram[bass.ds(m * TT, TT), :].rearrange("(t p) c -> p t c", p=P),
                             xb[b][:, :, :]).then_inc(acc_out[b], 16)

            def put_norm(b, m):
                sp.wait_ge(xn_ready, m + 1)
                sp.dma_start(rows_dram[bass.ds(m * TT, TT), 0:C].rearrange("(t p) c -> p t c", p=P),
                             xn[b][:, :, :]).then_inc(xn_out[b], 16)

            def step(it, b, last=False):
                n = 2 * it + b
                if not last:
                    put_x1(1 - b, n + 1)
                    put_norm(1 - b, n + 1)
                sp.wait_ge(wt_ready, n + 1)
                sp.dma_start(rows_dram[bass.ds(n * TT, TT), C:C + NE].rearrange("(t p) c -> p t c", p=P),
                             wt[b][:, :, :]).then_inc(wt_out[b], 16)

            sp.dma_start(shg[:, :, :], w_sh_gate.rearrange("(k p) i -> p k i", p=P)).then_inc(sh_in, 16)
            sp.dma_start(shu[:, :, :], w_sh_up.rearrange("(k p) i -> p k i", p=P)).then_inc(sh_in, 16)
            put_x1(0, 0)
            put_norm(0, 0)
            with sp.Fori(0, NL - 1) as it:
                step(it, 0)
                step(it, 1)
            step(NL - 1, 0)
            step(NL - 1, 1, last=True)
            sp.wait_ge(sh_in, 32)
            for b in range(2):
                sp.wait_ge(xn_out[b], 16 * NL + 16)
                sp.wait_ge(wt_out[b], 16 * NL + 16)
                sp.wait_ge(acc_out[b], 16 * NL)

        @block.gpsimd
        def _(pool):
            def get(b, n):
                pool.dma_start(oTb[b][:, :, :], oT_dram[:, bass.ds(n * TT, TT)].rearrange(
                    "(k p) t -> p k t", p=P)).then_inc(oT_in[b], 16)

            def get_x(b, n):
                pool.dma_start(xb[b][:, :, :], x[bass.ds(n * TT, TT), :].rearrange(
                    "(t p) c -> p t c", p=P)).then_inc(x_in[b], 16)

            for b in range(2):
                get(b, b)
                get_x(b, b)
            done = chained(pool, const_step)
            done(pool.iota(lefti[:, :], [[-P, TB]], base=T, channel_multiplier=-1))
            done(pool.iota(expertsi[:, :], [[1, NE]], base=0, channel_multiplier=0))
            pool.tensor_copy(left[:, :], lefti[:, :]).then_inc(consts, 1)
            pool.tensor_copy(experts[:, :], expertsi[:, :]).then_inc(consts, 1)
            done(pool.memset(zero[:, :], 0.0))
            pool.dma_start(acc_dram[T:T + P, :], zero[:, :]).then_inc(zero_out, 16)
            with pool.Fori(0, NL - 1) as it:
                for b in range(2):
                    n = 2 * it + b
                    pool.wait_ge(y_ready, TB * n + TB)
                    get(b, n + 2)
                    pool.wait_ge(xn_ready, n + 1)
                    pool.wait_ge(acc_out[b], 16 * it + 16)
                    get_x(b, n + 2)
            pool.wait_ge(zero_out, 16)

        @block.scalar
        def _(act):
            def root(m):
                act.wait_ge(var_ready, m + 1)
                nc.scalar.activation(rs[:, 1, :], rs[:, 0, :], ACT.Sqrt).then_inc(sd_ready, 1)

            def keys_out(it):
                act.wait_ge(kT_ready, it + 1)
                act.wait_ge(merged, it + 1)
                nc.scalar.copy(keyT[:, CAP:], misc[:, 2, :]).then_inc(kT_copied, 1)

            def step(it, b, last=False):
                n = 2 * it + b
                for k in range(KT):
                    act.wait_ge(xT_ready, KT * n + k + 1 + KT)
                    nc.scalar.activation(h2T[:, bass.ds(n * TB, TB), k * P:(k + 1) * P],
                                         misc[:, k, :].rearrange("p (t q) -> p t q", t=TB), ACT.Identity,
                                         scale=cols[:, CB, k:k + 1], bias=cols[:, SB, k:k + 1]
                                         ).then_inc(xT_copied, 1)
                act.wait_ge(lT_ready, n + 1)
                nc.scalar.copy(lT[:, :], misc[0:NE, 0, :]).then_inc(lT_copied, 1)
                if b == 0:
                    keys_out(it)
                act.wait_ge(lg_ready, n + 1)
                nc.scalar.copy(lg[:, :, :], misc[:, 1, 0:TB * NE].rearrange("p (t e) -> p t e", t=TB)
                               ).then_inc(lg_copied, 1)
                if not last:
                    root(n + 1)
                act.wait_ge(soft_in, n + 1)
                nc.scalar.activation(soft[:, :, :], soft[:, :, :], ACT.Exp).then_inc(soft_out, 1)

            root(0)
            with act.Fori(0, NL - 1) as it:
                step(it, 0)
                step(it, 1)
            step(NL - 1, 0)
            step(NL - 1, 1, last=True)
            keys_out(NL)

        @block.vector
        def _(dve):
            nc.vector.memset(keyT[:, 0:CAP], 0.0).then_inc(merged, 1)
            nc.vector.memset(keys[:, :, :, :], 0.0).then_inc(keys_ready, 2)
            nc.vector.memset(lg[:, 0, :], 0.0).then_inc(xT_ready, KT)
            nc.vector.memset(lg[:, 1, :], 0.0).then_inc(lg_copied, 1)
            for b in range(2):
                nc.vector.memset(wt[b][:, 1, :], 0.0).then_inc(xn_out[b], 16)
                nc.vector.memset(wt[b][:, 2, :], 0.0).then_inc(wt_out[b], 16)
            dve.wait_ge(consts, 2)

            def x1_and_norm(it, b, m, done, started=True):
                dve.wait_ge(x_in[b], 16 * it + 16)
                for t in range(TB):
                    dve.wait_ge(y_ready, TB * m + t + 1)
                    nc.vector.tensor_tensor(xb[b][:, t, :], y_ps[:, t, :], xb[b][:, t, :],
                                            ALU.add).then_inc(x1_ready, 1)
                dve.wait_ge(x1_ready, TB * m + TB)
                dve.wait_ge(xn_out[b], 16 * it + 16)
                dve.wait_ge(xT_ready, KT * m if started else KT)
                normalize_rows(nc, dve, done, xb[b], xn[b], stats, mv, rs, var_ready, sd_ready,
                               m + 1, passed=dve_passed).then_inc(xn_ready, 1)

            def choice(it, b, done):
                n = 2 * it + b
                wait_apart(dve, dve_passed, lg_copied, n + 2)
                for t in range(TB):
                    last = nc.vector.max(top[:, t, :], lg[:, t, :])
                done(last, dve_passed)
                for t in range(TB):
                    nc.vector.max_index(topi[:, t, :], top[:, t, :], lg[:, t, :])
                    last = nc.vector.tensor_scalar(soft[:, t, :], lg[:, t, :], top[:, t, 0:1], None, ALU.subtract)
                last.then_inc(soft_in, 1)
                dve.wait_ge(soft_in, n + 1)
                done(nc.vector.tensor_copy(topf[:, :, :], topi[:, :, :]))
                for t in range(TB):
                    last = nc.vector.tensor_scalar(chosen[:, t, :], experts[:, :], topf[:, t, 0:1], None,
                                                   ALU.is_equal)
                done(last)
                for r in range(1, TOPK):
                    for t in range(TB):
                        last = nc.vector.scalar_tensor_tensor(chosen[:, t, :], experts[:, :], topf[:, t, r:r + 1],
                                                              chosen[:, t, :], ALU.is_equal, ALU.add)
                    done(last)
                if b == 0:
                    dve.wait_ge(kT_ready, it + 1)
                for t in range(TB):
                    last = nc.vector.tensor_scalar(keys[:, t, b, :], chosen[:, t, :], left[:, t:t + 1], None,
                                                   ALU.mult)
                last.then_inc(keys_ready, 1)
                dve.wait_ge(keys_ready, n + 3)
                done(nc.vector.tensor_scalar(left[:, :], left[:, :], float(TT), None, ALU.subtract))
                dve.wait_ge(soft_out, n + 1)
                done(nc.vector.tensor_tensor(soft[:, :, :], soft[:, :, :], chosen[:, :, :], ALU.mult))
                done(nc.vector.reduce_sum(total[:, :], soft[:, :, :], axis=mybir.AxisListType.X))
                done(nc.vector.reciprocal(total[:, :], total[:, :]))
                dve.wait_ge(wt_out[b], 16 * it + 16)
                for t in range(TB):
                    last = nc.vector.tensor_scalar(wt[b][:, t, :], soft[:, t, :], total[:, t:t + 1], None, ALU.mult)
                last.then_inc(wt_ready, 1)

            def step(it, b, done, last=False):
                if not last:
                    x1_and_norm(it + b, 1 - b, 2 * it + b + 1, done)
                choice(it, b, done)
                if b == 0:
                    wait_apart(dve, dve_passed, kT_copied, it + 1)
                    for r in range(0, CAP, 8):
                        done(nc.vector.max(largest[:, r:r + 8], keyT[:, :]), dve_passed)
                        if r + 8 < CAP:
                            done(nc.vector.match_replace(keyT[:, :], largest[:, r:r + 8], keyT[:, :], 0.0), dve_passed)
                    nc.vector.tensor_copy(keyT[:, 0:CAP], largest[:, :]).then_inc(merged, 1)

            x1_and_norm(0, 0, 0, chained(dve, dve_step), started=False)
            with dve.Fori(0, NL - 1) as it:
                done = chained(dve, dve_step, PER_BODY * it + NORM)
                step(it, 0, done)
                step(it, 1, done)
            done = chained(dve, dve_step, PER_BODY * (NL - 1) + NORM)
            step(NL - 1, 0, done)
            step(NL - 1, 1, done, last=True)

        @block.tensor
        def _(pe):
            def products(it, b, m, tiles, started=True):
                pe.wait_ge(oT_in[b], 16 * it + 16)
                for t in tiles:
                    if started:
                        pe.wait_ge(x1_ready, TB * (m - 1) + t + 1)
                    for k in range(KT):
                        last = nc.tensor.matmul(y_ps[:, t, :], oTb[b][:, k, t * P:(t + 1) * P], woT[:, k, :],
                                                start=(k == 0), stop=(k == KT - 1))
                    last.then_inc(y_ready, 1)

            def turn_keys():
                for t in range(TB):
                    last = nc.tensor.transpose(misc[:, 2, t * P:(t + 1) * P], keys[:, t, :, :].rearrange(
                        "p b e -> p (b e)"), ident[:, :])
                last.then_inc(kT_ready, 1)

            def step(it, b, next_one=True, next_but_one=True):
                n = 2 * it + b
                pe.wait_ge(xn_ready, n + 1)
                for k in range(KT):
                    if k == 1:
                        pe.wait_ge(lg_copied, n + 1)
                    if k == 2 and b == 1:
                        pe.wait_ge(kT_copied, it + 1)
                    for t in range(TB):
                        last = nc.tensor.transpose(misc[:, k, t * P:(t + 1) * P], xn[b][:, t, k * P:(k + 1) * P],
                                                   ident[:, :])
                    last.then_inc(xT_ready, 1)
                pe.wait_ge(xT_copied, KT * n + KT)
                for k in range(KT):
                    last = nc.tensor.matmul(misc[0:NE, 0, :], wrT[:, k, :], h2T[:, bass.ds(n * TB, TB),
                                                                               k * P:(k + 1) * P],
                                            start=(k == 0), stop=(k == KT - 1))
                last.then_inc(lT_ready, 1)
                if b == 0:
                    pe.wait_ge(keys_ready, n + 2)
                    turn_keys()
                if next_one:
                    products(it + b, 1 - b, n + 1, [TB - 1])
                wait_apart(pe, pe_passed, lT_copied, n + 1)
                for t in range(TB):
                    last = nc.tensor.transpose(misc[:, 1, t * NE:(t + 1) * NE], lT[:, t * P:(t + 1) * P],
                                               ident[0:NE, 0:NE])
                last.then_inc(lg_ready, 1)
                if next_but_one:
                    products(it + 1, b, n + 2, range(TB - 1))

            products(0, 0, 0, range(TB), started=False)
            products(0, 1, 1, range(TB - 1))
            with pe.Fori(0, NL - 1) as it:
                step(it, 0)
                step(it, 1)
            step(NL - 1, 0, next_but_one=False)
            step(NL - 1, 1, next_one=False, next_but_one=False)
            pe.wait_ge(keys_ready, NT + 2)
            pe.wait_ge(xT_copied, KT * NT)
            turn_keys()


def slot_lists(nc, keyT, keys_dram, gather_at, add_at, T, keep):
    LARGEST = 2 * (CAP // 8) - 1
    with ExitStack() as ctx:
        half = ctx.enter_context(nc.sbuf_tensor("l_half", [P, CAP], F32))
        both = ctx.enter_context(nc.sbuf_tensor("l_both", [NE, 2, CAP], F32))
        first = ctx.enter_context(nc.sbuf_tensor("l_first", [NE, CAP], F32))
        pairs = ctx.enter_context(nc.sbuf_tensor("l_pairs", [NE // 2, 2 * CAP], F32))
        key = ctx.enter_context(nc.sbuf_tensor("l_key", [P, NE // 2], F32))
        tok = ctx.enter_context(nc.sbuf_tensor("l_tok", [P, NE // 2], F32))
        own = ctx.enter_context(nc.sbuf_tensor("l_own", [P, 2], F32))
        spare = ctx.enter_context(nc.sbuf_tensor("l_spare", [P, NE // 2], F32))
        sparei = ctx.enter_context(nc.sbuf_tensor("l_sparei", [P, NE // 2], mybir.dt.int32))
        ps = ctx.enter_context(nc.psum_tensor("l_ps", [P, C], F32))
        step = ctx.enter_context(nc.semaphore("l_step"))
        both_in = ctx.enter_context(nc.semaphore("l_both_in"))
        first_out = ctx.enter_context(nc.semaphore("l_first_out"))
        pairs_in = ctx.enter_context(nc.semaphore("l_pairs_in"))
        turned = ctx.enter_context(nc.semaphore("l_turned"))
        consts = ctx.enter_context(nc.semaphore("l_consts"))
        block = ctx.enter_context(nc.Block())

        @block.gpsimd
        def _(pool):
            done = chained(pool, consts)
            done(pool.memset(own[:, :], 1.0))
            done(pool.affine_select(out=own[:, 0:1], in_=own[:, 0:1], compare_op=ALU.is_ge, fill=0.0,
                                    base=CAP - 1, pattern=[[0, 1]], channel_multiplier=-1))
            done(pool.affine_select(out=own[:, 1:2], in_=own[:, 1:2], compare_op=ALU.is_ge, fill=0.0,
                                    base=-CAP, pattern=[[0, 1]], channel_multiplier=1))
            done(pool.iota(sparei[:, :], [[0, NE // 2]], base=T, channel_multiplier=1))
            done(pool.tensor_copy(spare[:, :], sparei[:, :]))

        @block.sync
        def _(sp):
            sp.wait_ge(step, LARGEST)
            for b in range(2):
                sp.dma_start(both[:, b, :], half[b * NE:(b + 1) * NE, :]).then_inc(both_in, 16)
            sp.wait_ge(step, 2 * LARGEST)
            sp.dma_start(keys_dram, first[:, :]).then_inc(first_out, 16)
            sp.wait_ge(first_out, 16)
            sp.dma_start(pairs[:, :], keys_dram.rearrange("(m b) s -> m (b s)", b=2)).then_inc(pairs_in, 16)

        @block.tensor
        def _(pe):
            pe.wait_ge(pairs_in, 16)
            nc.tensor.transpose(ps[:, 0:NE // 2], pairs[:, :], keep["ident"][0:NE // 2, 0:NE // 2]).then_inc(turned, 1)

        @block.vector
        def _(dve):
            done = chained(dve, step)

            def largest(out, src):
                for r in range(0, CAP, 8):
                    done(nc.vector.max(out[:, r:r + 8], src))
                    if r + 8 < CAP:
                        done(nc.vector.match_replace(src, out[:, r:r + 8], src, 0.0))

            largest(half[:, :], keyT[:, :])
            dve.wait_ge(both_in, 32)
            largest(first[:, :], both[:, :, :].rearrange("p b s -> p (b s)"))
            dve.wait_ge(turned, 1)
            dve.wait_ge(consts, 5)
            done(nc.vector.memset(gather_at[:, NE // 2:], 0))
            done(nc.vector.tensor_copy(key[:, :], ps[:, 0:NE // 2]))
            done(nc.vector.tensor_scalar(tok[:, :], key[:, :], -1.0, float(T), ALU.mult, ALU.add))
            done(nc.vector.tensor_scalar(gather_at[:, 0:NE // 2], tok[:, :], float(T - 1), None, ALU.min))
            for b in range(2):
                done(nc.vector.tensor_tensor(tok[:, :], tok[:, :], spare[:, :], ALU.subtract))
                done(nc.vector.scalar_tensor_tensor(tok[:, :], key[:, :], 0.0, tok[:, :], ALU.is_gt, ALU.mult))
                done(nc.vector.scalar_tensor_tensor(tok[:, :], tok[:, :], own[:, b:b + 1], spare[:, :],
                                                    ALU.mult, ALU.add))
                done(nc.vector.tensor_copy(add_at[:, b, 0:NE // 2], tok[:, :]))
                done(nc.vector.tensor_scalar(tok[:, :], key[:, :], -1.0, float(T), ALU.mult, ALU.add))


def experts_part(nc, rows_dram, acc_dram, w_gate, w_up, w_down, gather_at, add_at, shg, shu, w_shd, h2T, T, keep):
    NS = NE // 2
    NL = NS // 2
    RW = C + NE
    assert NS == T // P
    with ExitStack() as ctx:
        def sb(name, shape, dt=F32):
            return ctx.enter_context(nc.sbuf_tensor("e_" + name, shape, dt))

        def sem(name):
            return ctx.enter_context(nc.semaphore("e_" + name))

        wg = [sb(f"wg{b}", [P, 2, KT, FI]) for b in range(2)]
        wu = [sb(f"wu{b}", [P, 2, KT, FI]) for b in range(2)]
        wd = [sb(f"wd{b}", [P, 2, FT, C]) for b in range(2)]
        xg = [sb(f"xg{b}", [P, RW]) for b in range(2)]
        xeT = sb("xeT", [P, KT, P])
        hid, s_hid = sb("hid", [P, FI]), sb("s_hid", [P, FI])
        hidT = sb("hidT", [P, FT, P])
        wcol = [sb(f"wcol{b}", [P, 1]) for b in range(2)]
        from_rows = [sb(f"from_rows{b}", [P, 1], U32) for b in range(2)]
        to_rows = [sb(f"to_rows{b}", [P, 2], U32) for b in range(2)]
        y = [sb(f"y{b}", [P, C]) for b in range(2)]
        x_ps = ctx.enter_context(nc.psum_tensor("e_x_ps", [P, KT, P], F32))
        gu_ps = ctx.enter_context(nc.psum_tensor("e_gu_ps", [P, 2, C], F32))
        hT_ps = ctx.enter_context(nc.psum_tensor("e_hT_ps", [P, C], F32))
        y_ps = ctx.enter_context(nc.psum_tensor("e_y_ps", [P, C], F32))
        s_gu_ps = ctx.enter_context(nc.psum_tensor("e_s_gu_ps", [P, 2, C], F32))
        s_y_ps = ctx.enter_context(nc.psum_tensor("e_s_y_ps", [P, C], F32))
        gu_in = [sem(f"gu_in{b}") for b in range(2)]
        d_in = [sem(f"d_in{b}") for b in range(2)]
        x_in = [sem(f"x_in{b}") for b in range(2)]
        added, pair_added = sem("added"), sem("pair_added")
        rows_ready = sem("rows_ready")
        x_ready, xe_ready = sem("x_ready"), sem("xe_ready")
        gu_ready, tanh_ready, hid_ready = sem("gu_ready"), sem("tanh_ready"), sem("hid_ready")
        s_gu_ready, s_tanh_ready, s_hid_ready = sem("s_gu_ready"), sem("s_tanh_ready"), sem("s_hid_ready")
        hT_ready, hT_copied, y_ready, y_done = sem("hT_ready"), sem("hT_copied"), sem("y_ready"), sem("y_done")
        s_y_ready, s_y_copied = sem("s_y_ready"), sem("s_y_copied")
        step, pool_passed = sem("step"), sem("pool_passed")
        block = ctx.enter_context(nc.Block())
        ident, cols, gates = keep["ident"], keep["cols"], keep["gates"]
        slots = [slice(0, CAP), slice(CAP, 2 * CAP)]

        @block.sync
        def _(sp):
            with sp.Fori(0, NL) as it:
                for b in range(2):
                    n = 2 * it + b
                    sp.wait_ge(gu_ready, n + 1)
                    sp.dma_start(wg[b][:, :, :, :], w_gate[bass.ds(n * 2, 2), :, :].rearrange(
                        "e (k p) i -> p e k i", p=P)).then_inc(gu_in[b], 16)
                    sp.dma_start(wu[b][:, :, :, :], w_up[bass.ds(n * 2, 2), :, :].rearrange(
                        "e (k p) i -> p e k i", p=P)).then_inc(gu_in[b], 16)
                    sp.wait_ge(y_ready, n + 1)
                    sp.dma_start(wd[b][:, :, :, :], w_down[bass.ds(n * 2, 2), :, :].rearrange(
                        "e (f p) c -> p e f c", p=P)).then_inc(d_in[b], 16)

        @block.gpsimd
        def _(pool):
            def gather(b, n):
                wait_apart(pool, pool_passed, rows_ready, n + 1)
                pool.indirect_dma_start(xg[b][:, :], None, rows_dram, bass.IndirectOffsetOnAxis(
                    ap=from_rows[b][:, 0:1], axis=0), bounds_check=T - 1, oob_is_err=True).then_inc(x_in[b], 16)

            gather(0, 0)
            gather(1, 1)
            with pool.Fori(0, NL) as it:
                for b in range(2):
                    n = 2 * it + b
                    gather(b, n + 2)
                    wait_apart(pool, pool_passed, y_done, n + 2)
                    for one in range(2):
                        pool.indirect_dma_start(acc_dram, bass.IndirectOffsetOnAxis(
                            ap=to_rows[b][:, one:1 + one], axis=0), y[b][:, :], None, bounds_check=T + P - 1,
                            oob_is_err=True, compute_op=ALU.add).then_inc(added, 16)
                        wait_apart(pool, pool_passed, added, 16 * (2 * n + one + 1))
                    pool.sem_inc(pair_added, 1)
            for b in range(2):
                pool.wait_ge(x_in[b], 16 * (NL + 1))

        @block.scalar
        def _(act):
            def turned_in(m):
                act.wait_ge(x_ready, m + 1)
                for k in range(KT):
                    last = nc.scalar.activation(xeT[:, k, :], x_ps[:, k, :], ACT.Identity,
                                                scale=cols[:, CB, k:k + 1], bias=cols[:, SB, k:k + 1])
                last.then_inc(xe_ready, 1)

            turned_in(0)
            with act.Fori(0, NL) as it:
                for b in range(2):
                    n = 2 * it + b
                    act.wait_ge(s_gu_ready, n + 1)
                    nc.scalar.activation(s_hid[:, :], s_gu_ps[:, 0, 0:FI], ACT.Tanh,
                                         scale=0.5).then_inc(s_tanh_ready, 1)
                    act.wait_ge(gu_ready, n + 3)
                    nc.scalar.activation(hid[:, :], gu_ps[:, 0, 0:FI], ACT.Tanh, scale=0.5).then_inc(tanh_ready, 1)
                    turned_in(n + 1)
                    act.wait_ge(hT_ready, n + 1)
                    act.wait_ge(y_ready, n + 2)
                    nc.scalar.copy(hidT[:, :, :], hT_ps[:, 0:FT * P].rearrange("p (f s) -> p f s", f=FT)
                                   ).then_inc(hT_copied, 1)
                    act.wait_ge(s_y_ready, n + 1)
                    nc.scalar.copy(h2T[:, bass.ds(n, 1), :].rearrange("p n c -> p (n c)"), s_y_ps[:, :]
                                   ).then_inc(s_y_copied, 1)

        @block.vector
        def _(dve):
            nc.vector.memset(wcol[0][:, :], 0.0).then_inc(gu_ready, 2)
            nc.vector.memset(wcol[1][:, :], 0.0).then_inc(y_ready, 2)
            nc.vector.memset(y[0][:, 0:1], 0.0).then_inc(pair_added, 2)
            nc.vector.memset(y[0][:, 1:2], 0.0).then_inc(y_done, 1)
            nc.vector.memset(y[0][:, 2:3], 0.0).then_inc(s_y_copied, 1)

            def rows_to_gather(b, m):
                nc.vector.tensor_copy(from_rows[b][:, :], gather_at[:, bass.ds(m, 1)]).then_inc(rows_ready, 1)

            def gated(hidden, ps, products_ready, done):
                done(nc.vector.scalar_tensor_tensor(hidden[:, :], hidden[:, :], 1.0, ps[:, 0, 0:FI],
                                                    ALU.add, ALU.mult))
                nc.vector.tensor_tensor(hidden[:, :], ps[:, 1, 0:FI], hidden[:, :],
                                        ALU.mult).then_inc(products_ready, 1)

            rows_to_gather(0, 0)
            rows_to_gather(1, 1)
            with dve.Fori(0, NL) as it:
                done = chained(dve, step, 2 * 2 * it)
                for b in range(2):
                    n = 2 * it + b
                    dve.wait_ge(x_in[b], 16 * it + 16)
                    nc.vector.tensor_copy(wcol[b][0:CAP, :], xg[b][0:CAP, bass.ds(2 * n + C, 1)])
                    nc.vector.tensor_copy(wcol[b][CAP:, :], xg[b][CAP:, bass.ds(2 * n + C + 1, 1)])
                    dve.wait_ge(x_ready, n + 1)
                    rows_to_gather(b, n + 2)
                    dve.wait_ge(pair_added, n + 1)
                    nc.vector.tensor_copy(to_rows[b][:, 0:1], add_at[:, 0, bass.ds(n, 1)])
                    nc.vector.tensor_copy(to_rows[b][:, 1:2], add_at[:, 1, bass.ds(n, 1)])
                    dve.wait_ge(s_tanh_ready, n + 1)
                    gated(s_hid, s_gu_ps, s_hid_ready, done)
                    dve.wait_ge(tanh_ready, n + 1)
                    gated(hid, gu_ps, hid_ready, done)
                    dve.wait_ge(y_ready, n + 3)
                    nc.vector.scalar_tensor_tensor(y[b][:, :], y_ps[:, :], wcol[b][:, 0:1], gates[:, 1, :],
                                                   ALU.mult, ALU.mult).then_inc(y_done, 1)

        @block.tensor
        def _(pe):
            def turn_rows(it, b):
                pe.wait_ge(x_in[b], 16 * it + 16)
                for k in range(KT):
                    last = nc.tensor.transpose(x_ps[:, k, :], xg[b][:, k * P:(k + 1) * P], ident[:, :])
                last.then_inc(x_ready, 1)

            turn_rows(0, 0)
            with pe.Fori(0, NL) as it:
                for b in range(2):
                    n = 2 * it + b

                    def shared_down(f):
                        return nc.tensor.matmul(s_y_ps[:, :], s_hid[:, f * P:(f + 1) * P], w_shd[:, f, :],
                                                start=(f == 0), stop=(f == FT - 1))

                    for j, wj in enumerate((shg, shu)):
                        for f in range(FT):
                            for k in range(KT):
                                last = nc.tensor.matmul(s_gu_ps[:, j, f * P:(f + 1) * P], wj[:, k, f * P:(f + 1) * P],
                                                        h2T[:, bass.ds(n, 1), k * P:(k + 1) * P],
                                                        start=(k == 0), stop=(k == KT - 1))
                    last.then_inc(s_gu_ready, 1)
                    pe.wait_ge(xe_ready, n + 1)
                    pe.wait_ge(gu_in[b], 32 * it + 32)
                    for j, wj in enumerate((wg[b], wu[b])):
                        for k in range(KT):
                            for e in range(2):
                                last = nc.tensor.matmul(gu_ps[slots[e], j, 0:FI], xeT[:, k, slots[e]],
                                                        wj[:, e, k, :], start=(k == 0), stop=(k == KT - 1))
                    last.then_inc(gu_ready, 1)
                    turn_rows(it + b, 1 - b)
                    pe.wait_ge(s_hid_ready, n + 1)
                    pe.wait_ge(s_y_copied, n + 1)
                    for f in range(FT - 1):
                        shared_down(f)
                    pe.wait_ge(hid_ready, n + 1)
                    for f in range(FT):
                        last = nc.tensor.transpose(hT_ps[:, f * P:(f + 1) * P], hid[:, f * P:(f + 1) * P],
                                                   ident[:, :])
                    last.then_inc(hT_ready, 1)
                    shared_down(FT - 1).then_inc(s_y_ready, 1)
                    pe.wait_ge(hT_copied, n + 1)
                    pe.wait_ge(d_in[b], 16 * it + 16)
                    pe.wait_ge(y_done, n + 1)
                    for f in range(FT):
                        for e in range(2):
                            last = nc.tensor.matmul(y_ps[slots[e], :], hidT[:, f, slots[e]], wd[b][:, e, f, :],
                                                    start=(f == 0), stop=(f == FT - 1))
                    last.then_inc(y_ready, 1)


def sum_up(nc, acc_dram, h2T, out, T):
    NT = T // TT
    NB = 4
    with ExitStack() as ctx:
        rows = [ctx.enter_context(nc.sbuf_tensor(f"s_rows{b}", [P, TB, C], F32)) for b in range(NB)]
        rows_in = [ctx.enter_context(nc.semaphore(f"s_rows_in{b}")) for b in range(NB)]
        rows_out = [ctx.enter_context(nc.semaphore(f"s_rows_out{b}")) for b in range(NB)]
        summed = ctx.enter_context(nc.semaphore("s_summed"))
        block = ctx.enter_context(nc.Block())

        @block.sync
        def _(sp):
            for n in range(NT):
                if n >= NB:
                    sp.wait_ge(rows_out[n % NB], 16 * (n // NB))
                sp.dma_start(rows[n % NB][:, :, :], acc_dram[n * TT:(n + 1) * TT, :].rearrange(
                    "(t p) c -> p t c", p=P)).then_inc(rows_in[n % NB], 16)

        @block.vector
        def _(dve):
            for n in range(NT):
                dve.wait_ge(rows_in[n % NB], 16 * (n // NB + 1))
                nc.vector.tensor_tensor(rows[n % NB][:, :, :], rows[n % NB][:, :, :],
                                        h2T[:, n * TB:(n + 1) * TB, :], ALU.add).then_inc(summed, 1)

        @block.scalar
        def _(act):
            for n in range(NT):
                act.wait_ge(summed, n + 1)
                act.dma_start(out[n * TT:(n + 1) * TT, :].rearrange("(t p) c -> p t c", p=P),
                              rows[n % NB][:, :, :]).then_inc(rows_out[n % NB], 16)
            for b in range(min(NB, NT)):
                act.wait_ge(rows_out[b], 16 * ((NT - 1 - b) // NB + 1))


def layer_kernel(nc, x3, wq, wk, wv, wo, w_router, w_gate, w_up, w_down, w_sh_gate, w_sh_up, w_sh_down,
                 c, wmod, out3):
    x, out = x3[0], out3[0]
    T = x.shape[0]
    oT_dram = nc.dram_tensor("oT_scratch", (C, T), F32).ap()
    hT_dram = nc.dram_tensor("hT_scratch", (C, T), F32).ap()
    rows_dram = nc.dram_tensor("rows_scratch", (T, C + NE), F32).ap()
    acc_dram = nc.dram_tensor("acc_scratch", (T + P, C), F32).ap()
    keys_dram = nc.dram_tensor("keys_scratch", (NE, CAP), F32).ap()
    with ExitStack() as ctx:
        keep = {
            "ident": ctx.enter_context(nc.sbuf_tensor("ident", [P, P], F32)),
            "ones": ctx.enter_context(nc.sbuf_tensor("ones", [P, P], F32)),
            "cols": ctx.enter_context(nc.sbuf_tensor("mod_cols", [P, MODS, KT], F32)),
            "gates": ctx.enter_context(nc.sbuf_tensor("gates", [P, 2, C], F32)),
        }
        modulation(nc, c, wmod, keep)
        first_norm(nc, x, hT_dram, keep)
        attention(nc, hT_dram, T, wq, wk, wv, oT_dram, keep)
        def sb(name, shape, dt=F32):
            return ctx.enter_context(nc.sbuf_tensor(name, shape, dt))

        gather_at = sb("gather_at", [P, NE // 2 + 2], U32)
        add_at = sb("add_at", [P, 2, NE // 2], U32)
        h2T = sb("h2T", [P, T // P, KT * P])
        shg, shu = sb("sh_gate", [P, KT, FI]), sb("sh_up", [P, KT, FI])
        w_shd = sb("w_shd", [P, FT, C])
        with (nc.sbuf_tensor("keyT", [P, CAP + TT], F32) as keyT, nc.sbuf_tensor("woT", [P, KT, C], F32) as woT,
              nc.sbuf_tensor("wrT", [P, KT, NE], F32) as wrT):
            turn_weights(nc, wo, w_router, woT, wrT, w_shd, w_sh_down, keep)
            dense_part(nc, x, oT_dram, rows_dram, acc_dram, w_sh_gate, w_sh_up, woT, wrT, shg, shu, h2T, keyT, keep)
            slot_lists(nc, keyT, keys_dram, gather_at, add_at, T, keep)
        experts_part(nc, rows_dram, acc_dram, w_gate, w_up, w_down, gather_at, add_at, shg, shu, w_shd, h2T, T, keep)
        sum_up(nc, acc_dram, h2T, out, T)


_INS = ['L0_attn_x', 'L0_attn_Wq', 'L0_attn_Wk', 'L0_attn_Wv', 'L0_attn_Wo', 'L0_ffn_w_router', 'L0_ffn_w_gate',
        'L0_ffn_w_up', 'L0_ffn_w_down', 'L0_ffn_w_sh_gate', 'L0_ffn_w_sh_up', 'L0_ffn_w_sh_down', 'L0_c', 'L0_wmod']
_OUTS = [((1, 4096, 512), 'float32')]


def kernel(**inputs):
    import numpy as _np
    import concourse.bacc as _bacc
    from concourse import mybir as _mybir
    from concourse.bass_utils import run_bass_kernel_spmd as _run

    nc = _bacc.Bacc("TRN2", target_bir_lowering=False, num_devices=1)
    arrays, args = {}, []
    for name in _INS:
        a = _np.ascontiguousarray(inputs[name])
        arrays[f"in_{name}_dram"] = a
        args.append(nc.dram_tensor(f"in_{name}_dram", a.shape, _mybir.dt.from_np(a.dtype), kind="ExternalInput").ap())
    for i, (shape, dtype) in enumerate(_OUTS):
        dt = _mybir.dt.from_np(_np.dtype(dtype))
        args.append(nc.dram_tensor(f"out_{i}_dram", shape, dt, kind="ExternalOutput").ap())
    layer_kernel(nc, *args)
    r = _run(nc, [arrays], core_ids=[0])
    return r.results[0]["out_0_dram"]
```

```python
import concourse.bass as bass
from concourse import mybir
from contextlib import ExitStack

F32 = mybir.dt.float32
F32R = mybir.dt.float32r
U32 = mybir.dt.uint32
ALU = mybir.AluOpType
ACT = mybir.ActivationFunctionType

P = 128
C = 512
KT = C // P
H = 16
HD = C // H
HG = P // HD
NG = H // HG
TT = 512
TB = TT // P
SHIFT = 0.1
ATT_EPS = 1e-6
LN_EPS = 1e-5
NE = 64
TOPK = 4
CAP = 64
FI = 384
FT = FI // P
MODS = 6
SA, CA, GA, SB, CB, GB = range(MODS)
GATED = 0.5
SHARED_FIRST = 8


def wait_apart(eng, passed, *waits):
    for sem, value in zip(waits[::2], waits[1::2]):
        eng.wait_ge(sem, value)
    eng.sem_inc(passed, 1)


def chained(eng, sem, base=0):
    count = [base]

    def done(ins, passed=None):
        count[0] = count[0] + 1
        ins.then_inc(sem, 1)
        if passed:
            wait_apart(eng, passed, sem, count[0])
        else:
            eng.wait_ge(sem, count[0])

    return done


def normalize_rows(nc, dve, done, xb, xn, stats, mv, rs, var_ready, sd_ready, sd_count, passed=None):
    for t in range(TB):
        last = nc.vector.bn_stats(stats[:, t, :], xb[:, t, :])
    done(last, passed)
    for t in range(TB):
        last = nc.vector.bn_aggr(mv[:, t, :], stats[:, t, :])
    done(last)
    nc.vector.tensor_scalar(rs[:, 0, :], mv[:, :, 1], LN_EPS, None, ALU.add).then_inc(var_ready, 1)
    dve.wait_ge(sd_ready, sd_count)
    done(nc.vector.reciprocal(rs[:, 2, :], rs[:, 1, :]))
    done(nc.vector.tensor_tensor(rs[:, 1, :], rs[:, 2, :], rs[:, 2, :], ALU.mult))
    done(nc.vector.tensor_tensor(rs[:, 1, :], rs[:, 1, :], rs[:, 0, :], ALU.mult))
    done(nc.vector.tensor_scalar(rs[:, 1, :], rs[:, 1, :], -0.5, 1.5, ALU.mult, ALU.add))
    done(nc.vector.tensor_tensor(rs[:, 2, :], rs[:, 2, :], rs[:, 1, :], ALU.mult))
    for t in range(TB):
        last = nc.vector.tensor_scalar(xn[:, t, :], xb[:, t, :], mv[:, t, 0:1], rs[:, 2, t:t + 1],
                                       ALU.subtract, ALU.mult)
    return last


def first_part(nc, x, c, wmod, wq, wk, wv, k_dram, q_dram, v_dram, keep):
    T = x.shape[0]
    NT = T // TT
    NL = NT // 2
    NORM = 7
    UNITS = 2 * NG
    HALVES = (range(KT // 2), range(KT // 2, KT))
    with ExitStack() as ctx:
        def sb(name, shape, dt=F32):
            return ctx.enter_context(nc.sbuf_tensor("f_" + name, shape, dt))

        def sem(name):
            return ctx.enter_context(nc.semaphore("f_" + name))

        ccol, cexp, crep = sb("ccol", [P, KT]), sb("cexp", [P, KT]), sb("crep", [P, KT, P])
        wm = sb("wm", [P, 2, KT, C])
        rows = sb("mod_rows", [P, MODS, C])
        sign, size = sb("gate_sign", [P, C]), sb("gate_size", [P, C])
        w_rows = [sb(f"w_rows{b}", [P, KT, C]) for b in range(2)]
        wT = [sb(f"wT_{part}", [P, 3, KT, C], F32R) for part in ("hi", "lo")]
        xb = [sb(f"x{b}", [P, TB, C]) for b in range(2)]
        hT = sb("hT", [P, KT, TT])
        hparts = [[sb(f"hT_{part}{b}", [P, KT, TT], F32R) for part in ("hi", "lo")] for b in range(2)]
        parts = [sb(f"parts{b}", [P, 2, TT], F32R) for b in range(2)]
        vals = sb("vals", [P, TB, C])
        stats, mv, rs = sb("stats", [P, TB, 6]), sb("mv", [P, TB, 2]), sb("rs", [P, 3, TB])
        mod_ps = ctx.enter_context(nc.psum_tensor("mod_ps", [P, 2, C], F32))
        turned = ctx.enter_context(nc.psum_tensor("mod_turned", [P, 2, C], F32))
        xT_ps = ctx.enter_context(nc.psum_tensor("xT_ps", [P, 2, TT], F32))
        proj = ctx.enter_context(nc.psum_tensor("proj_ps", [P, 2, TT], F32))
        c_in = sem("c_in")
        wm_in = [sem(f"wm_in{m}") for m in range(MODS)]
        w_in = [sem(f"w_in{n}") for n in range(3)]
        x_in = [sem(f"x_in{b}") for b in range(2)]
        parts_out = [sem(f"parts_out{b}") for b in range(2)]
        vals_out = sem("vals_out")
        c_exp, c_ready, dve_step, pool_step = sem("c_exp"), sem("c_ready"), sem("dve_step"), sem("pool_step")
        norm_step, dve_passed = sem("norm_step"), sem("dve_passed")
        mod_ready, rows_ready = sem("mod_ready"), sem("rows_ready")
        turned_ready, turned_used = sem("turned_ready"), sem("turned_used")
        w_turned, w_hi, w_lo = sem("w_turned"), sem("w_hi"), sem("w_lo")
        var_ready, sd_ready, xn_ready = sem("var_ready"), sem("sd_ready"), sem("xn_ready")
        xT_ready, h_hi, h_lo = sem("xT_ready"), sem("h_hi"), sem("h_lo")
        unit_ready, unit_hi, unit_lo = sem("unit_ready"), sem("unit_hi"), sem("unit_lo")
        v_ready, v_copied = sem("v_ready"), sem("v_copied")
        block = ctx.enter_context(nc.Block())
        ident, cols, gates = keep["ident"], keep["cols"], keep["gates"]
        columns = [SA, CA, SB, CB]
        scales = {"k": 1.0, "q": HD ** -0.5}

        def unit_of(u):
            return "kq"[u // NG], u % NG

        @block.sync
        def _(sp):
            def load_mod(m):
                if m >= 2:
                    sp.wait_ge(mod_ready, m - 1)
                sp.dma_start(wm[:, m % 2, :, :], wmod[:, m * C:(m + 1) * C].rearrange(
                    "(p k) n -> p k n", p=P)).then_inc(wm_in[m], 16)

            def load_w(n, src):
                if n >= 2:
                    sp.wait_ge(w_turned, KT * (n - 1))
                sp.dma_start(w_rows[n % 2][:, :, :], src.rearrange("(o p) c -> p o c", p=P)).then_inc(w_in[n], 16)

            def step(it, b):
                n = 2 * it + b
                for u in range(UNITS):
                    kind, g = unit_of(u)
                    dst = k_dram if kind == "k" else q_dram
                    sp.wait_ge(unit_lo, UNITS * n + u + 1)
                    sp.dma_start(dst[g, :, :, bass.ds(n * TT, TT)], parts[u % 2][:, :, :].bitcast(F32)
                                 ).then_inc(parts_out[u % 2], 16)
                sp.wait_ge(v_copied, TB * n + TB + 2)
                sp.dma_start(v_dram[bass.ds(n * TT, TT), :].rearrange("(t p) c -> p t c", p=P),
                             vals[:, :, :]).then_inc(vals_out, 16)

            sp.dma_start(ccol[:, :], c[0, :].rearrange("(p k) -> p k", p=P)).then_inc(c_in, 16)
            load_mod(SA)
            load_mod(CA)
            load_w(0, wk)
            load_w(1, wq)
            load_w(2, wv)
            for m in range(2, MODS):
                load_mod(m)
            with sp.Fori(0, NL) as it:
                step(it, 0)
                step(it, 1)
            for b in range(2):
                sp.wait_ge(parts_out[b], 16 * (UNITS // 2) * NT + 16)
            sp.wait_ge(vals_out, 16 * NT + 16)

        @block.gpsimd
        def _(pool):
            def load_x(b, n):
                pool.dma_start(xb[b][:, :, :], x[bass.ds(n * TT, TT), :].rearrange(
                    "(t p) c -> p t c", p=P)).then_inc(x_in[b], 16)

            done = chained(pool, pool_step)
            load_x(0, 0)
            done(pool.memset(ident[:, :], 0.0))
            done(pool.affine_select(out=ident[:, :], in_=ident[:, :], compare_op=ALU.not_equal, fill=1.0,
                                    base=0, pattern=[[-1, P]], channel_multiplier=1))
            done(pool.memset(keep["ones"][:, :], 1.0))
            load_x(1, 1)
            with pool.Fori(0, NL - 1) as it:
                for b in range(2):
                    n = 2 * it + b
                    pool.wait_ge(xT_ready, KT * n + KT)
                    load_x(b, n + 2)

        @block.scalar
        def _(act):
            def mod_rows(m):
                act.wait_ge(mod_ready, m + 1)
                nc.scalar.copy(rows[:, m, :], mod_ps[:, m % 2, :]).then_inc(rows_ready, 1)

            def root(m):
                act.wait_ge(var_ready, m + 1)
                nc.scalar.activation(rs[:, 1, :], rs[:, 0, :], ACT.Sqrt).then_inc(sd_ready, 1)

            def modulated(b, m, which=range(KT)):
                for k in which:
                    act.wait_ge(xT_ready, KT * m + k + 1)
                    act.wait_ge(h_lo, KT * m + k + 1)
                    nc.scalar.activation(hT[:, k, :], xT_ps[:, k % 2, :], ACT.Identity,
                                         scale=cols[:, CA, k:k + 1], bias=cols[:, SA, k:k + 1])
                    nc.scalar.activation(hparts[b][0][:, k, :], xT_ps[:, k % 2, :], ACT.Identity,
                                         scale=cols[:, CA, k:k + 1], bias=cols[:, SA, k:k + 1]).then_inc(h_hi, 1)

            def units(n, which):
                for u in which:
                    kind, _ = unit_of(u)
                    act.wait_ge(unit_ready, UNITS * n + u + 1)
                    act.wait_ge(parts_out[u % 2], 16 * (UNITS // 2) * n + 16 * (u // 2) + 16)
                    nc.scalar.mul(parts[u % 2][:, 0, :], proj[:, u % 2, :], scales[kind]).then_inc(unit_hi, 1)

            def step(it, b, norm_ahead=True, last=False):
                n = 2 * it + b
                for half in HALVES:
                    units(n, half)
                    if not last:
                        modulated(1 - b, n + 1, half)
                units(n, range(KT, UNITS))
                for t in range(TB):
                    if t == 2 and norm_ahead:
                        root(n + 2)
                    act.wait_ge(v_ready, TB * n + t + 1)
                    if t == 0:
                        act.wait_ge(vals_out, 16 * n + 16)
                    nc.scalar.copy(vals[:, t, :], proj[:, t % 2, :]).then_inc(v_copied, 1)

            act.wait_ge(c_in, 16)
            nc.scalar.activation(cexp[:, :], ccol[:, :], ACT.Exp, scale=-1.0).then_inc(c_exp, 1)
            mod_rows(SA)
            mod_rows(CA)
            root(0)
            root(1)
            act.wait_ge(turned_used, 2)
            modulated(0, 0)
            for u in range(3 * KT):
                act.wait_ge(w_turned, u + 1)
                nc.scalar.copy(wT[0][:, u // KT, u % KT, :], turned[:, u % 2, :]).then_inc(w_hi, 1)
            for m in range(2, MODS):
                mod_rows(m)
            with act.Fori(0, NL - 1) as it:
                step(it, 0)
                step(it, 1)
            step(NL - 1, 0, norm_ahead=False)
            step(NL - 1, 1, norm_ahead=False, last=True)

        @block.vector
        def _(dve):
            once = chained(dve, dve_step)

            def keep_columns(n, m):
                dve.wait_ge(turned_ready, n + 1)
                one = 1.0 if m in (CA, CB) else 0.0
                src = turned[:, n % 2, :].rearrange("p (k t) -> p k t", k=KT)[:, :, 0]
                nc.vector.tensor_scalar(cols[:, m, :], src, one, None, ALU.add).then_inc(turned_used, 1)

            def norm(it, b, m, done, passed=None):
                dve.wait_ge(x_in[b], 16 * it + 16)
                normalize_rows(nc, dve, done, xb[b], xb[b], stats, mv, rs, var_ready, sd_ready,
                               m + 1, passed=passed).then_inc(xn_ready, 1)

            def rest(out, full, hi, scale=1.0):
                return nc.vector.scalar_tensor_tensor(out, full, scale, hi.bitcast(F32), ALU.mult, ALU.subtract)

            def h_rest(b, m, which=range(KT)):
                for k in which:
                    dve.wait_ge(h_hi, KT * m + k + 1)
                    rest(hparts[b][1][:, k, :], hT[:, k, :], hparts[b][0][:, k, :]).then_inc(h_lo, 1)

            def units(n, which):
                for u in which:
                    kind, _ = unit_of(u)
                    dve.wait_ge(unit_hi, UNITS * n + u + 1)
                    rest(parts[u % 2][:, 1, :], proj[:, u % 2, :], parts[u % 2][:, 0, :], scales[kind]
                         ).then_inc(unit_lo, 1)

            def step(it, b, done, last=False):
                n = 2 * it + b
                for half in HALVES:
                    units(n, half)
                    if not last:
                        h_rest(1 - b, n + 1, half)
                units(n, range(KT, UNITS))
                if done:
                    norm(it + 1, b, n + 2, done, passed=dve_passed)

            nc.vector.memset(stats[:, 0, :], 0.0).then_inc(parts_out[0], 16)
            nc.vector.memset(stats[:, 1, :], 0.0).then_inc(parts_out[1], 16)
            nc.vector.memset(stats[:, 2, :], 0.0).then_inc(vals_out, 16)
            nc.vector.memset(stats[:, 3, :], 0.0).then_inc(h_lo, KT)
            nc.vector.memset(mv[:, 0, :], 0.0).then_inc(v_copied, 2)
            dve.wait_ge(c_exp, 1)
            once(nc.vector.tensor_scalar(cexp[:, :], cexp[:, :], 1.0, None, ALU.add))
            once(nc.vector.reciprocal(cexp[:, :], cexp[:, :]))
            once(nc.vector.tensor_tensor(ccol[:, :], ccol[:, :], cexp[:, :], ALU.mult))
            once(nc.vector.memset(crep[:, :, :], 1.0))
            for k in range(KT):
                nc.vector.tensor_scalar(crep[:, k, :], crep[:, k, :], ccol[:, k:k + 1], None,
                                        ALU.mult).then_inc(c_ready, 1)
            first_norms = chained(dve, norm_step)
            norm(0, 0, 0, first_norms)
            norm(0, 1, 1, first_norms)
            keep_columns(0, SA)
            keep_columns(1, CA)
            h_rest(0, 0)
            for u in range(3 * KT):
                dve.wait_ge(w_hi, u + 1)
                rest(wT[1][:, u // KT, u % KT, :], turned[:, u % 2, :], wT[0][:, u // KT, u % KT, :]
                     ).then_inc(w_lo, 1)
            keep_columns(2, SB)
            keep_columns(3, CB)
            for n, (m, part) in enumerate(((GA, 1.0), (GB, GATED))):
                dve.wait_ge(rows_ready, m + 1)
                g = rows[:, m, :]
                once(nc.vector.tensor_scalar(sign[:, :], g, 0.0, 2.0 * part, ALU.is_ge, ALU.mult))
                once(nc.vector.tensor_scalar(sign[:, :], sign[:, :], part, None, ALU.subtract))
                once(nc.vector.scalar_tensor_tensor(size[:, :], g, -1.0, g, ALU.mult, ALU.max))
                once(nc.vector.scalar_tensor_tensor(gates[:, n, :], size[:, :], 0.25, sign[:, :],
                                                    ALU.max, ALU.mult))
            with dve.Fori(0, NL - 1) as it:
                done = chained(dve, norm_step, 2 * NORM * it + 2 * NORM)
                step(it, 0, done)
                step(it, 1, done)
            step(NL - 1, 0, None)
            step(NL - 1, 1, None, last=True)

        @block.tensor
        def _(pe):
            def modulate(m):
                pe.wait_ge(wm_in[m], 16)
                if m >= 2:
                    pe.wait_ge(rows_ready, m - 1)
                for k in range(KT):
                    last = nc.tensor.matmul(mod_ps[:, m % 2, :], crep[:, k, :], wm[:, m % 2, k, :],
                                            start=(k == 0), stop=(k == KT - 1))
                last.then_inc(mod_ready, 1)

            def turn_columns(n, m):
                pe.wait_ge(rows_ready, m + 1)
                for k in range(KT):
                    last = nc.tensor.transpose(turned[:, n % 2, k * P:(k + 1) * P],
                                               rows[:, m, k * P:(k + 1) * P], ident[:, :])
                last.then_inc(turned_ready, 1)

            def turn_group(b, m, which=range(KT)):
                pe.wait_ge(xn_ready, m + 1)
                for k in which:
                    pe.wait_ge(h_lo, KT * m + k + KT - 1)
                    for t in range(TB):
                        last = nc.tensor.transpose(xT_ps[:, k % 2, t * P:(t + 1) * P],
                                                   xb[b][:, t, k * P:(k + 1) * P], ident[:, :])
                    last.then_inc(xT_ready, 1)

            PRODUCTS = [(0, 0), (1, 0), (0, 1)]

            def summed(bank, stationary, moving):
                terms = [(a, m, k) for a, m in PRODUCTS for k in range(KT)]
                for n, (a, m, k) in enumerate(terms):
                    last = nc.tensor.matmul(bank, stationary(a, k), moving(m, k), start=(n == 0),
                                            stop=(n == len(terms) - 1))
                return last

            def units(b, n, which):
                for u in which:
                    kind, g = unit_of(u)
                    if u >= 2:
                        pe.wait_ge(unit_lo, UNITS * n + u - 1)
                    else:
                        pe.wait_ge(v_copied, TB * n + 1 + u)
                    summed(proj[:, u % 2, :], lambda a, k: wT[a][:, "kq".index(kind), k, g * P:(g + 1) * P],
                           lambda m, k: hparts[b][m][:, k, :]).then_inc(unit_ready, 1)

            def step(it, b, last=False):
                n = 2 * it + b
                pe.wait_ge(h_lo, KT * n + 2 * KT)
                for half in HALVES:
                    units(b, n, half)
                    if not last:
                        turn_group(1 - b, n + 1, half)
                units(b, n, range(KT, UNITS))
                for t in range(TB):
                    if t < 2:
                        pe.wait_ge(unit_lo, UNITS * n + UNITS - 1 + t)
                    else:
                        pe.wait_ge(v_copied, TB * n + t + 1)
                    summed(proj[:, t % 2, :], lambda a, k: hparts[b][a][:, k, t * P:(t + 1) * P],
                           lambda m, k: wT[m][:, 2, k, :]).then_inc(v_ready, 1)

            pe.wait_ge(c_ready, KT)
            modulate(SA)
            modulate(CA)
            pe.wait_ge(pool_step, 2)
            turn_columns(0, SA)
            turn_columns(1, CA)
            turn_group(0, 0)
            for u in range(3 * KT):
                pe.wait_ge(w_in[u // KT], 16)
                if u < 2:
                    pe.wait_ge(turned_used, u + 1)
                else:
                    pe.wait_ge(w_lo, u - 1)
                for o in range(KT):
                    last = nc.tensor.transpose(turned[:, u % 2, o * P:(o + 1) * P],
                                               w_rows[u // KT % 2][:, o, u % KT * P:(u % KT + 1) * P], ident[:, :])
                last.then_inc(w_turned, 1)
            for m in range(2, MODS):
                modulate(m)
            pe.wait_ge(w_lo, 3 * KT)
            turn_columns(2, SB)
            turn_columns(3, CB)
            with pe.Fori(0, NL - 1) as it:
                step(it, 0)
                step(it, 1)
            step(NL - 1, 0)
            step(NL - 1, 1, last=True)


CHUNK = 16


def attention_plan(NT):
    plan, late, quarters = [], [], []
    for i in range(NT):
        loads = {0: i + 2} if i + 2 < NT else {}
        if i + 1 == NT:
            loads = {TB + 3: NT, 2 * TB + 3: NT + 1}
        for j in range(TB * (i + 1)):
            plan.append(("s", i, j))
            late.append((i, j))
            if len(late) > 2:
                products(plan, quarters, NT, *late.pop(0))
            plan.append(("t", i, j))
            if j in loads:
                plan.append(("l", loads[j], 0))
            if quarters:
                plan.append(quarters.pop(0))
            li, lj = late[0]
            if len(late) > 1 and lj < TB * li:
                plan.append(("a", li, lj))
    for i, j in late:
        products(plan, quarters, NT, i, j)
    return plan + quarters


def ends_chunk(i, j):
    return j < TB * i and ((j + 1) % CHUNK == 0 or j + 1 == TB * i)


def products(plan, quarters, NT, i, j):
    if j > 1 and ends_chunk(i, j - 2):
        plan.append(("d", i, (j - 2) // CHUNK))
    plan.append(("p", i, j))
    if j == TB * (i + 1) - 1:
        plan.append(("n", i, 0))
        quarters += [("r", i, q) for q in range(4)]


def attention(nc, k_dram, q_dram, v_dram, T, oT_dram, keep):
    NT = T // TT
    plan = attention_plan(NT)
    STEPS = sum(e[0] == "s" for e in plan)
    ADDS = sum(e[0] == "a" and e[2] % CHUNK > 0 for e in plan)
    CHUNKS = sum(e[0] == "d" for e in plan)
    assert STEPS % 2 == 0 and NT % 2 == 0 and CHUNKS % 2 == 0
    LOADED = 16 * 9

    def before(event, what, order=plan):
        return sum(what(e) for e in order[:order.index(event) + 1])

    def step_of(i, j):
        return TB * i * (i + 1) // 2 + j

    def first_bank(step):
        return step % 2 * HG

    def width(i, j):
        return max(0, (j - TB * i) * P)

    def adds_for(i, j):
        if j >= TB * i:
            return 0
        return before(("a", i, j if j % CHUNK else j + 1), lambda e: e[0] == "a" and e[2] % CHUNK > 0)

    with ExitStack() as ctx:
        def sb(name, shape, dt=F32):
            return ctx.enter_context(nc.sbuf_tensor("at_" + name, shape, dt))

        def sem(name):
            return ctx.enter_context(nc.semaphore("at_" + name))

        kst, qst = sb("k_stack", [P, HG, T], F32R), sb("q_stack", [P, 4, HG, TT], F32R)
        vals = sb("vals", [P, T // P, P])
        w = sb("w", [P, 4, HG, TT])
        acc = sb("acc", [P, 2, HG, TT])
        rden, o = sb("rden", [P, TT]), sb("o", [P, 2, TT])
        s_ps = ctx.enter_context(nc.psum_tensor("s_ps", [P, HG + 2, TT], F32))
        num = ctx.enter_context(nc.psum_tensor("num_ps", [P, TT], F32))
        den = ctx.enter_context(nc.psum_tensor("den_ps", [P, TT], F32))
        loaded = [sem(f"loaded{b}") for b in range(2)]
        s_ready, sp_passed = sem("s_ready"), sem("sp_passed")
        relu = [sem("relu_a"), sem("relu_b")]
        masked, pv_done, chunk_done = sem("masked"), sem("pv_done"), sem("chunk_done")
        added, added_pool = sem("added"), sem("added_pool")
        num_out, den_out, rden_ready, o_ready = sem("num_out"), sem("den_out"), sem("rden_ready"), sem("o_ready")
        o_out = [sem(f"o_out{b}") for b in range(2)]
        pool_passed = sem("pool_passed")
        block = ctx.enter_context(nc.Block())
        ident, ones = keep["ident"], keep["ones"]

        def relu_done(eng, g, step, half):
            eng.wait_ge(relu[half], g * STEPS + step + 1)

        def w_free(eng, g, i, j):
            step = step_of(i, j)
            eng.wait_ge(pv_done, g * STEPS + step + 1)
            if step >= 4:
                li = i if j >= 4 else i - 1
                need = adds_for(li, j - 4 if j >= 4 else TB * i + j - 4)
                if need:
                    eng.wait_ge(added, g * ADDS + need)
                    eng.wait_ge(added_pool, g * ADDS + need)

        @block.sync
        def _(sp):
            def load(g, i):
                cols, done = slice(i * TT, (i + 1) * TT), loaded[i % 2]
                for src, dst, order in ((k_dram, kst[:, :, cols], (0, 1, 0, 1)), (q_dram, qst[:, i % 4, :, :], (0, 0, 1, 1))):
                    for r, part in enumerate(order):
                        sp.dma_start(dst[r * HD:(r + 1) * HD, :, :].bitcast(F32),
                                     src[bass.ds(g, 1), :, part, cols].rearrange("g (h d) t -> d (g h) t", d=HD)
                                     ).then_inc(done, 16)
                sp.dma_start(vals[:, TB * i:TB * (i + 1), :], v_dram[cols, bass.ds(g * P, P)].rearrange(
                    "(t p) o -> p t o", p=P)).then_inc(done, 16)

            load(0, 0)
            load(0, 1)
            with sp.Fori(0, NG) as g:
                now = 0
                for kind, i, j in plan:
                    if kind == "s":
                        now = i
                    if kind == "l":
                        wait_apart(sp, sp_passed, loaded[i % 2], LOADED * (g * (NT // 2) + i // 2))
                        last = step_of(now, TB * (i - NT + 1)) if i >= NT else step_of(max(now - 1, 0), 0)
                        sp.wait_ge(pv_done, g * STEPS + last + 4)
                        load((g + 1) % NG if i >= NT else g, i % NT)
                    elif kind == "r" and j == 3:
                        sp.wait_ge(o_ready, 4 * (g * NT + i) + 8)
                        sp.dma_start(oT_dram[bass.ds(g * P, P), i * TT:(i + 1) * TT],
                                     o[:, i % 2, :]).then_inc(o_out[i % 2], 16)
            for b in range(2):
                sp.wait_ge(o_out[b], 16 + 16 * NG * NT // 2)
                sp.wait_ge(loaded[b], LOADED * (NG * NT // 2 + 1))

        @block.scalar
        def _(act):
            with act.Fori(0, NG) as g:
                for kind, i, j in plan:
                    if kind == "s":
                        q0, step = width(i, j), step_of(i, j)
                        w_free(act, g, i, j)
                        act.wait_ge(s_ready, 2 * (g * STEPS + step) + 1)
                        bank = first_bank(step)
                        nc.scalar.activation(w[:, step % 4, 0:2, q0:], s_ps[:, bank:bank + 2, q0:], ACT.Relu,
                                             bias=SHIFT).then_inc(relu[0], 1)
                    elif kind == "t":
                        q0, step = width(i, j), step_of(i, j)
                        act.wait_ge(s_ready, 2 * (g * STEPS + step) + 2)
                        nc.scalar.activation(w[:, step % 4, 2:4, q0:], s_ps[:, 2:4, q0:], ACT.Relu,
                                             bias=SHIFT).then_inc(relu[1], 1)
                    elif kind == "n":
                        act.wait_ge(pv_done, g * STEPS + step_of(i + 1, 0) + 4)
                        act.wait_ge(o_out[i % 2], 16 * (g * (NT // 2) + i // 2) + 16)
                        nc.scalar.copy(o[:, i % 2, :], num[:, :]).then_inc(num_out, 1)

        @block.vector
        def _(dve):
            nc.vector.memset(rden[:, :], 0.0).then_inc(pv_done, 4)
            nc.vector.memset(acc[:, 0, 0, :], 0.0).then_inc(chunk_done, 2)
            nc.vector.memset(acc[:, 0, 1, :], 0.0).then_inc(den_out, 1)
            nc.vector.memset(acc[:, 0, 2, :], 0.0).then_inc(o_ready, 4)
            nc.vector.memset(o[:, 0, :], 0.0).then_inc(o_out[0], 16)
            nc.vector.memset(o[:, 1, :], 0.0).then_inc(o_out[1], 16)
            with dve.Fori(0, NG) as g:
                adds = chunk = 0
                for kind, i, j in plan:
                    if kind == "a" and j % CHUNK:
                        step = step_of(i, j)
                        relu_done(dve, g, step, 0)
                        relu_done(dve, g, step, 1)
                        total = acc[:, chunk % 2, 0:HG - 1, :]
                        if j % CHUNK == 1:
                            dve.wait_ge(chunk_done, g * CHUNKS + chunk + 1)
                            prev = w[:, (step - 1) % 4, 0:HG - 1, :]
                        else:
                            dve.wait_ge(added, g * ADDS + adds)
                            prev = total
                        nc.vector.tensor_tensor(total, prev, w[:, step % 4, 0:HG - 1, :], ALU.add).then_inc(added, 1)
                        adds += 1
                        chunk += ends_chunk(i, j)
                    elif kind == "n":
                        dve.wait_ge(o_ready, 4 * (g * NT + i) + 4)
                        dve.wait_ge(pv_done, g * STEPS + step_of(i + 1, 0) + 4)
                        nc.vector.tensor_scalar(rden[:, :], den[:, :], ATT_EPS, None, ALU.add).then_inc(den_out, 1)
                    elif kind == "r":
                        cut = slice(j * P, (j + 1) * P)
                        dve.wait_ge(den_out, g * NT + i + 2)
                        nc.vector.reciprocal(rden[:, cut], rden[:, cut]).then_inc(rden_ready, 1)
                        dve.wait_ge(rden_ready, 4 * (g * NT + i) + j + 1)
                        dve.wait_ge(num_out, g * NT + i + 1)
                        nc.vector.tensor_tensor(o[:, i % 2, cut], o[:, i % 2, cut], rden[:, cut],
                                                ALU.mult).then_inc(o_ready, 1)

        @block.gpsimd
        def _(pool):
            with pool.Fori(0, NG) as g:
                adds = chunk = 0
                for kind, i, j in plan:
                    if kind == "a" and j % CHUNK:
                        step = step_of(i, j)
                        relu_done(pool, g, step, 1)
                        total = acc[:, chunk % 2, HG - 1, :]
                        if j % CHUNK == 1:
                            pool.wait_ge(chunk_done, g * CHUNKS + chunk + 1)
                            prev = w[:, (step - 1) % 4, HG - 1, :]
                            relu_done(pool, g, step - 1, 1)
                        else:
                            pool.wait_ge(added_pool, g * ADDS + adds)
                            prev = total
                        pool.sem_inc(pool_passed, 1)
                        nc.gpsimd.tensor_tensor(total, prev, w[:, step % 4, HG - 1, :],
                                                ALU.add).then_inc(added_pool, 1)
                        adds += 1
                        chunk += ends_chunk(i, j)
                    if kind == "t" and j >= TB * i:
                        q0, step = width(i, j), step_of(i, j)
                        relu_done(pool, g, step, 0)
                        relu_done(pool, g, step, 1)
                        pool.sem_inc(pool_passed, 1)
                        tri = w[:, step % 4, :, q0:q0 + P]
                        pool.affine_select(out=tri, in_=tri, compare_op=ALU.is_ge, fill=0.0, base=0,
                                           pattern=[[0, HG], [1, P]], channel_multiplier=-1).then_inc(masked, 1)

        @block.tensor
        def _(pe):
            with pe.Fori(0, NG) as g:
                chunk = diag = 0
                for kind, i, j in plan:
                    if kind in "st":
                        q0, step, half = width(i, j), step_of(i, j), "st".index(kind)
                        if j == 0 and half == 0:
                            pe.wait_ge(loaded[i % 2], LOADED * (g * (NT // 2) + i // 2 + 1))
                        if step >= 2 - half:
                            relu_done(pe, g, step - 2 + half, half)
                        for h in (2 * half, 2 * half + 1):
                            bank = h if half else h + first_bank(step)
                            last = nc.tensor.matmul(s_ps[:, bank, q0:], kst[:, h, j * P:(j + 1) * P],
                                                    qst[:, i % 4, h, q0:], start=True, stop=True)
                        last.then_inc(s_ready, 1)
                    elif kind == "p":
                        q0, step = width(i, j), step_of(i, j)
                        if j == 0:
                            if i >= 1:
                                pe.wait_ge(num_out, g * NT + i)
                            pe.wait_ge(den_out, g * NT + i + 1)
                        relu_done(pe, g, step, 0)
                        relu_done(pe, g, step, 1)
                        cut = j >= TB * i
                        if cut:
                            diag += 1
                            pe.wait_ge(masked, g * TB * NT + diag)
                        last_j = j == TB * (i + 1) - 1
                        for h in range(HG):
                            last = nc.tensor.matmul(num[h * HD:(h + 1) * HD, q0:], vals[:, j, h * HD:(h + 1) * HD],
                                                    w[:, step % 4, h, q0:], start=(j == 0), stop=last_j)
                        if cut:
                            for h in range(HG):
                                last = nc.tensor.matmul(den[h * HD:(h + 1) * HD, q0:], ones[:, 0:HD],
                                                        w[:, step % 4, h, q0:], start=(j == TB * i <= CHUNK),
                                                        stop=last_j)
                        last.then_inc(pv_done, 1)
                    elif kind == "d":
                        need = adds_for(i, min(CHUNK * (j + 1), TB * i) - 1)
                        pe.wait_ge(added, g * ADDS + need)
                        pe.wait_ge(added_pool, g * ADDS + need)
                        for h in range(HG):
                            last = nc.tensor.matmul(den[h * HD:(h + 1) * HD, :], ones[:, 0:HD],
                                                    acc[:, chunk % 2, h, :], start=(j == 0 and TB * i > CHUNK), stop=False)
                        last.then_inc(chunk_done, 1)
                        chunk += 1


def dense_part(nc, x, oT_dram, rows_dram, acc_dram, wo, w_router, w_sh_gate, w_sh_up, w_sh_down, shg, shu, w_shd,
               h2T, keyT, keep):
    T = x.shape[0]
    NT = T // TT
    NL = NT // 2
    NORM = 7
    CHOICE = 6 + TOPK
    PER_BODY = 2 * NORM + 2 * CHOICE
    with ExitStack() as ctx:
        def sb(name, shape, dt=F32):
            return ctx.enter_context(nc.sbuf_tensor("d_" + name, shape, dt))

        def sem(name):
            return ctx.enter_context(nc.semaphore("d_" + name))

        wo_rows, router_rows = sb("wo_rows", [P, KT, C]), sb("router_rows", [NE, C])
        woT, wrT = sb("woT", [P, KT, C]), sb("wrT", [P, KT, NE])
        oTb = [sb(f"oT{b}", [P, KT, TT]) for b in range(2)]
        xb = [sb(f"x{b}", [P, TB, C]) for b in range(2)]
        xn = [sb(f"xn{b}", [P, TB, C]) for b in range(2)]
        stats, mv, rs = sb("stats", [P, TB, 6]), sb("mv", [P, TB, 2]), sb("rs", [P, 3, TB])
        lT = sb("logitsT", [NE, TT])
        lg = sb("logits", [P, TB, NE])
        top = sb("top", [P, TB, 8])
        topi = sb("topi", [P, TB, 8], U32)
        topf = sb("topf", [P, TB, 8])
        chosen = sb("chosen", [P, TB, NE])
        soft = sb("soft", [P, TB, NE])
        total = sb("total", [P, TB])
        wt = [sb(f"wt{b}", [P, TB, NE]) for b in range(2)]
        keys = sb("keys", [P, TB, 2, NE])
        left = sb("left", [P, TB])
        lefti = sb("lefti", [P, TB], mybir.dt.int32)
        experts = sb("experts", [P, NE])
        expertsi = sb("expertsi", [P, NE], mybir.dt.int32)
        zero = sb("zero", [P, C])
        y_ps = ctx.enter_context(nc.psum_tensor("d_y_ps", [P, TB, C], F32))
        misc = ctx.enter_context(nc.psum_tensor("d_misc_ps", [P, KT, TT], F32))
        sh_in, w_in, down_in = sem("sh_in"), sem("w_in"), sem("down_in")
        w_turned, woT_ready, wrT_ready = sem("w_turned"), sem("woT_ready"), sem("wrT_ready")
        oT_in = [sem(f"oT_in{b}") for b in range(2)]
        x_in = [sem(f"x_in{b}") for b in range(2)]
        xn_out = [sem(f"xn_out{b}") for b in range(2)]
        wt_out = [sem(f"wt_out{b}") for b in range(2)]
        acc_out = [sem(f"acc_out{b}") for b in range(2)]
        zero_out = sem("zero_out")
        consts = sem("consts")
        const_step = sem("const_step")
        y_ready, x1_ready = sem("y_ready"), sem("x1_ready")
        var_ready, sd_ready, xn_ready = sem("var_ready"), sem("sd_ready"), sem("xn_ready")
        xT_ready, xT_copied = sem("xT_ready"), sem("xT_copied")
        lT_ready, lT_copied = sem("lT_ready"), sem("lT_copied")
        lg_ready, lg_copied = sem("lg_ready"), sem("lg_copied")
        kT_ready, kT_copied = sem("kT_ready"), sem("kT_copied")
        soft_in, soft_out, wt_ready, keys_ready = sem("soft_in"), sem("soft_out"), sem("wt_ready"), sem("keys_ready")
        dve_step, dve_passed, pe_passed = sem("dve_step"), sem("dve_passed"), sem("pe_passed")
        block = ctx.enter_context(nc.Block())
        ident, cols, gates = keep["ident"], keep["cols"], keep["gates"]

        @block.sync
        def _(sp):
            def put_x1(b, m):
                sp.wait_ge(x1_ready, TB * m + TB)
                sp.dma_start(acc_dram[bass.ds(m * TT, TT), :].rearrange("(t p) c -> p t c", p=P),
                             xb[b][:, :, :]).then_inc(acc_out[b], 16)

            def put_norm(b, m):
                sp.wait_ge(xn_ready, m + 1)
                sp.dma_start(rows_dram[bass.ds(m * TT, TT), 0:C].rearrange("(t p) c -> p t c", p=P),
                             xn[b][:, :, :]).then_inc(xn_out[b], 16)

            def step(it, b, last=False):
                n = 2 * it + b
                if not last:
                    put_x1(1 - b, n + 1)
                    put_norm(1 - b, n + 1)
                sp.wait_ge(wt_ready, n + 1)
                sp.dma_start(rows_dram[bass.ds(n * TT, TT), C:C + NE].rearrange("(t p) c -> p t c", p=P),
                             wt[b][:, :, :]).then_inc(wt_out[b], 16)

            sp.dma_start(wo_rows[:, :, :], wo.rearrange("(o p) c -> p o c", p=P)).then_inc(w_in, 16)
            sp.dma_start(router_rows[:, :], w_router).then_inc(w_in, 16)
            sp.dma_start(w_shd[:, :, :], w_sh_down.rearrange("(f p) c -> p f c", p=P)).then_inc(down_in, 16)
            sp.dma_start(shg[:, :, :], w_sh_gate.rearrange("(k p) i -> p k i", p=P)).then_inc(sh_in, 16)
            sp.dma_start(shu[:, :, :], w_sh_up.rearrange("(k p) i -> p k i", p=P)).then_inc(sh_in, 16)
            put_x1(0, 0)
            put_norm(0, 0)
            with sp.Fori(0, NL - 1) as it:
                step(it, 0)
                step(it, 1)
            step(NL - 1, 0)
            step(NL - 1, 1, last=True)
            sp.wait_ge(sh_in, 32)
            for b in range(2):
                sp.wait_ge(xn_out[b], 16 * NL + 16)
                sp.wait_ge(wt_out[b], 16 * NL + 16)
                sp.wait_ge(acc_out[b], 16 * NL)

        @block.gpsimd
        def _(pool):
            def get(b, n):
                pool.dma_start(oTb[b][:, :, :], oT_dram[:, bass.ds(n * TT, TT)].rearrange(
                    "(k p) t -> p k t", p=P)).then_inc(oT_in[b], 16)

            def get_x(b, n):
                pool.dma_start(xb[b][:, :, :], x[bass.ds(n * TT, TT), :].rearrange(
                    "(t p) c -> p t c", p=P)).then_inc(x_in[b], 16)

            for b in range(2):
                get(b, b)
                get_x(b, b)
            done = chained(pool, const_step)
            done(pool.iota(lefti[:, :], [[-P, TB]], base=T, channel_multiplier=-1))
            done(pool.iota(expertsi[:, :], [[1, NE]], base=0, channel_multiplier=0))
            pool.tensor_copy(left[:, :], lefti[:, :]).then_inc(consts, 1)
            pool.tensor_copy(experts[:, :], expertsi[:, :]).then_inc(consts, 1)
            done(pool.memset(zero[:, :], 0.0))
            pool.dma_start(acc_dram[T:T + P, :], zero[:, :]).then_inc(zero_out, 16)
            with pool.Fori(0, NL - 1) as it:
                for b in range(2):
                    n = 2 * it + b
                    pool.wait_ge(y_ready, TB * n + TB)
                    get(b, n + 2)
                    pool.wait_ge(xn_ready, n + 1)
                    pool.wait_ge(acc_out[b], 16 * it + 16)
                    get_x(b, n + 2)
            pool.wait_ge(zero_out, 16)

        @block.scalar
        def _(act):
            def root(m):
                act.wait_ge(var_ready, m + 1)
                nc.scalar.activation(rs[:, 1, :], rs[:, 0, :], ACT.Sqrt).then_inc(sd_ready, 1)

            def keys_out(it):
                act.wait_ge(kT_ready, it + 1)
                nc.scalar.copy(keyT[:, bass.ds(it * TT, TT)], misc[:, 2, :]).then_inc(kT_copied, 1)

            def step(it, b, last=False):
                n = 2 * it + b
                for k in range(KT):
                    act.wait_ge(xT_ready, KT * n + k + 1 + KT)
                    nc.scalar.activation(h2T[:, bass.ds(n * TB, TB), k * P:(k + 1) * P],
                                         misc[:, k, :].rearrange("p (t q) -> p t q", t=TB), ACT.Identity,
                                         scale=cols[:, CB, k:k + 1], bias=cols[:, SB, k:k + 1]
                                         ).then_inc(xT_copied, 1)
                act.wait_ge(lT_ready, n + 1)
                nc.scalar.copy(lT[:, :], misc[0:NE, 0, :]).then_inc(lT_copied, 1)
                if b == 0:
                    keys_out(it)
                act.wait_ge(lg_ready, n + 1)
                nc.scalar.copy(lg[:, :, :], misc[:, 1, 0:TB * NE].rearrange("p (t e) -> p t e", t=TB)
                               ).then_inc(lg_copied, 1)
                if not last:
                    root(n + 1)
                act.wait_ge(soft_in, n + 1)
                nc.scalar.activation(soft[:, :, :], soft[:, :, :], ACT.Exp).then_inc(soft_out, 1)

            act.wait_ge(w_turned, KT + 1)
            nc.scalar.copy(wrT[:, :, :], misc[:, :, 0:NE]).then_inc(wrT_ready, 1)
            root(0)
            with act.Fori(0, NL - 1) as it:
                step(it, 0)
                step(it, 1)
            step(NL - 1, 0)
            step(NL - 1, 1, last=True)
            keys_out(NL)

        @block.vector
        def _(dve):
            nc.vector.memset(keys[:, :, :, :], 0.0).then_inc(keys_ready, 2)
            nc.vector.memset(lg[:, 0, :], 0.0).then_inc(xT_ready, KT)
            nc.vector.memset(lg[:, 1, :], 0.0).then_inc(lg_copied, 1)
            for b in range(2):
                nc.vector.memset(wt[b][:, 1, :], 0.0).then_inc(xn_out[b], 16)
                nc.vector.memset(wt[b][:, 2, :], 0.0).then_inc(wt_out[b], 16)
            dve.wait_ge(consts, 2)
            for k in range(KT):
                dve.wait_ge(w_turned, k + 1)
                nc.vector.tensor_tensor(woT[:, k, :], y_ps[:, k, :], gates[:, 0, :], ALU.mult).then_inc(woT_ready, 1)
            dve.wait_ge(down_in, 16)
            for f in range(FT):
                nc.vector.tensor_tensor(w_shd[:, f, :], w_shd[:, f, :], gates[:, 1, :], ALU.mult)

            def x1_and_norm(it, b, m, done, started=True):
                dve.wait_ge(x_in[b], 16 * it + 16)
                for t in range(TB):
                    dve.wait_ge(y_ready, TB * m + t + 1)
                    nc.vector.tensor_tensor(xb[b][:, t, :], y_ps[:, t, :], xb[b][:, t, :],
                                            ALU.add).then_inc(x1_ready, 1)
                dve.wait_ge(x1_ready, TB * m + TB)
                dve.wait_ge(xn_out[b], 16 * it + 16)
                dve.wait_ge(xT_ready, KT * m if started else KT)
                normalize_rows(nc, dve, done, xb[b], xn[b], stats, mv, rs, var_ready, sd_ready,
                               m + 1, passed=dve_passed).then_inc(xn_ready, 1)

            def choice(it, b, done):
                n = 2 * it + b
                wait_apart(dve, dve_passed, lg_copied, n + 2)
                for t in range(TB):
                    last = nc.vector.max(top[:, t, :], lg[:, t, :])
                done(last, dve_passed)
                for t in range(TB):
                    nc.vector.max_index(topi[:, t, :], top[:, t, :], lg[:, t, :])
                    last = nc.vector.tensor_scalar(soft[:, t, :], lg[:, t, :], top[:, t, 0:1], None, ALU.subtract)
                last.then_inc(soft_in, 1)
                dve.wait_ge(soft_in, n + 1)
                done(nc.vector.tensor_copy(topf[:, :, :], topi[:, :, :]))
                for t in range(TB):
                    last = nc.vector.tensor_scalar(chosen[:, t, :], experts[:, :], topf[:, t, 0:1], None,
                                                   ALU.is_equal)
                done(last)
                for r in range(1, TOPK):
                    for t in range(TB):
                        last = nc.vector.scalar_tensor_tensor(chosen[:, t, :], experts[:, :], topf[:, t, r:r + 1],
                                                              chosen[:, t, :], ALU.is_equal, ALU.add)
                    done(last)
                if b == 0:
                    dve.wait_ge(kT_ready, it + 1)
                for t in range(TB):
                    last = nc.vector.tensor_scalar(keys[:, t, b, :], chosen[:, t, :], left[:, t:t + 1], None,
                                                   ALU.mult)
                last.then_inc(keys_ready, 1)
                dve.wait_ge(keys_ready, n + 3)
                done(nc.vector.tensor_scalar(left[:, :], left[:, :], float(TT), None, ALU.subtract))
                dve.wait_ge(soft_out, n + 1)
                done(nc.vector.tensor_tensor(soft[:, :, :], soft[:, :, :], chosen[:, :, :], ALU.mult))
                done(nc.vector.reduce_sum(total[:, :], soft[:, :, :], axis=mybir.AxisListType.X))
                done(nc.vector.reciprocal(total[:, :], total[:, :]))
                dve.wait_ge(wt_out[b], 16 * it + 16)
                for t in range(TB):
                    last = nc.vector.tensor_scalar(wt[b][:, t, :], soft[:, t, :], total[:, t:t + 1], None, ALU.mult)
                last.then_inc(wt_ready, 1)

            def step(it, b, done, last=False):
                if not last:
                    x1_and_norm(it + b, 1 - b, 2 * it + b + 1, done)
                choice(it, b, done)

            x1_and_norm(0, 0, 0, chained(dve, dve_step), started=False)
            with dve.Fori(0, NL - 1) as it:
                done = chained(dve, dve_step, PER_BODY * it + NORM)
                step(it, 0, done)
                step(it, 1, done)
            done = chained(dve, dve_step, PER_BODY * (NL - 1) + NORM)
            step(NL - 1, 0, done)
            step(NL - 1, 1, done, last=True)

        @block.tensor
        def _(pe):
            def products(it, b, m, tiles, started=True):
                pe.wait_ge(oT_in[b], 16 * it + 16)
                for t in tiles:
                    if started:
                        pe.wait_ge(x1_ready, TB * (m - 1) + t + 1)
                    for k in range(KT):
                        last = nc.tensor.matmul(y_ps[:, t, :], oTb[b][:, k, t * P:(t + 1) * P], woT[:, k, :],
                                                start=(k == 0), stop=(k == KT - 1))
                    last.then_inc(y_ready, 1)

            def turn_keys():
                for t in range(TB):
                    last = nc.tensor.transpose(misc[:, 2, t * P:(t + 1) * P], keys[:, t, :, :].rearrange(
                        "p b e -> p (b e)"), ident[:, :])
                last.then_inc(kT_ready, 1)

            def step(it, b, next_one=True, next_but_one=True):
                n = 2 * it + b
                pe.wait_ge(xn_ready, n + 1)
                for k in range(KT):
                    if k == 1:
                        pe.wait_ge(lg_copied, n + 1)
                    if k == 2 and b == 1:
                        pe.wait_ge(kT_copied, it + 1)
                    for t in range(TB):
                        last = nc.tensor.transpose(misc[:, k, t * P:(t + 1) * P], xn[b][:, t, k * P:(k + 1) * P],
                                                   ident[:, :])
                    last.then_inc(xT_ready, 1)
                pe.wait_ge(xT_copied, KT * n + KT)
                for k in range(KT):
                    last = nc.tensor.matmul(misc[0:NE, 0, :], wrT[:, k, :], h2T[:, bass.ds(n * TB, TB),
                                                                               k * P:(k + 1) * P],
                                            start=(k == 0), stop=(k == KT - 1))
                last.then_inc(lT_ready, 1)
                if b == 0:
                    pe.wait_ge(keys_ready, n + 2)
                    turn_keys()
                if next_one:
                    products(it + b, 1 - b, n + 1, [TB - 1])
                wait_apart(pe, pe_passed, lT_copied, n + 1)
                for t in range(TB):
                    last = nc.tensor.transpose(misc[:, 1, t * NE:(t + 1) * NE], lT[:, t * P:(t + 1) * P],
                                               ident[0:NE, 0:NE])
                last.then_inc(lg_ready, 1)
                if next_but_one:
                    products(it + 1, b, n + 2, range(TB - 1))

            pe.wait_ge(w_in, 32)
            for k in range(KT):
                for o in range(KT):
                    last = nc.tensor.transpose(y_ps[:, k, o * P:(o + 1) * P], wo_rows[:, o, k * P:(k + 1) * P],
                                               ident[:, :])
                last.then_inc(w_turned, 1)
            for k in range(KT):
                last = nc.tensor.transpose(misc[:, k, 0:NE], router_rows[:, k * P:(k + 1) * P], ident[0:NE, 0:NE])
            last.then_inc(w_turned, 1)
            pe.wait_ge(woT_ready, KT)
            products(0, 0, 0, range(TB), started=False)
            products(0, 1, 1, range(TB - 1))
            pe.wait_ge(wrT_ready, 1)
            with pe.Fori(0, NL - 1) as it:
                step(it, 0)
                step(it, 1)
            step(NL - 1, 0, next_but_one=False)
            step(NL - 1, 1, next_one=False, next_but_one=False)
            pe.wait_ge(keys_ready, NT + 2)
            pe.wait_ge(xT_copied, KT * NT)
            turn_keys()


def shared_gate_up(nc, ps, shg, shu, h2T, tile):
    for j, wj in enumerate((shg, shu)):
        for f in range(FT):
            for k in range(KT):
                last = nc.tensor.matmul(ps[:, j, f * P:(f + 1) * P], wj[:, k, f * P:(f + 1) * P],
                                        h2T[:, bass.ds(tile, 1), k * P:(k + 1) * P],
                                        start=(k == 0), stop=(k == KT - 1))
    return last


def shared_down(nc, ps, hidden, w_shd, f):
    return nc.tensor.matmul(ps, hidden[:, f * P:(f + 1) * P], w_shd[:, f, :], start=(f == 0), stop=(f == FT - 1))


def shared_out(nc, h2T, tile, ps):
    return nc.scalar.copy(h2T[:, bass.ds(tile, 1), :].rearrange("p n c -> p (n c)"), ps)


def gated(nc, hidden, ps, done):
    done(nc.vector.scalar_tensor_tensor(hidden[:, :], hidden[:, :], 1.0, ps[:, 0, 0:FI], ALU.add, ALU.mult))
    return nc.vector.tensor_tensor(hidden[:, :], ps[:, 1, 0:FI], hidden[:, :], ALU.mult)


def load_pair(sp, n, w_gate, w_up, w_down, wg, wu, wd, gu_in, d_in, before_gu=(), before_d=()):
    if before_gu:
        sp.wait_ge(*before_gu)
    for w, src in ((wg, w_gate), (wu, w_up)):
        sp.dma_start(w[:, :, :, :], src[bass.ds(n * 2, 2), :, :].rearrange("e (k p) i -> p e k i", p=P)
                     ).then_inc(gu_in, 16)
    if before_d:
        sp.wait_ge(*before_d)
    sp.dma_start(wd[:, :, :, :], w_down[bass.ds(n * 2, 2), :, :].rearrange("e (f p) c -> p e f c", p=P)
                 ).then_inc(d_in, 16)


def slot_lists(nc, keyT, keys_dram, gather_at, add_at, shg, shu, w_shd, h2T, w_gate, w_up, w_down, first_pair,
               gu_in, d_in, T, keep):
    LARGEST = 2 * (CAP // 8) - 1
    TILES_AFTER_ROUND = {1: 0, 2: 1, 3: 2, 5: 3, 7: 4}
    with ExitStack() as ctx:
        def sb(name, shape, dt=F32):
            return ctx.enter_context(nc.sbuf_tensor("l_" + name, shape, dt))

        def sem(name):
            return ctx.enter_context(nc.semaphore("l_" + name))

        half, both, first = sb("half", [P, CAP]), sb("both", [NE, 2, CAP]), sb("first", [NE, CAP])
        pairs = sb("pairs", [NE // 2, 2 * CAP])
        key, tok, own = sb("key", [P, NE // 2]), sb("tok", [P, NE // 2]), sb("own", [P, 2])
        spare, sparei = sb("spare", [P, NE // 2]), sb("sparei", [P, NE // 2], mybir.dt.int32)
        hid = sb("hid", [P, 2, FI])
        ps = ctx.enter_context(nc.psum_tensor("l_ps", [P, C], F32))
        gu_ps = ctx.enter_context(nc.psum_tensor("l_gu_ps", [P, 2, 2, C], F32))
        y_ps = ctx.enter_context(nc.psum_tensor("l_y_ps", [P, 2, C], F32))
        half_step, first_step, list_step = sem("half_step"), sem("first_step"), sem("list_step")
        hid_step = sem("hid_step")
        both_in, first_out, pairs_in, turned, consts = (sem("both_in"), sem("first_out"), sem("pairs_in"),
                                                        sem("turned"), sem("consts"))
        gu_ready, tanh_ready, hid_ready = sem("gu_ready"), sem("tanh_ready"), sem("hid_ready")
        y_ready, y_copied = sem("y_ready"), sem("y_copied")
        block = ctx.enter_context(nc.Block())

        @block.gpsimd
        def _(pool):
            done = chained(pool, consts)
            done(pool.memset(own[:, :], 1.0))
            done(pool.affine_select(out=own[:, 0:1], in_=own[:, 0:1], compare_op=ALU.is_ge, fill=0.0,
                                    base=CAP - 1, pattern=[[0, 1]], channel_multiplier=-1))
            done(pool.affine_select(out=own[:, 1:2], in_=own[:, 1:2], compare_op=ALU.is_ge, fill=0.0,
                                    base=-CAP, pattern=[[0, 1]], channel_multiplier=1))
            done(pool.iota(sparei[:, :], [[0, NE // 2]], base=T, channel_multiplier=1))
            done(pool.tensor_copy(spare[:, :], sparei[:, :]))

        @block.sync
        def _(sp):
            load_pair(sp, 0, w_gate, w_up, w_down, *first_pair, gu_in, d_in)
            sp.wait_ge(half_step, LARGEST)
            for b in range(2):
                sp.dma_start(both[:, b, :], half[b * NE:(b + 1) * NE, :]).then_inc(both_in, 16)
            sp.wait_ge(first_step, LARGEST)
            sp.dma_start(keys_dram, first[:, :]).then_inc(first_out, 16)
            sp.wait_ge(first_out, 16)
            sp.dma_start(pairs[:, :], keys_dram.rearrange("(m b) s -> m (b s)", b=2)).then_inc(pairs_in, 16)

        @block.scalar
        def _(act):
            def out(n):
                act.wait_ge(y_ready, n + 1)
                shared_out(nc, h2T, n, y_ps[:, n % 2, :]).then_inc(y_copied, 1)

            for n in range(SHARED_FIRST):
                act.wait_ge(gu_ready, n + 1)
                if n >= 2:
                    act.wait_ge(y_ready, n - 1)
                nc.scalar.activation(hid[:, n % 2, :], gu_ps[:, n % 2, 0, 0:FI], ACT.Tanh,
                                     scale=0.5).then_inc(tanh_ready, 1)
                if n >= 1:
                    out(n - 1)
            out(SHARED_FIRST - 1)

        @block.vector
        def _(dve):
            hid_done = chained(dve, hid_step)

            def hidden(n):
                dve.wait_ge(tanh_ready, n + 1)
                gated(nc, hid[:, n % 2, :], gu_ps[:, n % 2, :, :], hid_done).then_inc(hid_ready, 1)

            def largest(out, src, done, tiles):
                for r in range(CAP // 8):
                    done(nc.vector.max(out[:, 8 * r:8 * r + 8], src))
                    if r + 1 < CAP // 8:
                        done(nc.vector.match_replace(src, out[:, 8 * r:8 * r + 8], src, 0.0))
                    if r in tiles:
                        hidden(tiles[r])

            largest(half[:, :], keyT[:, TT:], chained(dve, half_step), TILES_AFTER_ROUND)
            dve.wait_ge(both_in, 32)
            largest(first[:, :], both[:, :, :].rearrange("p b s -> p (b s)"), chained(dve, first_step), {})
            for n in range(len(TILES_AFTER_ROUND), SHARED_FIRST):
                hidden(n)
            done = chained(dve, list_step)
            dve.wait_ge(turned, 1)
            dve.wait_ge(consts, 5)
            done(nc.vector.memset(gather_at[:, NE // 2:], 0))
            done(nc.vector.tensor_copy(key[:, :], ps[:, 0:NE // 2]))
            done(nc.vector.tensor_scalar(tok[:, :], key[:, :], -1.0, float(T), ALU.mult, ALU.add))
            done(nc.vector.tensor_scalar(gather_at[:, 0:NE // 2], tok[:, :], float(T - 1), None, ALU.min))
            for b in range(2):
                done(nc.vector.tensor_tensor(tok[:, :], tok[:, :], spare[:, :], ALU.subtract))
                done(nc.vector.scalar_tensor_tensor(tok[:, :], key[:, :], 0.0, tok[:, :], ALU.is_gt, ALU.mult))
                done(nc.vector.scalar_tensor_tensor(tok[:, :], tok[:, :], own[:, b:b + 1], spare[:, :],
                                                    ALU.mult, ALU.add))
                done(nc.vector.tensor_copy(add_at[:, b, 0:NE // 2], tok[:, :]))
                done(nc.vector.tensor_scalar(tok[:, :], key[:, :], -1.0, float(T), ALU.mult, ALU.add))

        @block.tensor
        def _(pe):
            def down(n):
                pe.wait_ge(hid_ready, n + 1)
                if n >= 2:
                    pe.wait_ge(y_copied, n - 1)
                for f in range(FT):
                    last = shared_down(nc, y_ps[:, n % 2, :], hid[:, n % 2, :], w_shd, f)
                last.then_inc(y_ready, 1)

            for n in range(SHARED_FIRST):
                shared_gate_up(nc, gu_ps[:, n % 2, :, :], shg, shu, h2T, n).then_inc(gu_ready, 1)
                if 1 <= n < SHARED_FIRST - 1:
                    down(n - 1)
            down(SHARED_FIRST - 2)
            pe.wait_ge(pairs_in, 16)
            nc.tensor.transpose(ps[:, 0:NE // 2], pairs[:, :], keep["ident"][0:NE // 2, 0:NE // 2]).then_inc(turned, 1)
            down(SHARED_FIRST - 1)


def experts_part(nc, rows_dram, acc_dram, w_gate, w_up, w_down, gather_at, add_at, shg, shu, w_shd, h2T, first_pair,
                 gu_in, d_in, T, keep):
    NS = NE // 2
    NL = NS // 2
    BODY, TILES = 4, 3
    RW = C + NE
    assert T // P == SHARED_FIRST + TILES * (NS // BODY)
    with ExitStack() as ctx:
        def sb(name, shape, dt=F32):
            return ctx.enter_context(nc.sbuf_tensor("e_" + name, shape, dt))

        def sem(name):
            return ctx.enter_context(nc.semaphore("e_" + name))

        wg = [first_pair[0], sb("wg", [P, 2, KT, FI])]
        wu = [first_pair[1], sb("wu", [P, 2, KT, FI])]
        wd = [first_pair[2], sb("wd", [P, 2, FT, C])]
        xg = [sb(f"xg{b}", [P, RW]) for b in range(2)]
        xeT = sb("xeT", [P, KT, P])
        hid, s_hid = sb("hid", [P, FI]), sb("s_hid", [P, FI])
        hidT = sb("hidT", [P, FT, P])
        wcol = [sb(f"wcol{b}", [P, 1]) for b in range(2)]
        from_rows = [sb(f"from_rows{b}", [P, 1], U32) for b in range(2)]
        to_rows = [sb(f"to_rows{b}", [P, 2], U32) for b in range(2)]
        y = [sb(f"y{b}", [P, C]) for b in range(2)]
        x_ps = ctx.enter_context(nc.psum_tensor("e_x_ps", [P, KT, P], F32))
        gu_ps = ctx.enter_context(nc.psum_tensor("e_gu_ps", [P, 2, C], F32))
        hT_ps = ctx.enter_context(nc.psum_tensor("e_hT_ps", [P, C], F32))
        y_ps = ctx.enter_context(nc.psum_tensor("e_y_ps", [P, C], F32))
        s_gu_ps = ctx.enter_context(nc.psum_tensor("e_s_gu_ps", [P, 2, C], F32))
        s_y_ps = ctx.enter_context(nc.psum_tensor("e_s_y_ps", [P, C], F32))
        x_in = [sem(f"x_in{b}") for b in range(2)]
        added, pair_added = sem("added"), sem("pair_added")
        rows_ready = sem("rows_ready")
        x_ready, xe_ready = sem("x_ready"), sem("xe_ready")
        gu_ready, tanh_ready, hid_ready = sem("gu_ready"), sem("tanh_ready"), sem("hid_ready")
        s_gu_ready, s_tanh_ready, s_hid_ready = sem("s_gu_ready"), sem("s_tanh_ready"), sem("s_hid_ready")
        hT_ready, hT_copied, y_ready, y_done = sem("hT_ready"), sem("hT_copied"), sem("y_ready"), sem("y_done")
        s_y_ready, s_y_copied = sem("s_y_ready"), sem("s_y_copied")
        step, s_step, pool_passed = sem("step"), sem("s_step"), sem("pool_passed")
        block = ctx.enter_context(nc.Block())
        ident, cols, gates = keep["ident"], keep["cols"], keep["gates"]
        slots = [slice(0, CAP), slice(CAP, 2 * CAP)]

        def place(it, q):
            return BODY * it + q, q % 2, BODY // 2 * it + q // 2, TILES * it + q if q < TILES else None

        @block.sync
        def _(sp):
            for b in range(2):
                sp.wait_ge(x_in[b], 16)
            load_pair(sp, 1, w_gate, w_up, w_down, wg[1], wu[1], wd[1], gu_in[1], d_in[1])
            with sp.Fori(0, NL - 1) as it:
                for b in range(2):
                    n = 2 * it + b
                    load_pair(sp, n + 2, w_gate, w_up, w_down, wg[b], wu[b], wd[b], gu_in[b], d_in[b],
                              before_gu=(gu_ready, n + 1), before_d=(y_ready, n + 2))

        @block.gpsimd
        def _(pool):
            def gather(b, n):
                wait_apart(pool, pool_passed, rows_ready, n + 1)
                pool.indirect_dma_start(xg[b][:, :], None, rows_dram, bass.IndirectOffsetOnAxis(
                    ap=from_rows[b][:, 0:1], axis=0), bounds_check=T - 1, oob_is_err=True).then_inc(x_in[b], 16)

            gather(0, 0)
            gather(1, 1)
            gather(0, 2)
            with pool.Fori(0, NL) as it:
                for b in range(2):
                    n = 2 * it + b
                    wait_apart(pool, pool_passed, y_done, n + 2)
                    for one in range(2):
                        pool.indirect_dma_start(acc_dram, bass.IndirectOffsetOnAxis(
                            ap=to_rows[b][:, one:1 + one], axis=0), y[b][:, :], None, bounds_check=T + P - 1,
                            oob_is_err=True, compute_op=ALU.add).then_inc(added, 16)
                        if one == 0:
                            gather(1 - b, n + 3)
                        wait_apart(pool, pool_passed, added, 16 * (2 * n + one + 1))
                    pool.sem_inc(pair_added, 1)
            for b in range(2):
                pool.wait_ge(x_in[b], 16 * (NL + 2 - b))

        @block.scalar
        def _(act):
            def turned_in(m):
                act.wait_ge(x_ready, m + 1)
                for k in range(KT):
                    last = nc.scalar.activation(xeT[:, k, :], x_ps[:, k, :], ACT.Identity,
                                                scale=cols[:, CB, k:k + 1], bias=cols[:, SB, k:k + 1])
                last.then_inc(xe_ready, 1)

            def hidden_turned(n):
                act.wait_ge(hT_ready, n + 1)
                act.wait_ge(y_ready, n + 1)
                nc.scalar.copy(hidT[:, :, :], hT_ps[:, 0:FT * P].rearrange("p (f s) -> p f s", f=FT)
                               ).then_inc(hT_copied, 1)

            def step_of(body, q):
                n, b, it, tile = place(body, q)
                if tile is not None:
                    act.wait_ge(s_gu_ready, tile + 1)
                    nc.scalar.activation(s_hid[:, :], s_gu_ps[:, 0, 0:FI], ACT.Tanh,
                                         scale=0.5).then_inc(s_tanh_ready, 1)
                act.wait_ge(gu_ready, n + 1)
                nc.scalar.activation(hid[:, :], gu_ps[:, 0, 0:FI], ACT.Tanh, scale=0.5).then_inc(tanh_ready, 1)
                if tile is not None:
                    turned_in(n + 1)
                    hidden_turned(n)
                    act.wait_ge(s_y_ready, tile + 1)
                    shared_out(nc, h2T, tile + SHARED_FIRST, s_y_ps[:, :]).then_inc(s_y_copied, 1)
                else:
                    hidden_turned(n)
                    turned_in(n + 1)

            turned_in(0)
            with act.Fori(0, NS // BODY) as body:
                for q in range(BODY):
                    step_of(body, q)

        @block.vector
        def _(dve):
            nc.vector.memset(wcol[1][:, :], 0.0).then_inc(y_ready, 1)
            nc.vector.memset(y[0][:, 0:1], 0.0).then_inc(pair_added, 2)
            nc.vector.memset(y[0][:, 1:2], 0.0).then_inc(y_done, 1)
            nc.vector.memset(y[0][:, 2:3], 0.0).then_inc(s_y_copied, 1)

            def rows_to_gather(b, m):
                nc.vector.tensor_copy(from_rows[b][:, :], gather_at[:, bass.ds(m, 1)]).then_inc(rows_ready, 1)

            def step_of(body, q, done, s_done):
                n, b, it, tile = place(body, q)
                dve.wait_ge(pair_added, n + 1)
                nc.vector.tensor_copy(to_rows[b][:, 0:1], add_at[:, 0, bass.ds(n, 1)])
                nc.vector.tensor_copy(to_rows[b][:, 1:2], add_at[:, 1, bass.ds(n, 1)])
                if tile is not None:
                    dve.wait_ge(s_tanh_ready, tile + 1)
                    gated(nc, s_hid, s_gu_ps, s_done).then_inc(s_hid_ready, 1)
                dve.wait_ge(tanh_ready, n + 1)
                gated(nc, hid, gu_ps, done).then_inc(hid_ready, 1)
                weights_of(1 - b, it + b, n + 1, (n + 1) % NS)
                dve.wait_ge(y_ready, n + 2)
                nc.vector.scalar_tensor_tensor(y[b][:, :], y_ps[:, :], wcol[b][:, 0:1], gates[:, 1, :],
                                               ALU.mult, ALU.mult).then_inc(y_done, 1)

            def weights_of(b, it, m, pair):
                dve.wait_ge(x_in[b], 16 * it + 16)
                nc.vector.tensor_copy(wcol[b][0:CAP, :], xg[b][0:CAP, bass.ds(2 * pair + C, 1)])
                nc.vector.tensor_copy(wcol[b][CAP:, :], xg[b][CAP:, bass.ds(2 * pair + C + 1, 1)])
                dve.wait_ge(x_ready, m + 1)
                rows_to_gather(b, m + 2)

            rows_to_gather(0, 0)
            rows_to_gather(1, 1)
            weights_of(0, 0, 0, 0)
            with dve.Fori(0, NS // BODY) as body:
                done, s_done = chained(dve, step, BODY * body), chained(dve, s_step, TILES * body)
                for q in range(BODY):
                    step_of(body, q, done, s_done)

        @block.tensor
        def _(pe):
            def turn_rows(it, b):
                pe.wait_ge(x_in[b], 16 * it + 16)
                for k in range(KT):
                    last = nc.tensor.transpose(x_ps[:, k, :], xg[b][:, k * P:(k + 1) * P], ident[:, :])
                last.then_inc(x_ready, 1)

            def step_of(body, q):
                n, b, it, tile = place(body, q)
                if tile is not None:
                    shared_gate_up(nc, s_gu_ps, shg, shu, h2T, tile + SHARED_FIRST).then_inc(s_gu_ready, 1)
                pe.wait_ge(xe_ready, n + 1)
                pe.wait_ge(gu_in[b], 32 * it + 32)
                for j, wj in enumerate((wg[b], wu[b])):
                    for k in range(KT):
                        for e in range(2):
                            last = nc.tensor.matmul(gu_ps[slots[e], j, 0:FI], xeT[:, k, slots[e]],
                                                    wj[:, e, k, :], start=(k == 0), stop=(k == KT - 1))
                last.then_inc(gu_ready, 1)
                turn_rows(it + b, 1 - b)
                if tile is not None:
                    pe.wait_ge(s_hid_ready, tile + 1)
                    pe.wait_ge(s_y_copied, tile + 1)
                    for f in range(FT - 1):
                        shared_down(nc, s_y_ps[:, :], s_hid, w_shd, f)
                pe.wait_ge(hid_ready, n + 1)
                for f in range(FT):
                    last = nc.tensor.transpose(hT_ps[:, f * P:(f + 1) * P], hid[:, f * P:(f + 1) * P], ident[:, :])
                last.then_inc(hT_ready, 1)
                if tile is not None:
                    shared_down(nc, s_y_ps[:, :], s_hid, w_shd, FT - 1).then_inc(s_y_ready, 1)
                pe.wait_ge(hT_copied, n + 1)
                pe.wait_ge(d_in[b], 16 * it + 16)
                pe.wait_ge(y_done, n + 1)
                for f in range(FT):
                    for e in range(2):
                        last = nc.tensor.matmul(y_ps[slots[e], :], hidT[:, f, slots[e]], wd[b][:, e, f, :],
                                                start=(f == 0), stop=(f == FT - 1))
                last.then_inc(y_ready, 1)

            turn_rows(0, 0)
            with pe.Fori(0, NS // BODY) as body:
                for q in range(BODY):
                    step_of(body, q)


def sum_up(nc, acc_dram, h2T, out, T):
    NT = T // TT
    NB = 4
    with ExitStack() as ctx:
        rows = [ctx.enter_context(nc.sbuf_tensor(f"s_rows{b}", [P, TB, C], F32)) for b in range(NB)]
        rows_in = [ctx.enter_context(nc.semaphore(f"s_rows_in{b}")) for b in range(NB)]
        rows_out = [ctx.enter_context(nc.semaphore(f"s_rows_out{b}")) for b in range(NB)]
        summed = ctx.enter_context(nc.semaphore("s_summed"))
        block = ctx.enter_context(nc.Block())

        @block.sync
        def _(sp):
            for n in range(NT):
                if n >= NB:
                    sp.wait_ge(rows_out[n % NB], 16 * (n // NB))
                sp.dma_start(rows[n % NB][:, :, :], acc_dram[n * TT:(n + 1) * TT, :].rearrange(
                    "(t p) c -> p t c", p=P)).then_inc(rows_in[n % NB], 16)

        @block.vector
        def _(dve):
            for n in range(NT):
                dve.wait_ge(rows_in[n % NB], 16 * (n // NB + 1))
                nc.vector.tensor_tensor(rows[n % NB][:, :, :], rows[n % NB][:, :, :],
                                        h2T[:, n * TB:(n + 1) * TB, :], ALU.add).then_inc(summed, 1)

        @block.scalar
        def _(act):
            for n in range(NT):
                act.wait_ge(summed, n + 1)
                act.dma_start(out[n * TT:(n + 1) * TT, :].rearrange("(t p) c -> p t c", p=P),
                              rows[n % NB][:, :, :]).then_inc(rows_out[n % NB], 16)
            for b in range(min(NB, NT)):
                act.wait_ge(rows_out[b], 16 * ((NT - 1 - b) // NB + 1))


def layer_kernel(nc, x3, wq, wk, wv, wo, w_router, w_gate, w_up, w_down, w_sh_gate, w_sh_up, w_sh_down,
                 c, wmod, out3):
    x, out = x3[0], out3[0]
    T = x.shape[0]
    oT_dram = nc.dram_tensor("oT_scratch", (C, T), F32).ap()
    k_dram = nc.dram_tensor("k_scratch", (NG, P, 2, T), F32).ap()
    q_dram = nc.dram_tensor("q_scratch", (NG, P, 2, T), F32).ap()
    v_dram = nc.dram_tensor("v_scratch", (T, C), F32).ap()
    rows_dram = nc.dram_tensor("rows_scratch", (T, C + NE), F32).ap()
    acc_dram = nc.dram_tensor("acc_scratch", (T + P, C), F32).ap()
    keys_dram = nc.dram_tensor("keys_scratch", (NE, CAP), F32).ap()
    with ExitStack() as ctx:
        keep = {
            "ident": ctx.enter_context(nc.sbuf_tensor("ident", [P, P], F32)),
            "ones": ctx.enter_context(nc.sbuf_tensor("ones", [P, P], F32)),
            "cols": ctx.enter_context(nc.sbuf_tensor("mod_cols", [P, MODS, KT], F32)),
            "gates": ctx.enter_context(nc.sbuf_tensor("gates", [P, 2, C], F32)),
        }
        first_part(nc, x, c, wmod, wq, wk, wv, k_dram, q_dram, v_dram, keep)
        attention(nc, k_dram, q_dram, v_dram, T, oT_dram, keep)
        def sb(name, shape, dt=F32):
            return ctx.enter_context(nc.sbuf_tensor(name, shape, dt))

        gather_at = sb("gather_at", [P, NE // 2 + 3], U32)
        add_at = sb("add_at", [P, 2, NE // 2], U32)
        h2T = sb("h2T", [P, T // P, KT * P])
        shg, shu = sb("sh_gate", [P, KT, FI]), sb("sh_up", [P, KT, FI])
        w_shd = sb("w_shd", [P, FT, C])
        keyT = sb("keyT", [P, TT + T // 2])
        dense_part(nc, x, oT_dram, rows_dram, acc_dram, wo, w_router, w_sh_gate, w_sh_up, w_sh_down, shg, shu, w_shd,
                   h2T, keyT, keep)
        with (nc.sbuf_tensor("first_wg", [P, 2, KT, FI], F32) as wg, nc.sbuf_tensor("first_wu", [P, 2, KT, FI], F32) as wu,
              nc.sbuf_tensor("first_wd", [P, 2, FT, C], F32) as wd, nc.semaphore("gu_in0") as gu_in0,
              nc.semaphore("gu_in1") as gu_in1, nc.semaphore("d_in0") as d_in0, nc.semaphore("d_in1") as d_in1):
            first_pair = (wg, wu, wd)
            slot_lists(nc, keyT, keys_dram, gather_at, add_at, shg, shu, w_shd, h2T, w_gate, w_up, w_down,
                       first_pair, gu_in0, d_in0, T, keep)
            experts_part(nc, rows_dram, acc_dram, w_gate, w_up, w_down, gather_at, add_at, shg, shu, w_shd, h2T,
                         first_pair, (gu_in0, gu_in1), (d_in0, d_in1), T, keep)
        sum_up(nc, acc_dram, h2T, out, T)


_INS = ['L0_attn_x', 'L0_attn_Wq', 'L0_attn_Wk', 'L0_attn_Wv', 'L0_attn_Wo', 'L0_ffn_w_router', 'L0_ffn_w_gate',
        'L0_ffn_w_up', 'L0_ffn_w_down', 'L0_ffn_w_sh_gate', 'L0_ffn_w_sh_up', 'L0_ffn_w_sh_down', 'L0_c', 'L0_wmod']
_OUTS = [((1, 4096, 512), 'float32')]


def kernel(**inputs):
    import numpy as _np
    import concourse.bacc as _bacc
    from concourse import mybir as _mybir
    from concourse.bass_utils import run_bass_kernel_spmd as _run

    nc = _bacc.Bacc("TRN2", target_bir_lowering=False, num_devices=1)
    arrays, args = {}, []
    for name in _INS:
        a = _np.ascontiguousarray(inputs[name])
        arrays[f"in_{name}_dram"] = a
        args.append(nc.dram_tensor(f"in_{name}_dram", a.shape, _mybir.dt.from_np(a.dtype), kind="ExternalInput").ap())
    for i, (shape, dtype) in enumerate(_OUTS):
        dt = _mybir.dt.from_np(_np.dtype(dtype))
        args.append(nc.dram_tensor(f"out_{i}_dram", shape, dt, kind="ExternalOutput").ap())
    layer_kernel(nc, *args)
    r = _run(nc, [arrays], core_ids=[0])
    return r.results[0]["out_0_dram"]
```
